# Optimizing a Trainium2 kernel written in Bass

```python
import numpy as np
import jax
import jax.numpy as jnp

def _softmax(x, axis=-1):
    return jax.nn.softmax(x, axis=axis)

def _gelu(x):
    return jax.nn.gelu(x, approximate=True)

def _silu(x):
    return jax.nn.silu(x)

def _sigmoid(x):
    return jax.nn.sigmoid(x)

def _layernorm(x, axis=-1, eps=1e-05):
    m = jnp.mean(x, axis=axis, keepdims=True)
    v = jnp.var(x, axis=axis, keepdims=True)
    return (x - m) / jnp.sqrt(v + eps)

def _scatter_add(tgt, idx, src, axis=0):
    return tgt.at[idx].add(src)

def _segment_sum(src, seg, n):
    return jax.ops.segment_sum(src, seg, n)
kernel_name = 'mk_gnn_resnorm_d4_gnn_r32_0ad430'

def setup_inputs(seed: int=0):
    np.random.seed(seed)
    _w = jnp.asarray

    def _rec_inputs():
        import jax
        import jax.numpy as jnp
        _gk = jax.random.key(seed)
        x = -0.0003713 + 1 * jax.random.normal(jax.random.fold_in(_gk, 1), (3125, 128), jnp.float32)
        _s = jax.random.randint(jax.random.fold_in(_gk, 2), (25000,), 0, 3125, jnp.int32)
        _d = jax.random.randint(jax.random.fold_in(_gk, 3), (25000,), 0, 3125, jnp.int32)
        _loop = jnp.arange(3125, dtype=jnp.int32)
        src = jnp.concatenate([_s, _d, _loop])
        dst = jnp.concatenate([_d, _s, _loop])
        _o = jnp.argsort(dst, stable=True)
        src = src[_o]
        dst = dst[_o]
        edge_attr_20 = jax.random.uniform(jax.random.fold_in(_gk, 12), (53125, 20), jnp.float32, 0.0, 1)
        edge_attr_64 = -9.77346e-05 + 0.999888 * jax.random.normal(jax.random.fold_in(_gk, 13), (53125, 64), jnp.float32)
        edge_weight = jax.random.uniform(jax.random.fold_in(_gk, 15), (53125,), jnp.float32, 0.0, 0.999998)
        return (x, src, dst, edge_attr_20, edge_attr_64, edge_weight)
    x, src, dst, edge_attr_20, edge_attr_64, edge_weight = _rec_inputs()

    def _L0_gnn_setup():
        import jax, jax.numpy as jnp
        import numpy as np
        N_NODES = 3125
        N_EDGES = 50000
        D = 128
        L = 4
        H = 32
        BN_EPS = 1e-05

        def _bn(x, g, b):
            m = jnp.mean(x, axis=0)
            v = jnp.var(x, axis=0)
            return g * (x - m) * jax.lax.rsqrt(v + BN_EPS) + b
        key = jax.random.key(seed)
        ks = jax.random.split(key, 8)
        X = jax.random.normal(ks[0], (N_NODES, D), dtype=jnp.float32)
        edge_index = jax.random.randint(ks[1], (2, N_EDGES), 0, N_NODES, dtype=jnp.int64)
        eps = jax.random.normal(ks[2], (L,), dtype=jnp.float32)
        W1 = jax.random.normal(ks[3], (L, H, D), dtype=jnp.float32) * 0.1
        W2 = jax.random.normal(ks[4], (L, H, H), dtype=jnp.float32) * 0.1
        W3 = jax.random.normal(ks[5], (L, D, H), dtype=jnp.float32) * 0.1
        return {'X': X, 'edge_index': edge_index, 'eps': eps, 'W1': W1, 'b1': jnp.zeros((L, H), jnp.float32), 'g1': jnp.ones((L, H), jnp.float32), 'bt1': jnp.zeros((L, H), jnp.float32), 'W2': W2, 'b2': jnp.zeros((L, H), jnp.float32), 'g2': jnp.ones((L, H), jnp.float32), 'bt2': jnp.zeros((L, H), jnp.float32), 'W3': W3, 'b3': jnp.zeros((L, D), jnp.float32)}
    _L0_gnn_all = _L0_gnn_setup()
    _L0_gnn_in = {k: v for k, v in _L0_gnn_all.items() if k in ('eps', 'W1', 'b1', 'g1', 'bt1', 'W2', 'b2', 'g2', 'bt2', 'W3', 'b3')}
    del _L0_gnn_all

    def _L1_gnn_setup():
        import jax, jax.numpy as jnp
        import numpy as np
        N_NODES = 50000
        N_EDGES = 25000
        D_NODE = 128
        D_EDGE = 64
        D_HID = 128
        D_OUT = 128

        def _linear_params(key, fan_in, fan_out):
            k1, k2 = jax.random.split(key)
            bound = 1.0 / np.sqrt(fan_in)
            W = jax.random.uniform(k1, (fan_out, fan_in), jnp.float32, -bound, bound)
            b = jax.random.uniform(k2, (fan_out,), jnp.float32, -bound, bound)
            return (W, b)
        key = jax.random.key(seed)
        ks = jax.random.split(key, 8)
        node_features = jax.random.normal(ks[0], (N_NODES, D_NODE), jnp.float32)
        edge_features = jax.random.normal(ks[1], (N_EDGES, D_EDGE), jnp.float32)
        edge_index = jax.random.randint(ks[2], (2, N_EDGES), 0, N_NODES, jnp.int64)
        W1, b1 = _linear_params(ks[3], 2 * D_NODE + D_EDGE, D_HID)
        W2, b2 = _linear_params(ks[4], D_HID, D_HID)
        U1, c1 = _linear_params(ks[5], D_NODE + D_HID, D_HID)
        U2, c2 = _linear_params(ks[6], D_HID, D_OUT)
        return {'node_features': node_features, 'edge_features': edge_features, 'edge_index': edge_index, 'W1': W1, 'b1': b1, 'W2': W2, 'b2': b2, 'U1': U1, 'c1': c1, 'U2': U2, 'c2': c2}
    _L1_gnn_all = _L1_gnn_setup()
    _L1_gnn_in = {k: v for k, v in _L1_gnn_all.items() if k in ('W1', 'b1', 'W2', 'b2', 'U1', 'c1', 'U2', 'c2')}
    del _L1_gnn_all

    def _L2_gnn_setup():
        import jax, jax.numpy as jnp
        import numpy as np
        N, E, H = (50000, 25000, 128)
        N_AGGR, HID2 = (3, 256)
        EPS_MSG, EPS_BN, EPS_SM = (1e-07, 1e-05, 1e-16)

        def _segment_softmax(logits, seg, num_segments):
            m = jax.ops.segment_max(logits, seg, num_segments=num_segments)
            m = jnp.where(jnp.isfinite(m), m, 0.0)
            e = jnp.exp(logits - m[seg])
            s = jax.ops.segment_sum(e, seg, num_segments=num_segments)
            return e / (s[seg] + EPS_SM)

        def _genconv(x, src, dst, W1, W2, gamma, beta, t):
            n = x.shape[0]
            msg = jax.nn.relu(x[src]) + EPS_MSG
            w = _segment_softmax(msg * t, dst, n)
            aggr = jax.ops.segment_sum(msg * w, dst, num_segments=n)
            h = x + aggr
            h = h @ W1
            mu = h.mean(axis=0)
            var = h.var(axis=0)
            h = (h - mu) * jax.lax.rsqrt(var + EPS_BN) * gamma + beta
            h = jax.nn.relu(h)
            return h @ W2
        key = jax.random.key(seed)
        ks = jax.random.split(key, 6)
        x_hat = jax.random.normal(ks[0], (N, H), jnp.float32)
        edge_index = jax.random.randint(ks[1], (2, E), 0, N)
        W1 = jax.random.normal(ks[2], (N_AGGR, H, HID2), jnp.float32) / np.sqrt(H).astype(np.float32)
        W2 = jax.random.normal(ks[3], (N_AGGR, HID2, H), jnp.float32) / np.sqrt(HID2).astype(np.float32)
        gamma = jnp.ones((N_AGGR, HID2), jnp.float32)
        beta = jnp.zeros((N_AGGR, HID2), jnp.float32)
        t = jnp.ones((N_AGGR,), jnp.float32)
        return {'x_hat': x_hat, 'edge_index': edge_index, 'W1': W1, 'W2': W2, 'gamma': gamma, 'beta': beta, 't': t}
    _L2_gnn_all = _L2_gnn_setup()
    _L2_gnn_in = {k: v for k, v in _L2_gnn_all.items() if k in ('W1', 'W2', 'gamma', 'beta', 't')}
    del _L2_gnn_all

    def _L3_gnn_setup():
        import jax, jax.numpy as jnp
        import numpy as np
        import math
        LOG2 = math.log(2.0)

        def shifted_softplus(x):
            return jax.nn.softplus(x) - LOG2
        key = jax.random.key(seed)
        ks = jax.random.split(key, 12)
        n_atoms, n_pairs = (1250, 20000)
        d_basis, d_filt, n_rbf = (128, 128, 20)
        x = jax.random.normal(ks[0], (n_atoms, d_basis), dtype=jnp.float32)
        f_ij = jax.random.uniform(ks[1], (n_pairs, n_rbf), dtype=jnp.float32)
        idx_i = jax.random.randint(ks[2], (n_pairs,), 0, n_atoms)
        idx_j = jax.random.randint(ks[3], (n_pairs,), 0, n_atoms)
        rcut_ij = jax.random.uniform(ks[4], (n_pairs,), dtype=jnp.float32)
        s_in = 1.0 / math.sqrt(d_basis)
        s_f = 1.0 / math.sqrt(n_rbf)
        s_out = 1.0 / math.sqrt(d_filt)
        W_in = jax.random.uniform(ks[5], (d_filt, d_basis), minval=-s_in, maxval=s_in)
        b_in = jax.random.uniform(ks[6], (d_filt,), minval=-s_in, maxval=s_in)
        W_f = jax.random.uniform(ks[7], (d_filt, n_rbf), minval=-s_f, maxval=s_f)
        b_f = jax.random.uniform(ks[8], (d_filt,), minval=-s_f, maxval=s_f)
        W_out = jax.random.uniform(ks[9], (d_basis, d_filt), minval=-s_out, maxval=s_out)
        b_out = jax.random.uniform(ks[10], (d_basis,), minval=-s_out, maxval=s_out)
        return {'x': x, 'f_ij': f_ij, 'idx_i': idx_i, 'idx_j': idx_j, 'rcut_ij': rcut_ij, 'W_in': W_in, 'b_in': b_in, 'W_f': W_f, 'b_f': b_f, 'W_out': W_out, 'b_out': b_out}
    _L3_gnn_all = _L3_gnn_setup()
    _L3_gnn_in = {k: v for k, v in _L3_gnn_all.items() if k in ('W_in', 'b_in', 'W_f', 'b_f', 'W_out', 'b_out')}
    del _L3_gnn_all
    return {'x': x, 'src': src, 'dst': dst, 'edge_attr_20': edge_attr_20, 'edge_attr_64': edge_attr_64, 'edge_weight': edge_weight, 'L0_gnn_eps': _L0_gnn_in['eps'], 'L0_gnn_W1': _L0_gnn_in['W1'], 'L0_gnn_b1': _L0_gnn_in['b1'], 'L0_gnn_g1': _L0_gnn_in['g1'], 'L0_gnn_bt1': _L0_gnn_in['bt1'], 'L0_gnn_W2': _L0_gnn_in['W2'], 'L0_gnn_b2': _L0_gnn_in['b2'], 'L0_gnn_g2': _L0_gnn_in['g2'], 'L0_gnn_bt2': _L0_gnn_in['bt2'], 'L0_gnn_W3': _L0_gnn_in['W3'], 'L0_gnn_b3': _L0_gnn_in['b3'], 'L1_gnn_W1': _L1_gnn_in['W1'], 'L1_gnn_b1': _L1_gnn_in['b1'], 'L1_gnn_W2': _L1_gnn_in['W2'], 'L1_gnn_b2': _L1_gnn_in['b2'], 'L1_gnn_U1': _L1_gnn_in['U1'], 'L1_gnn_c1': _L1_gnn_in['c1'], 'L1_gnn_U2': _L1_gnn_in['U2'], 'L1_gnn_c2': _L1_gnn_in['c2'], 'L2_gnn_W1': _L2_gnn_in['W1'], 'L2_gnn_W2': _L2_gnn_in['W2'], 'L2_gnn_gamma': _L2_gnn_in['gamma'], 'L2_gnn_beta': _L2_gnn_in['beta'], 'L2_gnn_t': _L2_gnn_in['t'], 'L3_gnn_W_in': _L3_gnn_in['W_in'], 'L3_gnn_b_in': _L3_gnn_in['b_in'], 'L3_gnn_W_f': _L3_gnn_in['W_f'], 'L3_gnn_b_f': _L3_gnn_in['b_f'], 'L3_gnn_W_out': _L3_gnn_in['W_out'], 'L3_gnn_b_out': _L3_gnn_in['b_out']}

def reference(x, src, dst, edge_attr_20, edge_attr_64, edge_weight, L0_gnn_eps, L0_gnn_W1, L0_gnn_b1, L0_gnn_g1, L0_gnn_bt1, L0_gnn_W2, L0_gnn_b2, L0_gnn_g2, L0_gnn_bt2, L0_gnn_W3, L0_gnn_b3, L1_gnn_W1, L1_gnn_b1, L1_gnn_W2, L1_gnn_b2, L1_gnn_U1, L1_gnn_c1, L1_gnn_U2, L1_gnn_c2, L2_gnn_W1, L2_gnn_W2, L2_gnn_gamma, L2_gnn_beta, L2_gnn_t, L3_gnn_W_in, L3_gnn_b_in, L3_gnn_W_f, L3_gnn_b_f, L3_gnn_W_out, L3_gnn_b_out):
    import jax
    import jax.numpy as jnp

    def _L0_gnn_ref(X, edge_index, eps, W1, b1, g1, bt1, W2, b2, g2, bt2, W3, b3):
        import jax, jax.numpy as jnp
        import numpy as np
        N_NODES = 3125
        N_EDGES = 50000
        D = 128
        L = 4
        H = 32
        BN_EPS = 1e-05

        def _bn(x, g, b):
            m = jnp.mean(x, axis=0)
            v = jnp.var(x, axis=0)
            return g * (x - m) * jax.lax.rsqrt(v + BN_EPS) + b
        src, dst = (edge_index[0], edge_index[1])
        for l in range(L):
            S = jax.ops.segment_sum(X[src], dst, num_segments=N_NODES)
            Z = (1.0 + eps[l]) * X + S
            h = jax.nn.relu(_bn(Z @ W1[l].T + b1[l], g1[l], bt1[l]))
            h = jax.nn.relu(_bn(h @ W2[l].T + b2[l], g2[l], bt2[l]))
            X = h @ W3[l].T + b3[l]
        return X

    def _L1_gnn_ref(node_features, edge_features, edge_index, W1, b1, W2, b2, U1, c1, U2, c2):
        import jax, jax.numpy as jnp
        import numpy as np
        N_NODES = 50000
        N_EDGES = 25000
        D_NODE = 128
        D_EDGE = 64
        D_HID = 128
        D_OUT = 128

        def _linear_params(key, fan_in, fan_out):
            k1, k2 = jax.random.split(key)
            bound = 1.0 / np.sqrt(fan_in)
            W = jax.random.uniform(k1, (fan_out, fan_in), jnp.float32, -bound, bound)
            b = jax.random.uniform(k2, (fan_out,), jnp.float32, -bound, bound)
            return (W, b)
        row, col = (edge_index[0], edge_index[1])
        msg_in = jnp.concatenate([node_features[row], node_features[col], edge_features], axis=1)
        h = jax.nn.relu(msg_in @ W1.T + b1)
        messages = h @ W2.T + b2
        agg = jax.ops.segment_sum(messages, col, num_segments=node_features.shape[0])
        upd_in = jnp.concatenate([node_features, agg], axis=1)
        g = jax.nn.relu(upd_in @ U1.T + c1)
        return g @ U2.T + c2

    def _L2_gnn_ref(x_hat, edge_index, W1, W2, gamma, beta, t):
        import jax, jax.numpy as jnp
        import numpy as np
        N, E, H = (50000, 25000, 128)
        N_AGGR, HID2 = (3, 256)
        EPS_MSG, EPS_BN, EPS_SM = (1e-07, 1e-05, 1e-16)

        def _segment_softmax(logits, seg, num_segments):
            m = jax.ops.segment_max(logits, seg, num_segments=num_segments)
            m = jnp.where(jnp.isfinite(m), m, 0.0)
            e = jnp.exp(logits - m[seg])
            s = jax.ops.segment_sum(e, seg, num_segments=num_segments)
            return e / (s[seg] + EPS_SM)

        def _genconv(x, src, dst, W1, W2, gamma, beta, t):
            n = x.shape[0]
            msg = jax.nn.relu(x[src]) + EPS_MSG
            w = _segment_softmax(msg * t, dst, n)
            aggr = jax.ops.segment_sum(msg * w, dst, num_segments=n)
            h = x + aggr
            h = h @ W1
            mu = h.mean(axis=0)
            var = h.var(axis=0)
            h = (h - mu) * jax.lax.rsqrt(var + EPS_BN) * gamma + beta
            h = jax.nn.relu(h)
            return h @ W2
        src, dst = (edge_index[0], edge_index[1])
        h = x_hat
        for l in range(N_AGGR):
            h = _genconv(h, src, dst, W1[l], W2[l], gamma[l], beta[l], t[l])
            h = jax.nn.relu(h)
        return h

    def _L3_gnn_ref(x, f_ij, idx_i, idx_j, rcut_ij, W_in, b_in, W_f, b_f, W_out, b_out):
        import jax, jax.numpy as jnp
        import numpy as np
        import math
        LOG2 = math.log(2.0)

        def shifted_softplus(x):
            return jax.nn.softplus(x) - LOG2
        n_atoms = x.shape[0]
        h = x @ W_in.T + b_in
        Wij = shifted_softplus(f_ij @ W_f.T + b_f) * rcut_ij[:, None]
        x_ij = h[idx_j] * Wij
        agg = jax.ops.segment_sum(x_ij, idx_i, num_segments=n_atoms)
        return shifted_softplus(agg @ W_out.T + b_out)
    edge_index = jnp.stack([src, dst])
    x = _layernorm(x + _L0_gnn_ref(x, edge_index, L0_gnn_eps, L0_gnn_W1, L0_gnn_b1, L0_gnn_g1, L0_gnn_bt1, L0_gnn_W2, L0_gnn_b2, L0_gnn_g2, L0_gnn_bt2, L0_gnn_W3, L0_gnn_b3), axis=-1)
    x = _layernorm(x + _L1_gnn_ref(x, edge_attr_64, edge_index, L1_gnn_W1, L1_gnn_b1, L1_gnn_W2, L1_gnn_b2, L1_gnn_U1, L1_gnn_c1, L1_gnn_U2, L1_gnn_c2), axis=-1)
    x = _layernorm(x + _L2_gnn_ref(x, edge_index, L2_gnn_W1, L2_gnn_W2, L2_gnn_gamma, L2_gnn_beta, L2_gnn_t), axis=-1)
    x = _layernorm(x + _L3_gnn_ref(x, edge_attr_20, src, dst, edge_weight, L3_gnn_W_in, L3_gnn_b_in, L3_gnn_W_f, L3_gnn_b_f, L3_gnn_W_out, L3_gnn_b_out), axis=-1)
    return x

_drawn_inputs = setup_inputs


def setup_inputs(seed=0):
    import zlib

    import numpy as np

    out = dict(_drawn_inputs(seed))
    spreads = {'L0_gnn_b1': (0.0, 0.8),
     'L0_gnn_g1': (1.0, 0.2),
     'L0_gnn_bt1': (0.0, 0.1),
     'L0_gnn_b2': (0.0, 0.8),
     'L0_gnn_g2': (1.0, 0.2),
     'L0_gnn_bt2': (0.0, 0.1),
     'L0_gnn_b3': (0.0, 0.1),
     'L2_gnn_gamma': (1.0, 0.2),
     'L2_gnn_beta': (0.0, 0.1),
     'L2_gnn_t': (1.0, 0.2)}
    factors = {'L1_gnn_c1': 4.05}
    for name, (base, spread) in spreads.items():
        noise = np.random.default_rng([zlib.crc32(name.encode()), seed]).standard_normal(out[name].shape)
        drawn = base * np.exp(spread * noise) if base else spread * noise
        out[name] = jnp.asarray(drawn.astype(out[name].dtype))
    for name, factor in factors.items():
        out[name] = (out[name] * factor).astype(out[name].dtype)
    return out
```

```python
import numpy as np
import concourse.bass as bass
import concourse.mybir as mybir
from contextlib import ExitStack

F32, BF16, F16 = mybir.dt.float32, mybir.dt.bfloat16, mybir.dt.float16
I32, I16 = mybir.dt.int32, mybir.dt.int16
ALU = mybir.AluOpType
ACT = mybir.ActivationFunctionType
AX = mybir.AxisListType

N = 3125
E = 53125
D = 128
P = 125
NT = N // P
NC = E // P
CR = 85
CJ = NC // CR
U = 5
PW = 450
PIECES = [(j, j * PW, min(PW, N - j * PW)) for j in range((N + PW - 1) // PW)]
NP = len(PIECES)
ACT_P = [0, 2, 4]
DVE_P = [1, 3, 5, 6]
GL, GH = 4, 32
FE, FR = 64, 20
ROW = 24
ONE_C, RCUT_C, DST_C, SRC_C = 20, 21, 22, 23
AL, AH = 3, 256
EPS_MSG = 1e-7
EPS_BN = 1e-5
EPS_LN = 1e-5
BAND = 64.0
REACH = 70.0
LOG2 = float(np.log(2.0))
R_ADJ, R_DST, R_SRC, R_BAND = 0, 3, 6, 9
NR = 10


class Steps:

    def __init__(self, eng, sem, base=0, apart=False):
        self.eng, self.sem, self.base, self.n, self.apart = eng, sem, base, 0, apart

    def __call__(self, ins):
        self.n += 1
        ins.then_inc(self.sem, 1)
        self.eng.wait_ge(self.sem, self.base + self.n)
        if self.apart:
            self.eng.nop(nofuse=True)


class Words:

    def __init__(self, region, at=0, end=None):
        self.region, self.at, self.end = region, at, end or region.shape[1]

    def __call__(self, rows, cols, dt=F32):
        words = cols if dt in (F32, I32) else (cols + 1) // 2
        ap = self.region[:, self.at:self.at + words]
        self.at += words
        assert self.at <= self.end, (self.at, self.end)
        return (ap if dt == F32 else ap.bitcast(dt))[0:rows, 0:cols]


def build(nc, a, out):
    ctx = ExitStack()
    with ctx, nc.allow_non_contiguous_dma(reason="small columns"):
        used, held = {}, []

        def sem(name):
            used[name] = used.get(name, 0) + 1
            held.append(nc.alloc_semaphore(f"{name}_{used[name]}"))
            return held[-1]

        def phase(body, *args, **options):
            body(G, *args, **options)
            nc.clear_and_free_semaphores(held)
            held.clear()
            nc.all_engine_barrier()

        adj_all = ctx.enter_context(nc.sbuf_tensor("adj", [P, NT * N + 1], F16))
        adj = adj_all[:, 0:NT * N].rearrange("p (s n) -> p s n", n=N)
        work = ctx.enter_context(nc.sbuf_tensor("work", [128, 4 * N], F32))
        small = ctx.enter_context(nc.sbuf_tensor("small", [128, 1256], F32))
        ranges = ctx.enter_context(nc.sbuf_tensor("ranges", [1, NR * NT], I32))
        ident = ctx.enter_context(nc.sbuf_tensor("ident", [128, 128], F32))
        ps = ctx.enter_context(nc.psum_tensor("ps", [128, 8, 512], F32))
        T = [work[:, k * N:(k + 1) * N] for k in range(4)]

        p_rows = nc.dram_tensor("p_rows", (N, D), F32, kind="Internal").ap()
        h_rows = nc.dram_tensor("h_rows", (N, D), F32, kind="Internal").ap()
        edge_rows = nc.dram_tensor("edge_rows", (E, ROW), F32, kind="Internal").ap()
        deg_row = nc.dram_tensor("deg_row", (1, N), F32, kind="Internal").ap()
        x_kept = nc.dram_tensor("x_kept", (D, N), F32, kind="Internal").ap()

        G = dict(nc=nc, adj_words=adj_all[:, :].bitcast(F32), a=a, out=out, sem=sem, adj=adj, work=work, small=small, ranges=ranges, ident=ident,
                 ps=ps, T=T, p_rows=p_rows, h_rows=h_rows, edge_rows=edge_rows, deg_row=deg_row, x_kept=x_kept)
        index = Words(work, 6400)
        keep = dict(src_f=index(P, NC + 1), dst_f=index(P, NC + 1), pos_f=index(P, NC), meta=index(P, 3 * NC))
        phase(prepare, keep)
        phase(adjacency, keep)
        phase(gin)
        phase(layernorm, save_degree=True)
        phase(edge_mlp)
        phase(layernorm)
        phase(genconv)
        phase(layernorm)
        phase(interaction)
        phase(layernorm)
        phase(store)


def load_range(eng, ranges, row, w, hi):
    return [eng.value_load(ranges[0:1, bass.ds(w + NT * (row + k), 1)], min_val=lo, max_val=top)
            for k, (lo, top) in enumerate(((0, NC), (1, hi), (0, 1 << 20)))]


def prepare(G, keep):
    nc, a, sem, work, ranges, ident, ps = (G[k] for k in ("nc", "a", "sem", "work", "ranges", "ident", "ps"))
    src_f, dst_f, pos_f, meta = (keep[k] for k in ("src_f", "dst_f", "pos_f", "meta"))
    w_ = Words(work, 0, 6400)
    raw_s, raw_d, raw_r = w_(P, NC, I32), w_(P, NC, I32), w_(P, NC)
    rows_i, rows_f = w_(CR, CJ * P, I32), w_(CR, CJ * P)
    cmm, tile_lo, chunk_id, chunk_rev = w_(CR, 2 * CJ), w_(CR, NT), w_(CR, CJ), w_(CR, CJ)
    hit, hit2, keys, keym = w_(CR, NT * CJ), w_(CR, NT * CJ), w_(CR, 2 * NT), w_(CR, 2 * NT)
    table, tmp, fix, whole = w_(1, NR * NT), w_(1, NT), w_(1, NT), w_(1, NT, I32)
    zeros, bin_id, bins = w_(P, NC), w_(P, NT), w_(P, NT + 1)
    hi, fixb, whole_b = w_(P, NC), w_(P, NC), w_(P, NC, I32)
    incl, val = w_(P, NC), w_(P, NC)
    before, ones = w_(P, P, BF16), w_(P, P, BF16)
    hot = w_(P, NC, BF16)

    s_load, s_const, s_v = sem("indices_loaded"), sem("constants_ready"), sem("vector_step")
    s_keys, s_keym, s_hot, s_rank = sem("keys_ready"), sem("keys_reduced"), sem("bin_hot"), sem("bin_ranked")
    s_p = sem("pool_step")

    with nc.Block() as block:
        @block.sync
        def _(eng):
            eng.dma_start(raw_s, a["src_cols"][:, :]).then_inc(s_load, 16)
            eng.dma_start(raw_d, a["dst_cols"][:, :]).then_inc(s_load, 16)
            eng.dma_start(raw_r, a["weight_cols"][:, :]).then_inc(s_load, 16)
            eng.dma_start(rows_i, a["dst"].rearrange("(r c) -> r c", r=CR)).then_inc(s_load, 16)

        @block.gpsimd
        def _(eng):
            imprecise = dict(allow_small_or_imprecise_dtypes=True)
            step = Steps(eng, s_p)
            eng.iota(tile_lo, pattern=[[P, NT]], base=0, channel_multiplier=0, **imprecise).then_inc(s_const, 1)
            eng.iota(chunk_id, pattern=[[1, CJ]], base=1, channel_multiplier=CJ, **imprecise).then_inc(s_const, 1)
            eng.iota(bin_id, pattern=[[1, NT]], base=0, channel_multiplier=0, **imprecise).then_inc(s_const, 1)
            eng.memset(ident[:, :], 0.0)
            eng.memset(ones, 1.0).then_inc(s_const, 1)
            step(eng.memset(before, 1.0))
            eng.affine_select(out=ident[:, :], in_=ident[:, :], compare_op=ALU.not_equal, fill=1.0, base=0,
                              pattern=[[-1, 128]], channel_multiplier=1).then_inc(s_const, 1)
            eng.affine_select(out=before, in_=before, compare_op=ALU.is_gt, fill=0.0, base=0,
                              pattern=[[1, P]], channel_multiplier=-1).then_inc(s_const, 1)
            eng.wait_ge(s_keys, 1)
            eng.partition_all_reduce(keym, keys, CR, bass.bass_isa.ReduceOp.max).then_inc(s_keym, 1)

        @block.tensor
        def _(eng):
            eng.wait_ge(s_const, 6)
            with eng.Fori(0, NT) as h:
                eng.wait_ge(s_hot, h + 1)
                eng.matmul(ps[0:P, 0, 0:NC], before, hot, start=True, stop=True)
                eng.matmul(ps[0:P, 1, 0:NC], ones, hot, start=True, stop=True).then_inc(s_rank, 1)

        @block.vector
        def _(eng):
            step = Steps(eng, s_v)
            eng.wait_ge(s_load, 64)
            eng.wait_ge(s_const, 6)
            eng.tensor_copy(src_f[:, 0:NC], raw_s)
            eng.tensor_copy(dst_f[:, 0:NC], raw_d)
            eng.memset(src_f[:, NC:NC + 1], -1.0)
            eng.memset(dst_f[:, NC:NC + 1], -1.0)
            eng.memset(zeros, 0.0)
            eng.memset(pos_f, 0.0)
            eng.memset(bins, 0.0)
            m3 = meta.rearrange("p (c f) -> p c f", f=3)
            eng.tensor_copy(m3[:, :, 0], raw_r)
            eng.tensor_copy(m3[:, :, 1], raw_d)
            eng.tensor_copy(m3[:, :, 2], raw_s)
            eng.tensor_scalar(chunk_rev, chunk_id, -1.0, float(NC + 1), ALU.mult, ALU.add)
            step(eng.tensor_copy(rows_f, rows_i))

            r3 = rows_f.rearrange("p (j e) -> p j e", j=CJ)
            eng.tensor_reduce(cmm[:, 0:CJ], r3, axis=AX.X, op=ALU.min)
            step(eng.tensor_reduce(cmm[:, CJ:2 * CJ], r3, axis=AX.X, op=ALU.max))
            h3, g3 = (x.rearrange("p (w j) -> p w j", j=CJ) for x in (hit, hit2))
            lo3 = tile_lo.unsqueeze(2).to_broadcast([CR, NT, CJ])
            mn3, mx3 = (cmm[:, k * CJ:(k + 1) * CJ].unsqueeze(1).to_broadcast([CR, NT, CJ]) for k in (0, 1))
            id3, rv3 = (x.unsqueeze(1).to_broadcast([CR, NT, CJ]) for x in (chunk_id, chunk_rev))
            eng.tensor_tensor(h3, mx3, lo3, ALU.is_ge)
            step(eng.tensor_tensor(g3, mn3, lo3, ALU.subtract))
            step(eng.tensor_scalar(g3, g3, float(P), None, ALU.is_lt))
            step(eng.tensor_tensor(h3, h3, g3, ALU.mult))
            step(eng.tensor_tensor(g3, h3, rv3, ALU.mult))
            step(eng.tensor_reduce(keys[:, 0:NT], g3, axis=AX.X, op=ALU.max))
            step(eng.tensor_tensor(g3, h3, id3, ALU.mult))
            eng.tensor_reduce(keys[:, NT:2 * NT], g3, axis=AX.X, op=ALU.max).then_inc(s_keys, 1)

            step(eng.tensor_scalar(whole_b, src_f[:, 0:NC], 1.0 / P, None, ALU.mult))
            step(eng.tensor_copy(hi, whole_b))
            step(eng.tensor_scalar(fixb, hi, float(P), None, ALU.mult))
            step(eng.tensor_tensor(fixb, fixb, src_f[:, 0:NC], ALU.is_gt))
            step(eng.tensor_tensor(hi, hi, fixb, ALU.subtract))
            step(eng.tensor_scalar(fixb, hi, float(P), float(P), ALU.mult, ALU.add))
            step(eng.tensor_tensor(fixb, fixb, src_f[:, 0:NC], ALU.is_le))
            step(eng.tensor_tensor(hi, hi, fixb, ALU.add))

            at = step.n
            with eng.Fori(0, NT) as h:
                inner = Steps(eng, s_v, h * 6 + at)
                eng.tensor_scalar(hot, hi, bin_id[:, bass.ds(h, 1)], None, ALU.is_equal).then_inc(s_hot, 1)
                eng.wait_ge(s_rank, h + 1)
                rank, total = ps[0:P, 0, 0:NC], ps[0:P, 1, 0:NC]
                inner(eng.tensor_tensor_scan(incl, total, zeros, bins[:, bass.ds(h, 1)], ALU.add, ALU.add))
                inner(eng.tensor_tensor(val, incl, total, ALU.subtract))
                inner(eng.tensor_copy(bins[:, bass.ds(h + 1, 1)], incl[:, NC - 1:NC]))
                inner(eng.tensor_tensor(val, val, rank, ALU.add))
                inner(eng.tensor_tensor(val, val, hot, ALU.mult))
                inner(eng.tensor_tensor(pos_f, pos_f, val, ALU.add))
                assert inner.n == 6
            step.n = at + 6 * NT
            step(eng.tensor_scalar(whole_b, pos_f, 1.0 / P, None, ALU.mult))
            step(eng.tensor_copy(hi, whole_b))
            step(eng.tensor_scalar(fixb, hi, float(P), None, ALU.mult))
            step(eng.tensor_tensor(fixb, fixb, pos_f, ALU.is_gt))
            step(eng.tensor_tensor(hi, hi, fixb, ALU.subtract))
            step(eng.tensor_scalar(fixb, hi, float(P), float(P), ALU.mult, ALU.add))
            step(eng.tensor_tensor(fixb, fixb, pos_f, ALU.is_le))
            step(eng.tensor_tensor(hi, hi, fixb, ALU.add))
            step(eng.tensor_scalar(fixb, hi, -float(P), None, ALU.mult))
            step(eng.tensor_tensor(fixb, pos_f, fixb, ALU.add))
            step(eng.tensor_scalar(fixb, fixb, float(NC), None, ALU.mult))
            step(eng.tensor_tensor(pos_f, fixb, hi, ALU.add))

            def row(k):
                return table[:, k * NT:(k + 1) * NT]

            def ceil_div(out, x, size):
                step(eng.tensor_scalar(whole, x, 1.0 / size, None, ALU.mult))
                step(eng.tensor_copy(out, whole))
                step(eng.tensor_scalar(fix, out, float(size), None, ALU.mult))
                step(eng.tensor_tensor(fix, fix, x, ALU.is_lt))
                step(eng.tensor_tensor(out, out, fix, ALU.add))
                step(eng.tensor_scalar(fix, out, float(size), float(-size), ALU.mult, ALU.add))
                step(eng.tensor_tensor(fix, fix, x, ALU.is_ge))
                step(eng.tensor_tensor(out, out, fix, ALU.subtract))

            def steps_before(k):
                step(eng.tensor_tensor_scan(row(k + 2), row(k + 1), zeros[0:1, 0:NT], 0.0, ALU.add, ALU.add))
                step(eng.tensor_tensor(row(k + 2), row(k + 2), row(k + 1), ALU.subtract))

            def steps_of_u(k, start):
                ceil_div(row(k + 1), tmp, U)
                step(eng.tensor_scalar(row(k + 1), row(k + 1), 1.0, None, ALU.max))
                step(eng.tensor_scalar(row(k), row(k + 1), -float(U), float(NC), ALU.mult, ALU.add))
                step(eng.tensor_tensor(row(k), row(k), start, ALU.min))
                steps_before(k)

            eng.wait_ge(s_keym, 1)
            start = row(R_ADJ)
            step(eng.tensor_scalar(start, keym[0:1, 0:NT], -1.0, float(NC), ALU.mult, ALU.add))
            step(eng.tensor_scalar(start, start, float(NC - 3), None, ALU.min))
            step(eng.tensor_scalar(tmp, start, 3.0, None, ALU.add))
            step(eng.tensor_tensor(tmp, keym[0:1, NT:2 * NT], tmp, ALU.max))
            step(eng.tensor_tensor(tmp, tmp, start, ALU.subtract))
            ceil_div(row(R_ADJ + 1), tmp, 2)
            steps_before(R_ADJ)
            steps_of_u(R_DST, start)
            step(eng.tensor_scalar(tmp, bins[0:1, 0:NT], float(1 - P), None, ALU.add))
            ceil_div(row(R_BAND), tmp, P)
            ceil_div(tmp, bins[0:1, 1:NT + 1], P)
            step(eng.tensor_tensor(tmp, tmp, row(R_BAND), ALU.subtract))
            steps_of_u(R_SRC, row(R_BAND))
            eng.tensor_copy(ranges[:, :], table)


def adjacency(G, keep):
    nc, a, sem, work, ranges, ident, ps, adj = (G[k] for k in
                                                ("nc", "a", "sem", "work", "ranges", "ident", "ps", "adj"))
    small, edge_rows = G["small"], G["edge_rows"]
    src_f, dst_f, pos_f, meta = (keep[k] for k in ("src_f", "dst_f", "pos_f", "meta"))
    w_ = Words(work, 0, 6400)
    iota16 = w_(P, N, I16)
    src_hot, dst_hot = [w_(P, N, BF16) for _ in range(2)], [w_(P, P, BF16) for _ in range(2)]
    counts, zero16, ident16 = w_(P, N, F16), small[:, 0:63].bitcast(BF16)[0:P, 0:P], small[:, 64:127].bitcast(F16)[0:P, 0:P]
    s_ = Words(small, 128)
    pay = [s_(P, ROW) for _ in range(U)]
    idx = [s_(P, 1, I32) for _ in range(U)]

    s_iota, s_const = sem("iota_ready"), sem("constants_ready")
    s_hot, s_free = [sem("hots_ready") for _ in range(2)], [sem("hots_free") for _ in range(2)]
    s_tile, s_even, s_odd = sem("tile_counted"), sem("even_pieces_copied"), sem("odd_pieces_copied")
    s_tr, s_trs, s_trv = sem("blocks_transposed"), sem("blocks_stored_scalar"), sem("blocks_stored_vector")
    s_attr, s_pay = [sem("attributes_in_row") for _ in range(U)], [sem("row_and_place_ready") for _ in range(U)]
    s_sc = [sem("row_scattered") for _ in range(U)]
    edges = [0, 7, 13, 19, NT]
    groups = [range(edges[g], edges[g + 1]) for g in range(4)]
    banks = [ps[:, 7, :].bitcast(F16), ps[:, 6, :].bitcast(F16)]

    def block_store(w, g):
        n = len(groups[g])
        return (adj[:, groups[g][0]:groups[g][-1] + 1, bass.ds(w * P, P)],
                banks[g % 2][0:P, 0:128 * n].rearrange("p (b q) -> p b q", q=128)[:, :, 0:P])

    with nc.Block() as block:
        @block.sync
        def _(eng):
            def fill(q, first):
                for k in range(U):
                    if not first:
                        eng.wait_ge(s_sc[k], q * 16)
                    eng.dma_start(pay[k][:, 0:FR], a["edge_attr_20"][bass.ds((q * U + k) * P, P), :]).then_inc(s_attr[k], 16)

            fill(0, True)
            with eng.Fori(1, NC // U) as q:
                fill(q, False)
            for k in range(U):
                eng.wait_ge(s_sc[k], 16 * (NC // U))

        @block.gpsimd
        def _(eng):
            eng.iota(iota16, pattern=[[1, N]], base=0, channel_multiplier=0,
                     allow_small_or_imprecise_dtypes=True).then_inc(s_iota, 1)
            with eng.Fori(0, NC // U) as q:
                for k in range(U):
                    eng.wait_ge(s_pay[k], q + 1)
                    eng.wait_ge(s_attr[k], q * 16 + 16)
                    eng.nop(nofuse=True)
                    eng.indirect_dma_start(edge_rows[:, :], bass.IndirectOffsetOnAxis(ap=idx[k], axis=0),
                                           pay[k], None).then_inc(s_sc[k], 16)

        @block.scalar
        def _(eng):
            def place(q, k, first):
                if not first:
                    eng.wait_ge(s_sc[k], q * 16)
                eng.activation(pay[k][:, RCUT_C:ROW], meta[:, bass.ds((q * U + k) * 3, 3)], ACT.Copy)
                if first:
                    eng.activation(pay[k][:, ONE_C:ONE_C + 1], meta[:, 0:1], ACT.Copy, scale=0.0, bias=1.0)
                eng.activation(idx[k], pos_f[:, bass.ds(q * U + k, 1)], ACT.Copy).then_inc(s_pay[k], 1)

            for k in range(U):
                place(0, k, True)

            def tile(w, rows):
                for q in rows:
                    for k in range(U):
                        place(q, k, False)
                eng.wait_ge(s_tile, w + 1)
                for j in ACT_P:
                    _, c0, cw = PIECES[j]
                    ins = eng.activation(counts[:, c0:c0 + cw], ps[0:P, j, 0:cw], ACT.Copy)
                ins.then_inc(s_even, 1)
                for i, g in enumerate((0, 2)):
                    eng.wait_ge(s_tr, w * 4 + g + 1)
                    eng.activation(*block_store(w, g), ACT.Copy).then_inc(s_trs, 1)

            with eng.Fori(0, 21) as w:
                tile(w, [w * 4 + 1 + i for i in range(4)])
            with eng.Fori(21, NT) as w:
                tile(w, [])

        @block.vector
        def _(eng):
            eng.memset(zero16, 0.0).then_inc(s_const, 1)
            eng.tensor_copy(ident16, ident[0:P, 0:P]).then_inc(s_const, 1)
            eng.wait_ge(s_iota, 1)
            with eng.Fori(0, NT) as w:
                start, count, before = load_range(eng, ranges, R_ADJ, w, (NC + 2) // 2)
                with eng.Fori(0, count) as i:
                    c, t = nc.s_assert_within(start + i * 2, 0, NC - 1), before + i
                    for k in range(2):
                        eng.wait_ge(s_free[k], t + 1)
                        eng.tensor_scalar(dst_hot[k], iota16[:, bass.ds(w * P, P)], dst_f[:, bass.ds(c + k, 1)],
                                          None, ALU.is_equal)
                        eng.tensor_scalar(src_hot[k], iota16, src_f[:, bass.ds(c + k, 1)], None,
                                          ALU.is_equal).then_inc(s_hot[k], 1)
                eng.wait_ge(s_tile, w + 1)
                for j in DVE_P:
                    _, c0, cw = PIECES[j]
                    ins = eng.tensor_copy(counts[:, c0:c0 + cw], ps[0:P, j, 0:cw])
                ins.then_inc(s_odd, 1)
                for i, g in enumerate((1, 3)):
                    eng.wait_ge(s_tr, w * 4 + g + 1)
                    eng.tensor_copy(*block_store(w, g)).then_inc(s_trv, 1)

        @block.tensor
        def _(eng):
            eng.wait_ge(s_const, 2)
            eng.nop(nofuse=True).then_inc(s_free[0], 1)
            eng.nop(nofuse=True).then_inc(s_free[1], 1)

            def pair(t, start):
                for k in range(2):
                    eng.wait_ge(s_hot[k], t + 1)
                    for j, c0, cw in PIECES:
                        ins = eng.matmul(ps[0:P, j, 0:cw], dst_hot[k], src_hot[k][:, c0:c0 + cw],
                                         start=start and k == 0, stop=False, skip_group_check=True)
                    ins.then_inc(s_free[k], 1)

            with eng.Fori(0, NT) as w:
                _, count, before = load_range(eng, ranges, R_ADJ, w, (NC + 2) // 2)
                pair(before, True)
                with eng.Fori(1, count) as i:
                    pair(before + i, False)
                eng.matmul(ps[0:P, NP - 1, 0:1], zero16, zero16[:, 0:1], start=False, stop=True,
                           skip_group_check=True).then_inc(s_tile, 1)
                eng.wait_ge(s_even, w + 1)
                eng.wait_ge(s_odd, w + 1)
                for g, blocks in enumerate(groups):
                    if g == 2:
                        eng.wait_ge(s_trs, w * 2 + 1)
                    if g == 3:
                        eng.wait_ge(s_trv, w * 2 + 1)
                    for b, s in enumerate(blocks):
                        ins = eng.transpose(banks[g % 2][0:P, b * 128:b * 128 + P], counts[:, s * P:s * P + P],
                                            ident16)
                    ins.then_inc(s_tr, 1)
                eng.wait_ge(s_trs, w * 2 + 2)
                eng.wait_ge(s_trv, w * 2 + 2)


def gin(G):
    nc, a, sem, small, ident, ps, adj, T, deg_row = (
        G[k] for k in ("nc", "a", "sem", "small", "ident", "ps", "adj", "T", "deg_row"))
    s_ = Words(small)
    w1, w2, w3 = s_(D, GL * GH), s_(GH, GL * GH), s_(GH, GL * D)
    vec = s_(GH, 6 * GL)
    b3, eps = s_(D, GL), s_(D, GL)
    w1l, w1e, w2l, w3l = s_(D, GH), s_(D, GH), s_(GH, GH), s_(GH, D)
    vl, b3l = s_(GH, 6), s_(D, 1)
    merge = s_(3 * GH + 1, GH)
    stats, mv, sd, scale, shift, tmp = s_(GH, 6 * NP), s_(GH, 2), s_(GH, 1), s_(GH, 1), s_(GH, 1), s_(GH, 1)
    epsc = s_(GH, 1)
    YW = 3 * GH + 2
    y_hbm = Words(T[3])
    parts = y_hbm(P, NT * YW, BF16).rearrange("p (s c) -> p s c", c=YW)
    rest = y_hbm(P, NT * GH).rearrange("p (s c) -> p s c", c=GH)
    X, S, zb, h = T[1], T[2], T[3][0:GH, :], T[2][0:GH, :]
    halves = [(0, 0, 16), (1, 16, NT)]

    s_load, s_merge, s_v, s_a = sem("weights_loaded"), sem("merge_ready"), sem("vector_step"), sem("scalar_step")
    s_wl, s_xa, s_xv = sem("layer_weights_ready"), sem("x_by_scalar"), sem("x_by_vector")
    s_y, s_hi, s_parts = sem("y_ready"), sem("y_high_ready"), sem("y_parts_ready")
    s_sum, s_sa, s_sv = sem("piece_summed"), sem("sum_by_scalar"), sem("sum_by_vector")
    s_z = [sem("z1_ready"), sem("z2_ready")]
    s_zb, s_var, s_sd, s_aff, s_h = ([sem(f"{n}{i}") for i in (1, 2)] for n in
                                     ("biased", "variance", "deviation", "affine", "hidden"))
    s_x = sem("x_product_ready")

    with nc.Block() as block:
        @block.sync
        def _(eng):
            for dst, src in ((T[0], a["x"]), (w1, a["gin_w1"]), (w2, a["gin_w2"]), (w3, a["gin_w3"]),
                             (b3, a["gin_b3"]),
                             (eps, a["gin_eps"].rearrange("(o l) -> o l", o=1).to_broadcast([D, GL]))):
                eng.dma_start(dst, src).then_inc(s_load, 16)
            for i, name in enumerate(("b1", "g1", "bt1", "b2", "g2", "bt2")):
                eng.dma_start(vec[:, i * GL:(i + 1) * GL], a["gin_" + name]).then_inc(s_load, 16)

        @block.vector
        def _(eng):
            once = Steps(eng, s_v)
            eng.memset(epsc, EPS_BN)
            once(eng.memset(merge, 0.0))
            for i in range(3):
                ins = eng.tensor_copy(merge[i * GH:(i + 1) * GH, :], ident[i * GH:(i + 1) * GH, i * GH:(i + 1) * GH])
            ins.then_inc(s_merge, 1)
            eng.wait_ge(s_load, 192)
            once(eng.tensor_scalar(eps, eps, 1.0, None, ALU.add))
            for j in DVE_P:
                _, c0, cw = PIECES[j]
                eng.tensor_copy(X[:, c0:c0 + cw], T[0][:, c0:c0 + cw]).then_inc(s_xv, 1)
            first = once.n
            PER = 12
            with eng.Fori(0, GL) as l:
                step = Steps(eng, s_v, l * PER + first)
                eng.wait_ge(s_xa, (l + 1) * len(ACT_P))
                eng.wait_ge(s_xv, (l + 1) * len(DVE_P))
                eng.tensor_copy(w1l, w1[:, bass.ds(l * GH, GH)])
                eng.tensor_scalar(w1e, w1[:, bass.ds(l * GH, GH)], eps[:, bass.ds(l, 1)], None, ALU.mult)
                eng.tensor_copy(w2l, w2[:, bass.ds(l * GH, GH)])
                eng.tensor_copy(w3l, w3[:, bass.ds(l * D, D)])
                eng.tensor_copy(vl, vec.rearrange("p (i l) -> p i l", l=GL)[:, :, bass.ds(l, 1)].rearrange("p i o -> p (i o)"))
                eng.tensor_copy(b3l, b3[:, bass.ds(l, 1)])
                eng.memset(parts[:, :, 3 * GH:YW], 1.0).then_inc(s_wl, 1)
                for b, s0, s1 in halves:
                    y = ps[0:P, b, 0:(s1 - s0) * GH].rearrange("p (s c) -> p s c", c=GH)
                    eng.wait_ge(s_hi, l * 2 + b + 1)
                    step(eng.tensor_tensor(rest[:, s0:s1, :], y, parts[:, s0:s1, 0:GH], ALU.subtract))
                    step(eng.tensor_copy(parts[:, s0:s1, GH:2 * GH], rest[:, s0:s1, :]))
                    eng.tensor_tensor(parts[:, s0:s1, 2 * GH:3 * GH], rest[:, s0:s1, :],
                                      parts[:, s0:s1, GH:2 * GH], ALU.subtract).then_inc(s_parts, 1)
                for i, j in enumerate(DVE_P):
                    _, c0, cw = PIECES[j]
                    eng.wait_ge(s_sum, l * NP + j + 1)
                    eng.tensor_copy(S[0:YW - 1, c0:c0 + cw], ps[0:YW - 1, j, 0:cw]).then_inc(s_sv, 1)
                for n in range(2):
                    for j, c0, cw in PIECES:
                        eng.wait_ge(s_zb[n], l * NP + j + 1)
                        ins = eng.bn_stats(stats[:, 6 * j:6 * j + 6], zb[:, c0:c0 + cw])
                    step(ins)
                    eng.nop(nofuse=True)
                    eng.bn_aggr(mv, stats.rearrange("p (j f) -> p j f", f=6)).then_inc(s_var[n], 1)
                    eng.wait_ge(s_sd[n], l + 1)
                    step(eng.reciprocal(scale, sd))
                    step(eng.tensor_tensor(scale, scale, vl[:, 3 * n + 1:3 * n + 2], ALU.mult))
                    step(eng.tensor_tensor(tmp, mv[:, 0:1], scale, ALU.mult))
                    eng.tensor_tensor(shift, vl[:, 3 * n + 2:3 * n + 3], tmp, ALU.subtract).then_inc(s_aff[n], 1)
                for j in DVE_P:
                    _, c0, cw = PIECES[j]
                    eng.wait_ge(s_x, l * NP + j + 1)
                    eng.tensor_scalar(X[:, c0:c0 + cw], ps[:, j, 0:cw], b3l, None, ALU.add).then_inc(s_xv, 1)
                assert step.n == PER, step.n

        @block.scalar
        def _(eng):
            eng.wait_ge(s_load, 192)
            for j in ACT_P:
                _, c0, cw = PIECES[j]
                eng.activation(X[:, c0:c0 + cw], T[0][:, c0:c0 + cw], ACT.Copy).then_inc(s_xa, 1)
            with eng.Fori(0, GL) as l:
                for b, s0, s1 in halves:
                    eng.wait_ge(s_y, l * 2 + b + 1)
                    eng.activation(parts[:, s0:s1, 0:GH],
                                   ps[0:P, b, 0:(s1 - s0) * GH].rearrange("p (s c) -> p s c", c=GH),
                                   ACT.Copy).then_inc(s_hi, 1)
                for j in ACT_P:
                    _, c0, cw = PIECES[j]
                    eng.wait_ge(s_sum, l * NP + j + 1)
                    eng.activation(S[0:YW - 1, c0:c0 + cw], ps[0:YW - 1, j, 0:cw], ACT.Copy).then_inc(s_sa, 1)
                for n in range(2):
                    for j, c0, cw in PIECES:
                        eng.wait_ge(s_z[n], l * NP + j + 1)
                        eng.activation(zb[:, c0:c0 + cw], ps[0:GH, j, 0:cw], ACT.Identity,
                                       bias=vl[:, 3 * n:3 * n + 1]).then_inc(s_zb[n], 1)
                    eng.wait_ge(s_var[n], l + 1)
                    eng.activation(sd, mv[:, 1:2], ACT.Sqrt, bias=epsc).then_inc(s_sd[n], 1)
                    eng.wait_ge(s_aff[n], l + 1)
                    for j, c0, cw in PIECES:
                        eng.activation(h[:, c0:c0 + cw], zb[:, c0:c0 + cw], ACT.Relu, bias=shift,
                                       scale=scale).then_inc(s_h[n], 1)
                for j in ACT_P:
                    _, c0, cw = PIECES[j]
                    eng.wait_ge(s_x, l * NP + j + 1)
                    eng.activation(X[:, c0:c0 + cw], ps[:, j, 0:cw], ACT.Identity, bias=b3l).then_inc(s_xa, 1)

        @block.tensor
        def _(eng):
            eng.wait_ge(s_merge, 1)
            with eng.Fori(0, GL) as l:
                eng.wait_ge(s_wl, l + 1)
                eng.wait_ge(s_xa, (l + 1) * len(ACT_P))
                eng.wait_ge(s_xv, (l + 1) * len(DVE_P))
                for b, s0, s1 in halves:
                    for s in range(s0, s1):
                        ins = eng.matmul(ps[0:P, b, (s - s0) * GH:(s - s0 + 1) * GH], X[:, s * P:(s + 1) * P], w1l,
                                         start=True, stop=True)
                    ins.then_inc(s_y, 1)
                eng.wait_ge(s_parts, l * 2 + 2)

                def tile(s, start, last):
                    for j, c0, cw in PIECES:
                        if isinstance(s, int):
                            w, m = parts[:, s, 0:YW - 1], adj[:, s, c0:c0 + cw]
                        else:
                            w = parts[:, bass.ds(s, 1), 0:YW - 1].rearrange("p o c -> p (o c)")
                            m = adj[:, bass.ds(s, 1), c0:c0 + cw].rearrange("p o c -> p (o c)")
                        ins = eng.matmul(ps[0:YW - 1, j, 0:cw], w, m, start=start, stop=last, skip_group_check=True)
                        if last:
                            ins.then_inc(s_sum, 1)

                tile(0, True, False)
                with eng.Fori(1, NT - 1) as s:
                    tile(s, False, False)
                tile(NT - 1, False, True)
                for j, c0, cw in PIECES:
                    if j in ACT_P:
                        eng.wait_ge(s_sa, l * len(ACT_P) + ACT_P.index(j) + 1)
                    else:
                        eng.wait_ge(s_sv, l * len(DVE_P) + DVE_P.index(j) + 1)
                    eng.matmul(ps[0:GH, j, 0:cw], merge, S[0:YW - 1, c0:c0 + cw], start=True, stop=False)
                    eng.matmul(ps[0:GH, j, 0:cw], w1e, X[:, c0:c0 + cw], start=False, stop=True).then_inc(s_z[0], 1)
                for j, c0, cw in PIECES:
                    eng.wait_ge(s_h[0], l * NP + j + 1)
                    eng.nop(nofuse=True)
                    eng.matmul(ps[0:GH, j, 0:cw], w2l, h[:, c0:c0 + cw], start=True, stop=True).then_inc(s_z[1], 1)
                for j, c0, cw in PIECES:
                    eng.wait_ge(s_h[1], l * NP + j + 1)
                    eng.matmul(ps[:, j, 0:cw], w3l, h[:, c0:c0 + cw], start=True, stop=True).then_inc(s_x, 1)


def layernorm(G, save_degree=False):
    nc, sem, small, ps, T, deg_row = (G[k] for k in ("nc", "sem", "small", "ps", "T", "deg_row"))
    s_ = Words(small)
    ones, epsc = s_(D, D), s_(D, 1)
    z, d, sq = T[1], T[2], T[3]
    s_const, s_z, s_mean, s_d, s_sq = (sem(n) for n in ("constants_ready", "residual_added", "mean_ready",
                                                        "centred", "squared"))
    s_var, s_sd, s_inv, s_deg = (sem(n) for n in ("variance_ready", "deviation_ready", "inverted", "degree_saved"))
    with nc.Block() as block:
        @block.sync
        def _(eng):
            if save_degree:
                eng.dma_start(deg_row[:, :], T[2][3 * GH:3 * GH + 1, :]).then_inc(s_deg, 16)
                eng.wait_ge(s_deg, 16)

        @block.vector
        def _(eng):
            eng.memset(epsc, EPS_LN)
            eng.memset(ones, 1.0 / D).then_inc(s_const, 1)
            for j, c0, cw in PIECES:
                eng.tensor_tensor(z[:, c0:c0 + cw], T[0][:, c0:c0 + cw], z[:, c0:c0 + cw], ALU.add).then_inc(s_z, 1)
            if save_degree:
                eng.wait_ge(s_deg, 16)
            for j, c0, cw in PIECES:
                eng.wait_ge(s_mean, j + 1)
                eng.tensor_tensor(d[:, c0:c0 + cw], z[:, c0:c0 + cw], ps[:, j, 0:cw], ALU.subtract).then_inc(s_d, 1)
            for j, c0, cw in PIECES:
                eng.wait_ge(s_sd, j + 1)
                eng.reciprocal(sq[:, c0:c0 + cw], sq[:, c0:c0 + cw]).then_inc(s_inv, 1)
                eng.wait_ge(s_inv, j + 1)
                eng.tensor_tensor(T[0][:, c0:c0 + cw], d[:, c0:c0 + cw], sq[:, c0:c0 + cw], ALU.mult)

        @block.tensor
        def _(eng):
            eng.wait_ge(s_const, 1)
            for j, c0, cw in PIECES:
                eng.wait_ge(s_z, j + 1)
                eng.matmul(ps[:, j, 0:cw], ones, z[:, c0:c0 + cw], start=True, stop=True).then_inc(s_mean, 1)
            for j, c0, cw in PIECES:
                eng.wait_ge(s_sq, j + 1)
                eng.matmul(ps[:, j, 0:cw], ones, sq[:, c0:c0 + cw], start=True, stop=True).then_inc(s_var, 1)

        @block.scalar
        def _(eng):
            for j, c0, cw in PIECES:
                eng.wait_ge(s_d, j + 1)
                eng.activation(sq[:, c0:c0 + cw], d[:, c0:c0 + cw], ACT.Square).then_inc(s_sq, 1)
            eng.wait_ge(s_const, 1)
            for j, c0, cw in PIECES:
                eng.wait_ge(s_var, j + 1)
                eng.activation(sq[:, c0:c0 + cw], ps[:, j, 0:cw], ACT.Sqrt, bias=epsc).then_inc(s_sd, 1)


def edge_mlp(G):
    nc, a, sem, work, small, ranges, ident, ps, T, p_rows, deg_row = (
        G[k] for k in ("nc", "a", "sem", "work", "small", "ranges", "ident", "ps", "T", "p_rows", "deg_row"))
    x, R = T[0], T[2]
    q_rows = work[0:P, 4 * N - NT * D:4 * N].rearrange("p (s c) -> p s c", c=D)
    r_ = Words(work, N, 2 * N)
    src_i, dst_f = r_(P, NC, I32), r_(P, NC)
    row_ring = r_(P, U * D)
    rows = [row_ring[:, k * D:(k + 1) * D] for k in range(U)]
    stage = [T[2][0:P, g * 512:(g + 1) * 512] for g in range(5)] + [row_ring[:, 0:512], row_ring[:, 512:640]]
    wa, wb = r_(D, D), r_(D, D)
    hots = r_(P, U * P)
    hot = [hots[:, k * P:(k + 1) * P] for k in range(U)]
    dst_i = hots[:, 0:NC].bitcast(I32)
    tile_lo, iota, b1 = r_(P, NT), r_(P, P), r_(P, D)
    idx = [r_(P, 1, I32) for _ in range(U)]
    s_ = Words(small)
    attr = [s_(FE, P) for _ in range(U)]
    w1e, zero = s_(FE, D), s_(1, D)
    hot_t = [s_(P, P) for _ in range(3)] + [r_(P, P) for _ in range(U - 3)]
    groups = [(g, range(4 * g, min(NT, 4 * g + 4))) for g in range((NT + 3) // 4)]

    s_load, s_const, s_v = sem("weights_loaded"), sem("constants_ready"), sem("vector_step")
    s_rows, s_p, s_q, s_prow = sem("rows_ready"), sem("p_read_out"), sem("q_read_out"), sem("p_rows_written")
    s_idx, s_g, s_attr = sem("index_ready"), [sem("row_gathered") for _ in range(U)], [sem("attributes") for _ in range(U)]
    s_hot, s_tr, s_ht = sem("hot_ready"), sem("hot_transposed"), sem("hot_t_ready")
    s_pre, s_sum, s_relu, s_agg = sem("products_ready"), sem("preactivation"), sem("relu_ready"), sem("edges_summed")
    s_tile, s_ev = sem("tile_summed"), sem("tile_read_out")
    SUM = ps[:, 7, 0:P]

    def units(eng, body, begin=None, end=None):
        with eng.Fori(0, NT) as w:
            start, count, before = load_range(eng, ranges, R_DST, w, NC // U)
            if begin:
                begin(w)
            with eng.Fori(0, count) as u:
                body(w, nc.s_assert_within(start + u * U, 0, NC - U), before + u)
            if end:
                end(w)

    with nc.Block() as block:
        @block.sync
        def _(eng):
            for dst, src in ((src_i, a["src_cols"]), (dst_i, a["dst_cols"]), (wa, a["mlp_w1a"]),
                             (wb, a["mlp_w1b"]), (w1e, a["mlp_w1e"]),
                             (b1, a["mlp_b1"].rearrange("(o c) -> o c", o=1).to_broadcast([P, D]))):
                eng.dma_start(dst, src).then_inc(s_load, 16)
            p_view = p_rows.rearrange("(s p) c -> p s c", p=P)
            for g, tiles in groups:
                eng.wait_ge(s_p, g + 1)
                eng.dma_start(p_view[:, tiles[0]:tiles[-1] + 1, :],
                              stage[g].rearrange("p (s c) -> p s c", c=D)).then_inc(s_prow, 16)

            def body(w, c, q):
                for k in range(U):
                    eng.wait_ge(s_pre, q * U + k + 1)
                    eng.dma_start(attr[k], a["edge_attr_64"][:, bass.ds((c + k) * P, P)]).then_inc(s_attr[k], 16)

            units(eng, body)

        @block.gpsimd
        def _(eng):
            imprecise = dict(allow_small_or_imprecise_dtypes=True)
            eng.iota(tile_lo, pattern=[[P, NT]], base=0, channel_multiplier=0, **imprecise).then_inc(s_const, 1)
            eng.iota(iota, pattern=[[1, P]], base=0, channel_multiplier=0, **imprecise).then_inc(s_const, 1)
            eng.memset(zero, 0.0).then_inc(s_const, 1)
            eng.wait_ge(s_load, 96)
            eng.wait_ge(s_prow, 16 * len(groups))

            def body(w, c, q):
                for k in range(U):
                    eng.wait_ge(s_agg, q * U + k + 1)
                    eng.tensor_copy(idx[k], src_i[:, bass.ds(c + k, 1)]).then_inc(s_idx, 1)
                    eng.wait_ge(s_idx, q * U + k + 1)
                    eng.nop(nofuse=True)
                    eng.indirect_dma_start(rows[k], None, p_rows[:, :],
                                           bass.IndirectOffsetOnAxis(ap=idx[k], axis=0)).then_inc(s_g[k], 16)

            units(eng, body)

        @block.vector
        def _(eng):
            eng.wait_ge(s_load, 96)
            eng.tensor_copy(dst_f, dst_i).then_inc(s_v, 1)
            for g, tiles in groups:
                n = len(tiles)
                eng.wait_ge(s_rows, g + 1)
                eng.tensor_tensor(q_rows[:, tiles[0]:tiles[-1] + 1, :],
                                  ps[0:P, 4 + g % 4, 0:n * D].rearrange("p (s c) -> p s c", c=D),
                                  b1.unsqueeze(1).to_broadcast([P, n, D]), ALU.add).then_inc(s_q, 1)
            eng.wait_ge(s_v, 1)
            eng.wait_ge(s_const, 3)

            def body(w, c, q):
                for k in range(U):
                    eng.wait_ge(s_agg, q * U + k + 1)
                    eng.tensor_scalar(hot[k], iota, tile_lo[:, bass.ds(w, 1)], dst_f[:, bass.ds(c + k, 1)],
                                      ALU.add, ALU.is_equal).then_inc(s_hot, 1)
                for k in range(U):
                    eng.wait_ge(s_pre, q * U + k + 1 + U)
                    eng.wait_ge(s_g[k], q * 16 + 16)
                    eng.tensor_tensor(rows[k], ps[0:P, k, 0:D], rows[k], ALU.add).then_inc(s_sum, 1)

            units(eng, body)

        @block.scalar
        def _(eng):
            for g, tiles in groups:
                eng.wait_ge(s_rows, g + 1)
                eng.activation(stage[g], ps[0:P, g % 4, 0:len(tiles) * D], ACT.Copy).then_inc(s_p, 1)

            def body(w, c, q):
                def transposed(k):
                    eng.wait_ge(s_tr, q * U + k + 1)
                    eng.activation(hot_t[k], ps[0:P, 5 + k % 2, 0:P], ACT.Copy).then_inc(s_ht, 1)

                def relu(k):
                    eng.wait_ge(s_sum, q * U + k + 1)
                    eng.activation(rows[k], rows[k], ACT.Relu).then_inc(s_relu, 1)

                transposed(0)
                transposed(1)
                transposed(2)
                relu(0)
                transposed(3)
                relu(1)
                transposed(4)
                relu(2)
                relu(3)
                relu(4)

            def end(w):
                eng.wait_ge(s_tile, w + 1)
                eng.activation(R[:, bass.ds(w * P, P)], SUM, ACT.Copy).then_inc(s_ev, 1)

            units(eng, body, end=end)

        @block.tensor
        def _(eng):
            eng.wait_ge(s_load, 96)
            for g, tiles in groups:
                if g >= 4:
                    eng.wait_ge(s_p, g - 3)
                    eng.wait_ge(s_q, g - 3)
                for b, w in ((g % 4, wa), (4 + g % 4, wb)):
                    for i, s in enumerate(tiles):
                        ins = eng.matmul(ps[0:P, b, i * D:(i + 1) * D], x[:, s * P:(s + 1) * P], w,
                                         start=True, stop=True)
                ins.then_inc(s_rows, 1)
            eng.wait_ge(s_p, len(groups))
            eng.wait_ge(s_q, len(groups))
            eng.wait_ge(s_const, 3)
            for _ in range(U):
                eng.nop(nofuse=True).then_inc(s_agg, 1)
                eng.nop(nofuse=True).then_inc(s_pre, 1)
            eng.nop(nofuse=True).then_inc(s_ev, 1)

            def begin(w):
                eng.wait_ge(s_ev, w + 1)
                eng.nop(nofuse=True)
                eng.matmul(SUM, zero, zero[:, 0:P], start=True, stop=False, skip_group_check=True)

            def body(w, c, q):
                def transpose(k):
                    eng.wait_ge(s_hot, q * U + k + 1)
                    if k >= 2:
                        eng.wait_ge(s_ht, q * U + k - 1)
                    eng.transpose(ps[0:P, 5 + k % 2, 0:P], hot[k], ident[0:P, 0:P]).then_inc(s_tr, 1)

                def products(k):
                    eng.wait_ge(s_ht, q * U + k + 1)
                    eng.matmul(ps[0:P, k, 0:D], hot_t[k],
                               q_rows[:, bass.ds(w, 1), :].rearrange("p o c -> p (o c)"), start=True, stop=False)
                    eng.wait_ge(s_attr[k], q * 16 + 16)
                    eng.matmul(ps[0:P, k, 0:D], attr[k], w1e, start=False, stop=True).then_inc(s_pre, 1)

                def total(k):
                    eng.wait_ge(s_relu, q * U + k + 1)
                    eng.matmul(SUM, rows[k], hot[k], start=False, stop=False, skip_group_check=True).then_inc(s_agg, 1)

                transpose(0)
                transpose(1)
                products(0)
                transpose(2)
                products(1)
                transpose(3)
                total(0)
                products(2)
                transpose(4)
                total(1)
                products(3)
                total(2)
                products(4)
                total(3)
                total(4)

            def end(w):
                eng.matmul(SUM, zero, zero[:, 0:P], start=False, stop=True, skip_group_check=True).then_inc(s_tile, 1)

            units(eng, body, begin, end)

    n_ = Words(small)
    w2, u1a, u1b, u2 = (n_(D, D) for _ in range(4))
    b2, c1, c2 = n_(1, D), n_(D, 1), n_(D, 1)
    deg, agg, out = T[3][0:1, :], T[1], T[1]
    s_load, s_m, s_mo = sem("weights_loaded"), sem("messages_ready"), sem("messages_read_out")
    s_u, s_uo, s_o = sem("hidden_ready"), sem("hidden_read_out"), sem("update_ready")
    with nc.Block() as block:
        @block.sync
        def _(eng):
            for dst, src in ((w2, a["mlp_w2"]), (u1a, a["mlp_u1a"]), (u1b, a["mlp_u1b"]), (u2, a["mlp_u2"]),
                             (b2, a["mlp_b2"].rearrange("(o c) -> o c", o=1)), (deg, deg_row),
                             (c1, a["mlp_c1"].rearrange("(c o) -> c o", o=1)),
                             (c2, a["mlp_c2"].rearrange("(c o) -> c o", o=1))):
                eng.dma_start(dst, src).then_inc(s_load, 16)

        @block.tensor
        def _(eng):
            eng.wait_ge(s_load, 128)
            for j, c0, cw in PIECES:
                eng.matmul(ps[:, j, 0:cw], w2, R[:, c0:c0 + cw], start=True, stop=False)
                eng.matmul(ps[:, j, 0:cw], b2, deg[:, c0:c0 + cw], start=False, stop=True).then_inc(s_m, 1)
            for j, c0, cw in PIECES:
                eng.wait_ge(s_mo, j + 1)
                eng.matmul(ps[:, j, 0:cw], u1b, agg[:, c0:c0 + cw], start=True, stop=False)
                eng.matmul(ps[:, j, 0:cw], u1a, x[:, c0:c0 + cw], start=False, stop=True).then_inc(s_u, 1)
            for j, c0, cw in PIECES:
                eng.wait_ge(s_uo, j + 1)
                eng.matmul(ps[:, j, 0:cw], u2, R[:, c0:c0 + cw], start=True, stop=True).then_inc(s_o, 1)

        @block.vector
        def _(eng):
            for j, c0, cw in PIECES:
                eng.wait_ge(s_m, j + 1)
                eng.tensor_copy(agg[:, c0:c0 + cw], ps[:, j, 0:cw]).then_inc(s_mo, 1)
            for j, c0, cw in PIECES:
                eng.wait_ge(s_o, j + 1)
                eng.tensor_scalar(out[:, c0:c0 + cw], ps[:, j, 0:cw], c2, None, ALU.add)

        @block.scalar
        def _(eng):
            for j, c0, cw in PIECES:
                eng.wait_ge(s_u, j + 1)
                eng.activation(R[:, c0:c0 + cw], ps[:, j, 0:cw], ACT.Relu, bias=c1).then_inc(s_uo, 1)


def genconv(G):
    nc, a, sem, small, ranges, ident, ps, adj, T, x_kept = (
        G[k] for k in ("nc", "a", "sem", "small", "ranges", "ident", "ps", "adj", "T", "x_kept"))
    acc, x, z, den = T
    h1 = [T[2], T[3]]
    w2 = T[0][:, 0:2 * D].rearrange("p (k c) -> p k c", k=2)
    s_ = Words(small)
    parts = [s_(P, 3 * D, BF16) for _ in range(2)]
    e = [s_(D, P) for _ in range(2)]
    m, rest = s_(D, P), s_(P, D)
    w1 = s_(D, AH)
    vec = s_(D, 4)
    t_all = s_(D, AL)
    ext, lim, spread, top = s_(D, 2), s_(D, 2), s_(D, 1), s_(D, 1)
    shift_s, t_l, before_f, steps_f = s_(D, 1), s_(D, 1), s_(1, 1), s_(1, 1)
    stats, mv, sd, scale, shift, tmp, epsc = (s_(D, n) for n in (6 * NP, 2, 1, 2, 2, 1, 1))
    MISC = ps[0:P, 7, 0:D]
    SL = (N - 1) // 11

    s_saved, s_t, s_w1, s_w2 = sem("x_saved"), sem("t_loaded"), sem("w1_loaded"), sem("w2_loaded")
    s_v, s_spread, s_top, s_band = sem("vector_step"), sem("spread_ready"), sem("spread_reduced"), sem("bands_ready")
    s_z, s_e, s_m, s_f = sem("exponents_ready"), sem("exp_ready"), sem("message_ready"), sem("weighted_ready")
    s_tr, s_hi, s_rest, s_mid, s_parts = (sem(n) for n in ("transposed", "high_ready", "rest_ready", "middle_ready",
                                                           "parts_ready"))
    s_used, s_sum, s_dena, s_denv = (sem(n) for n in ("parts_used", "piece_summed", "den_by_scalar", "den_by_vector"))
    s_inv, s_num, s_agg, s_h = sem("den_step"), sem("sums_combined"), sem("aggregate_step"), sem("node_input_ready")
    s_h1, s_h1o, s_var, s_sd, s_aff, s_r1 = (sem(n) for n in ("hidden_product", "hidden_read_out", "variance",
                                                              "deviation", "affine", "hidden_ready"))
    s_x, s_xa, s_xv, s_fin, s_back = (sem(n) for n in ("x_product", "x_by_scalar", "x_by_vector", "weights_free",
                                                       "x_restored"))

    def bands(eng, l):
        return [eng.value_load(ranges[0:1, bass.ds(l * 2 + NT * R_BAND + k, 1)], min_val=lo, max_val=1 << 20)
                for k, lo in ((0, 1), (1, 0))]

    def tiles(eng, body, middle=None):
        body(0, 0, True, False)
        with eng.Fori(0, 11) as i:
            body(i * 2 + 1, 1, False, False)
            body(i * 2 + 2, 0, False, False)
            if middle:
                middle(i)
        body(23, 1, False, False)
        body(24, 0, False, True)

    def tile_cols(table, s):
        return table[:, s * P:(s + 1) * P] if isinstance(s, int) else table[:, bass.ds(s * P, P)]

    with nc.Block() as block:
        @block.sync
        def _(eng):
            eng.dma_start(t_all, a["agg_t"].rearrange("(o l) -> o l", o=1).to_broadcast([D, AL])).then_inc(s_t, 16)
            eng.dma_start(x_kept[:, :], T[0]).then_inc(s_saved, 16)
            with eng.Fori(0, AL) as l:
                eng.wait_ge(s_fin, l + 1)
                eng.dma_start(w1, a["agg_w1"][:, bass.ds(l * AH, AH)]).then_inc(s_w1, 16)
                eng.dma_start(vec, a["agg_vec"][:, bass.ds(l * 4, 4)]).then_inc(s_w1, 16)
                eng.wait_ge(s_h, (l + 1) * NP)
                eng.dma_start(w2, a["agg_w2"][:, bass.ds(l * 2, 2), :]).then_inc(s_w2, 16)
            eng.wait_ge(s_fin, AL + 1)
            eng.dma_start(T[0], x_kept[:, :]).then_inc(s_back, 16)
            eng.wait_ge(s_back, 16)

        @block.gpsimd
        def _(eng):
            with eng.Fori(0, AL) as l:
                eng.wait_ge(s_spread, l + 1)
                eng.nop(nofuse=True)
                eng.partition_all_reduce(top, spread, D, bass.bass_isa.ReduceOp.max).then_inc(s_top, 1)

        @block.vector
        def _(eng):
            once = Steps(eng, s_v)
            eng.memset(epsc, EPS_BN)
            once(eng.memset(before_f, 0.0))
            eng.tensor_copy(x, T[0])
            once(eng.memset(tmp, 0.0))
            eng.wait_ge(s_t, 16)
            eng.wait_ge(s_saved, 16)
            first = once.n
            PER = 18
            with eng.Fori(0, AL) as l:
                step = Steps(eng, s_v, l * PER + first)
                eng.wait_ge(s_xa, l * len(ACT_P) + 1)
                eng.wait_ge(s_xv, l * len(DVE_P) + 1)
                eng.tensor_copy(t_l, t_all[:, bass.ds(l, 1)])
                eng.memset(acc, 0.0)
                eng.tensor_reduce(ext[:, 0:1], x, axis=AX.X, op=ALU.max)
                step(eng.tensor_reduce(ext[:, 1:2], x, axis=AX.X, op=ALU.min))
                step(eng.tensor_scalar(ext, ext, 0.0, EPS_MSG, ALU.max, ALU.add))
                step(eng.tensor_scalar(ext, ext, t_l, None, ALU.mult))
                eng.tensor_reduce(lim[:, 0:1], ext, axis=AX.X, op=ALU.max)
                step(eng.tensor_reduce(lim[:, 1:2], ext, axis=AX.X, op=ALU.min))
                step(eng.tensor_tensor(spread, lim[:, 0:1], lim[:, 1:2], ALU.subtract))
                step(eng.tensor_scalar(spread, spread, BAND - REACH, 1.0 / BAND, ALU.add, ALU.mult))
                eng.tensor_scalar(spread, spread, 0.0, float(1 << 19), ALU.max, ALU.min).then_inc(s_spread, 1)
                step(eng.tensor_copy(shift_s, lim[:, 0:1]))
                eng.wait_ge(s_top, l + 1)
                step.apart = True
                bl = ranges[0:1, bass.ds(l * 2 + NT * R_BAND, 1)]
                step(eng.tensor_scalar(bl, top[0:1, :], 1.0, None, ALU.add))
                step(eng.tensor_copy(ranges[0:1, bass.ds(l * 2 + NT * R_BAND + 1, 1)], before_f))
                step(eng.tensor_copy(steps_f, bl))
                eng.tensor_tensor(before_f, before_f, steps_f, ALU.add).then_inc(s_band, 1)
                step.apart = False
                eng.wait_ge(s_band, l + 1)
                eng.nop(nofuse=True)
                count, before = bands(eng, l)
                with eng.Fori(0, count) as b:
                    r = before + b
                    zs = Steps(eng, s_agg, r * (NP + 3))
                    for c0, c1 in ((0, P), (P, N)):
                        zc, xc = z[:, c0:c1], x[:, c0:c1]
                        zs(eng.tensor_scalar(zc, xc, 0.0, EPS_MSG, ALU.max, ALU.add))
                        eng.tensor_scalar(zc, zc, t_l, shift_s, ALU.mult, ALU.subtract).then_inc(s_z, 1)
                        eng.wait_ge(s_z, r * 4 + (2 if c0 else 0) + 1)
                        eng.tensor_scalar(zc, zc, 0.0, None, ALU.min).then_inc(s_z, 1)

                    def tile(q, s, k):
                        n = r * (2 * NT) + q * NT + s
                        if q == 1:
                            nf = r * NT + s
                            eng.tensor_scalar(m, tile_cols(x, s), 0.0, EPS_MSG, ALU.max, ALU.add).then_inc(s_m, 1)
                            eng.wait_ge(s_m, nf + 1)
                            eng.wait_ge(s_e, n + 1)
                            eng.tensor_tensor(e[k], e[k], m, ALU.mult).then_inc(s_f, 1)
                            eng.wait_ge(s_f, nf + 1)
                        eng.wait_ge(s_hi, n + 1)
                        eng.tensor_tensor(rest, MISC, parts[k][:, 0:D], ALU.subtract).then_inc(s_rest, 1)
                        eng.wait_ge(s_rest, n + 1)
                        eng.tensor_copy(parts[k][:, D:2 * D], rest).then_inc(s_mid, 1)
                        eng.wait_ge(s_mid, n + 1)
                        eng.tensor_tensor(parts[k][:, 2 * D:3 * D], rest, parts[k][:, D:2 * D],
                                          ALU.subtract).then_inc(s_parts, 1)
                        eng.wait_ge(s_parts, n + 2)
                        eng.nop(nofuse=True)

                    def weights(i, c0, cw):
                        d, ac = den[:, bass.ds(c0, cw)], acc[:, bass.ds(c0, cw)]
                        ds_ = Steps(eng, s_inv, r * 48 + i * 4, apart=True)
                        ds_(eng.tensor_scalar(d, d, 1e-31, None, ALU.max))
                        ds_(eng.reciprocal(d, d))
                        ds_(eng.scalar_tensor_tensor(d, d, float(np.exp(REACH)), d, ALU.is_le, ALU.mult))
                        ds_(eng.scalar_tensor_tensor(d, ac, 0.0, d, ALU.is_equal, ALU.mult))

                    tiles(eng, lambda s, k, first, last: tile(0, s, k))
                    for i, j in enumerate(DVE_P):
                        _, c0, cw = PIECES[j]
                        eng.wait_ge(s_sum, r * (2 * NP) + j + 2)
                        eng.tensor_copy(den[:, c0:c0 + cw], ps[:, j, 0:cw]).then_inc(s_denv, 1)
                    eng.wait_ge(s_denv, r * len(DVE_P) + len(DVE_P))
                    eng.wait_ge(s_dena, r * len(ACT_P) + len(ACT_P))
                    tiles(eng, lambda s, k, first, last: tile(1, s, k), lambda i: weights(i, i * SL, SL))
                    weights(11, 11 * SL, N - 11 * SL)
                    for j, c0, cw in PIECES:
                        eng.wait_ge(s_sum, r * (2 * NP) + NP + j + 2)
                        d, ac = den[:, c0:c0 + cw], acc[:, c0:c0 + cw]
                        eng.tensor_tensor(d, ps[:, j, 0:cw], d, ALU.mult).then_inc(s_num, 1)
                        eng.wait_ge(s_num, r * NP + j + 2)
                        zs(eng.tensor_tensor(ac, ac, d, ALU.add))
                    zs(eng.tensor_scalar(shift_s, shift_s, -BAND, None, ALU.add))
                    assert zs.n == NP + 3
                for j, c0, cw in PIECES:
                    eng.tensor_tensor(x[:, c0:c0 + cw], x[:, c0:c0 + cw], acc[:, c0:c0 + cw], ALU.add).then_inc(s_h, 1)
                eng.wait_ge(s_w1, l * 32 + 32)
                for k in range(2):
                    for j, c0, cw in PIECES:
                        eng.wait_ge(s_h1o, l * (2 * NP) + k * NP + j + 1)
                        ins = eng.bn_stats(stats[:, 6 * j:6 * j + 6], h1[k][:, c0:c0 + cw])
                    step(ins)
                    eng.nop(nofuse=True)
                    eng.bn_aggr(mv, stats.rearrange("p (j f) -> p j f", f=6)).then_inc(s_var, 1)
                    eng.wait_ge(s_sd, l * 2 + k + 1)
                    sc, sh = scale[:, k:k + 1], shift[:, k:k + 1]
                    step(eng.reciprocal(sc, sd))
                    step(eng.tensor_tensor(sc, sc, vec[:, k:k + 1], ALU.mult))
                    step(eng.tensor_tensor(tmp, mv[:, 0:1], sc, ALU.mult))
                    eng.tensor_tensor(sh, vec[:, 2 + k:3 + k], tmp, ALU.subtract).then_inc(s_aff, 1)
                for j in DVE_P:
                    _, c0, cw = PIECES[j]
                    eng.wait_ge(s_x, l * NP + j + 1)
                    eng.tensor_scalar(x[:, c0:c0 + cw], ps[:, j, 0:cw], 0.0, None, ALU.max).then_inc(s_xv, 1)
                assert step.n == PER, step.n

        @block.scalar
        def _(eng):
            with eng.Fori(0, AL) as l:
                eng.wait_ge(s_band, l + 1)
                eng.nop(nofuse=True)
                count, before = bands(eng, l)
                with eng.Fori(0, count) as b:
                    r = before + b

                    def exponential(q, s, k, first):
                        n = r * (2 * NT) + q * NT + s
                        eng.wait_ge(s_z, r * 4 + (2 if first else 4))
                        eng.wait_ge(s_tr, n + (2 if first else 1))
                        eng.activation(e[k], tile_cols(z, s), ACT.Exp).then_inc(s_e, 1)

                    def high(q, s, k, first):
                        n = r * (2 * NT) + q * NT + s
                        if first:
                            eng.wait_ge(s_sum, (r * 2 + q) * NP + 1)
                        else:
                            eng.wait_ge(s_used, (r * 2 + q) * (NT - 1) + s)
                        eng.wait_ge(s_tr, n + 3)
                        eng.activation(parts[k][:, 0:D], MISC, ACT.Copy).then_inc(s_hi, 1)

                    for q in range(2):
                        exponential(q, 0, 0, True)
                        exponential(q, 1, 1, False)

                        def body(s, k, first, last):
                            high(q, s, k, first)
                            if not last and not (isinstance(s, int) and s >= 23):
                                exponential(q, s + 2, k, False)

                        tiles(eng, body)
                        if q == 0:
                            for j in ACT_P:
                                _, c0, cw = PIECES[j]
                                eng.wait_ge(s_sum, r * (2 * NP) + j + 2)
                                eng.activation(den[:, c0:c0 + cw], ps[:, j, 0:cw], ACT.Copy).then_inc(s_dena, 1)
                for k in range(2):
                    for j, c0, cw in PIECES:
                        eng.wait_ge(s_h1, l * (2 * NP) + k * NP + j + 1)
                        eng.activation(h1[k][:, c0:c0 + cw], ps[:, j, 0:cw], ACT.Copy).then_inc(s_h1o, 1)
                    eng.wait_ge(s_var, l * 2 + k + 1)
                    eng.activation(sd, mv[:, 1:2], ACT.Sqrt, bias=epsc).then_inc(s_sd, 1)
                for j, c0, cw in PIECES:
                    for k in range(2):
                        if j == 0:
                            eng.wait_ge(s_aff, l * 2 + k + 1)
                        eng.activation(h1[k][:, c0:c0 + cw], h1[k][:, c0:c0 + cw], ACT.Relu,
                                       bias=shift[:, k:k + 1], scale=scale[:, k:k + 1]).then_inc(s_r1, 1)
                for j in ACT_P:
                    _, c0, cw = PIECES[j]
                    eng.wait_ge(s_x, l * NP + j + 1)
                    eng.activation(x[:, c0:c0 + cw], ps[:, j, 0:cw], ACT.Relu).then_inc(s_xa, 1)

        @block.tensor
        def _(eng):
            for s, n in ((s_xa, 1), (s_xv, 1), (s_num, 1), (s_tr, 2), (s_used, 1), (s_sum, 1), (s_parts, 1), (s_fin, 1)):
                for _ in range(n):
                    eng.nop(nofuse=True).then_inc(s, 1)
            with eng.Fori(0, AL) as l:
                eng.wait_ge(s_band, l + 1)
                eng.nop(nofuse=True)
                count, before = bands(eng, l)
                eng.wait_ge(s_xa, l * len(ACT_P) + 1)
                eng.wait_ge(s_xv, l * len(DVE_P) + 1)
                eng.nop(nofuse=True)
                with eng.Fori(0, count) as b:
                    r = before + b
                    for q in range(2):
                        def transpose(s, k):
                            n = r * (2 * NT) + q * NT + s
                            eng.wait_ge(s_e, n + 1) if q == 0 else eng.wait_ge(s_f, r * NT + s + 1)
                            eng.wait_ge(s_parts, n + 1)
                            eng.transpose(MISC, e[k], ident[:, :]).then_inc(s_tr, 1)

                        def products(s, k, first, last):
                            n = r * (2 * NT) + q * NT + s
                            eng.wait_ge(s_parts, n + 2)
                            for i in range(3):
                                for j, c0, cw in PIECES:
                                    if first and i == 0:
                                        if q == 0 and j == 0:
                                            eng.wait_ge(s_num, r * NP + 1)
                                        if q == 1 and j in ACT_P:
                                            eng.wait_ge(s_dena, r * len(ACT_P) + ACT_P.index(j) + 1)
                                        if q == 1 and j in DVE_P:
                                            eng.wait_ge(s_denv, r * len(DVE_P) + DVE_P.index(j) + 1)
                                    if isinstance(s, int):
                                        cols = adj[:, s, c0:c0 + cw]
                                    else:
                                        cols = adj[:, bass.ds(s, 1), c0:c0 + cw].rearrange("p o c -> p (o c)")
                                    ins = eng.matmul(ps[:, j, 0:cw], parts[k][:, i * D:(i + 1) * D], cols,
                                                     start=first and i == 0, stop=last and i == 2,
                                                     skip_group_check=True)
                                    if last and i == 2:
                                        ins.then_inc(s_sum, 1)
                            if not last:
                                ins.then_inc(s_used, 1)

                        transpose(0, 0)

                        def both(s, k, first, last):
                            if not last:
                                transpose(s + 1, 1 - k)
                            products(s, k, first, last)

                        tiles(eng, both)
                for k in range(2):
                    for j, c0, cw in PIECES:
                        if k == 0:
                            eng.wait_ge(s_h, l * NP + j + 1)
                            if j == 0:
                                eng.wait_ge(s_w1, l * 32 + 32)
                        else:
                            eng.wait_ge(s_h1o, l * (2 * NP) + j + 1)
                        eng.matmul(ps[:, j, 0:cw], w1[:, k * D:(k + 1) * D], x[:, c0:c0 + cw],
                                   start=True, stop=True).then_inc(s_h1, 1)
                eng.wait_ge(s_w2, l * 16 + 16)
                for j, c0, cw in PIECES:
                    eng.wait_ge(s_r1, l * (2 * NP) + 2 * j + 2)
                    eng.matmul(ps[:, j, 0:cw], w2[:, 0, :], h1[0][:, c0:c0 + cw], start=True, stop=False)
                    eng.matmul(ps[:, j, 0:cw], w2[:, 1, :], h1[1][:, c0:c0 + cw], start=False,
                               stop=True).then_inc(s_x, 1)
                eng.wait_ge(s_xa, (l + 1) * len(ACT_P) + 1)
                eng.wait_ge(s_xv, (l + 1) * len(DVE_P) + 1)
                eng.nop(nofuse=True).then_inc(s_fin, 1)


def interaction(G):
    nc, a, sem, work, small, ranges, ident, ps, T, adj = (
        G[k] for k in ("nc", "a", "sem", "work", "small", "ranges", "ident", "ps", "T", "adj"))
    h_rows, edge_rows = G["h_rows"], G["edge_rows"]
    x, S = T[0], T[2]
    free = Words(G["adj_words"])
    rows_t = free(P, NC * ROW)
    row3 = rows_t.rearrange("p (c f) -> p c f", f=ROW)
    dst_i = free(P, NC, I32)
    groups = [(g, range(4 * g, min(NT, 4 * g + 4))) for g in range((NT + 3) // 4)]
    stage = [free(P, 4 * D) for _ in groups]
    gathered, sp, hot = ([free(P, n) for _ in range(U)] for n in (D, D, P))
    attr_t = [free(FR + 1, P) for _ in range(U)]
    attr, rel = free(P, U * ROW), free(P, U)
    iota, tile_lo, idx = free(P, P), free(P, NT), [free(P, 1, I32) for _ in range(U)]
    b_in, zero = free(P, D), free(1, D)
    s_ = Words(small)
    w_in, w_out, b_out, w_f = s_(D, D), s_(D, D), s_(D, 1), s_(FR + 1, D)
    LOADS = 5
    cuts = [i * (NC // LOADS) for i in range(LOADS + 1)]

    s_load, s_const, s_er, s_dst = sem("weights_loaded"), sem("constants_ready"), sem("edge_rows_loaded"), sem("dst_ready")
    s_rows, s_h, s_hrow = sem("rows_ready"), sem("h_read_out"), sem("h_rows_written")
    s_idx, s_g = sem("index_ready"), [sem("row_gathered") for _ in range(U)]
    s_st, s_rel, s_hot, s_tr, s_at = sem("attributes_staged"), sem("places_ready"), sem("hot_ready"), sem("transposed"), sem("attributes_ready")
    s_pre, s_exp, s_min, s_ln = sem("filter_product"), sem("exp_ready"), sem("exp_bounded"), sem("log_ready")
    s_sp, s_msg, s_agg, s_half = sem("softplus_ready"), sem("message_ready"), sem("edges_summed"), sem("half_ready")
    E_MAX = float(np.exp(40.0))
    half = s_(D, 1)
    s_tile, s_ev = sem("tile_summed"), sem("tile_read_out")
    SUM = ps[:, 7, 0:P]

    def units(eng, body, begin=None, end=None):
        with eng.Fori(0, NT) as w:
            start, count, before = load_range(eng, ranges, R_SRC, w, NC // U)
            if begin:
                begin(w)
            with eng.Fori(0, count) as u:
                body(w, nc.s_assert_within(start + u * U, 0, NC - U), before + u)
            if end:
                end(w)

    with nc.Block() as block:
        @block.sync
        def _(eng):
            for dst, src in ((w_in, a["int_w_in"]), (w_out, a["int_w_out"]), (w_f[0:FR, :], a["int_w_f"]),
                             (w_f[FR:FR + 1, :], a["int_b_f"].rearrange("(o c) -> o c", o=1)),
                             (b_out, a["int_b_out"].rearrange("(c o) -> c o", o=1)),
                             (b_in, a["int_b_in"].rearrange("(o c) -> o c", o=1).to_broadcast([P, D]))):
                eng.dma_start(dst, src).then_inc(s_load, 16)
            er = edge_rows.rearrange("(p c) f -> p (c f)", p=P)
            for c0, c1 in zip(cuts, cuts[1:]):
                eng.dma_start(rows_t[:, c0 * ROW:c1 * ROW], er[:, c0 * ROW:c1 * ROW]).then_inc(s_er, 16)
            h_view = h_rows.rearrange("(s p) c -> p s c", p=P)
            for g, tiles in groups:
                eng.wait_ge(s_h, g + 1)
                eng.dma_start(h_view[:, tiles[0]:tiles[-1] + 1, :],
                              stage[g][:, 0:len(tiles) * D].rearrange("p (s c) -> p s c", c=D)).then_inc(s_hrow, 16)
            eng.wait_ge(s_hrow, 16 * len(groups))

        @block.gpsimd
        def _(eng):
            imprecise = dict(allow_small_or_imprecise_dtypes=True)
            eng.iota(tile_lo, pattern=[[P, NT]], base=0, channel_multiplier=0, **imprecise).then_inc(s_const, 1)
            eng.iota(iota, pattern=[[1, P]], base=0, channel_multiplier=0, **imprecise).then_inc(s_const, 1)
            eng.memset(zero, 0.0).then_inc(s_const, 1)
            eng.wait_ge(s_dst, 1)
            eng.wait_ge(s_hrow, 16 * len(groups))

            def body(w, c, q):
                for k in range(U):
                    eng.wait_ge(s_msg, q * U + k + 1)
                    eng.tensor_copy(idx[k], dst_i[:, bass.ds(c + k, 1)]).then_inc(s_idx, 1)
                    eng.wait_ge(s_idx, q * U + k + 1)
                    eng.nop(nofuse=True)
                    eng.indirect_dma_start(gathered[k], None, h_rows[:, :],
                                           bass.IndirectOffsetOnAxis(ap=idx[k], axis=0)).then_inc(s_g[k], 16)

            units(eng, body)

        @block.vector
        def _(eng):
            eng.memset(half, 0.5).then_inc(s_half, 1)
            eng.wait_ge(s_load, 96)
            for g, tiles in groups:
                n = len(tiles)
                eng.wait_ge(s_rows, g + 1)
                eng.tensor_tensor(stage[g][:, 0:n * D].rearrange("p (s c) -> p s c", c=D),
                                  ps[0:P, g % 4, 0:n * D].rearrange("p (s c) -> p s c", c=D),
                                  b_in.unsqueeze(1).to_broadcast([P, n, D]), ALU.add).then_inc(s_h, 1)
            eng.wait_ge(s_er, 16 * LOADS)
            eng.tensor_copy(dst_i, row3[:, :, DST_C]).then_inc(s_dst, 1)
            eng.wait_ge(s_const, 3)

            def body(w, c, q):
                eng.wait_ge(s_tr, q * U + 1)
                eng.tensor_copy(attr, row3[:, bass.ds(c, U), :].rearrange("p c f -> p (c f)")).then_inc(s_st, 1)
                eng.wait_ge(s_st, q + 1)
                at3 = attr.rearrange("p (c f) -> p c f", f=ROW)
                eng.tensor_scalar(rel, at3[:, :, SRC_C], tile_lo[:, bass.ds(w, 1)], None, ALU.subtract).then_inc(s_rel, 1)
                eng.wait_ge(s_rel, q + 1)
                for k in range(U):
                    eng.wait_ge(s_agg, q * U + k + 1)
                    eng.tensor_scalar(hot[k], iota, rel[:, k:k + 1], at3[:, k, RCUT_C:RCUT_C + 1],
                                      ALU.is_equal, ALU.mult).then_inc(s_hot, 1)

                def bound(k):
                    eng.wait_ge(s_exp, q * U + k + 1)
                    eng.tensor_scalar(sp[k], sp[k], E_MAX, None, ALU.min).then_inc(s_min, 1)

                def message(k):
                    eng.wait_ge(s_ln, q * U + k + 1)
                    eng.scalar_tensor_tensor(sp[k], ps[0:P, k, 0:D], -LOG2, sp[k], ALU.add, ALU.max).then_inc(s_sp, 1)
                    eng.wait_ge(s_sp, q * U + k + 1)
                    eng.wait_ge(s_g[k], q * 16 + 16)
                    eng.tensor_tensor(sp[k], sp[k], gathered[k], ALU.mult).then_inc(s_msg, 1)

                bound(0)
                bound(1)
                message(0)
                bound(2)
                message(1)
                bound(3)
                message(2)
                bound(4)
                message(3)
                message(4)

            units(eng, body)

        @block.scalar
        def _(eng):
            eng.wait_ge(s_half, 1)

            def body(w, c, q):
                def transposed(k):
                    eng.wait_ge(s_tr, (q + 1) * U + k + 1)
                    eng.activation(attr_t[k], ps[0:FR + 1, 5 + k % 2, 0:P], ACT.Copy).then_inc(s_at, 1)

                def exponential(k):
                    eng.wait_ge(s_pre, q * U + k + 1)
                    eng.activation(sp[k], ps[0:P, k, 0:D], ACT.Exp).then_inc(s_exp, 1)

                def log(k):
                    eng.wait_ge(s_min, q * U + k + 1)
                    eng.activation(sp[k], sp[k], ACT.Ln, bias=half[0:P, :], scale=0.5).then_inc(s_ln, 1)

                transposed(0)
                transposed(1)
                transposed(2)
                exponential(0)
                transposed(3)
                exponential(1)
                log(0)
                transposed(4)
                exponential(2)
                log(1)
                exponential(3)
                log(2)
                exponential(4)
                log(3)
                log(4)

            def end(w):
                eng.wait_ge(s_tile, w + 1)
                eng.activation(S[:, bass.ds(w * P, P)], SUM, ACT.Copy).then_inc(s_ev, 1)

            units(eng, body, end=end)

        @block.tensor
        def _(eng):
            eng.wait_ge(s_load, 96)
            for g, tiles in groups:
                if g >= 4:
                    eng.wait_ge(s_h, g - 3)
                for i, s in enumerate(tiles):
                    ins = eng.matmul(ps[0:P, g % 4, i * D:(i + 1) * D], x[:, s * P:(s + 1) * P], w_in,
                                     start=True, stop=True)
                ins.then_inc(s_rows, 1)
            eng.wait_ge(s_h, len(groups))
            eng.wait_ge(s_const, 3)
            for _ in range(U):
                for s in (s_agg, s_tr):
                    eng.nop(nofuse=True).then_inc(s, 1)
            eng.nop(nofuse=True).then_inc(s_ev, 1)

            def begin(w):
                eng.wait_ge(s_ev, w + 1)
                eng.nop(nofuse=True)
                eng.matmul(SUM, zero, zero[:, 0:P], start=True, stop=False, skip_group_check=True)

            def body(w, c, q):
                def transpose(k):
                    if k == 0:
                        eng.wait_ge(s_st, q + 1)
                    if k >= 2:
                        eng.wait_ge(s_at, q * U + k - 1)
                    eng.transpose(ps[0:FR + 1, 5 + k % 2, 0:P], attr[:, k * ROW:k * ROW + FR + 1],
                                  ident[0:P, 0:P]).then_inc(s_tr, 1)

                def product(k):
                    eng.wait_ge(s_at, q * U + k + 1)
                    eng.matmul(ps[0:P, k, 0:D], attr_t[k], w_f, start=True, stop=True).then_inc(s_pre, 1)

                def total(k):
                    eng.wait_ge(s_hot, q * U + k + 1)
                    eng.wait_ge(s_msg, q * U + k + 1 + U)
                    eng.matmul(SUM, sp[k], hot[k], start=False, stop=False, skip_group_check=True).then_inc(s_agg, 1)

                transpose(0)
                transpose(1)
                product(0)
                transpose(2)
                product(1)
                transpose(3)
                product(2)
                total(0)
                transpose(4)
                product(3)
                total(1)
                product(4)
                total(2)
                total(3)
                total(4)

            for _ in range(U):
                eng.nop(nofuse=True).then_inc(s_msg, 1)
            units(eng, body, begin,
                  lambda w: eng.matmul(SUM, zero, zero[:, 0:P], start=False, stop=True,
                                       skip_group_check=True).then_inc(s_tile, 1))

    s_o, s_e, s_m, s_l, s_b = (sem(n) for n in ("output_product", "exp_ready", "exp_bounded", "log_ready", "bias_ready"))
    b_low = s_(D, 1)
    with nc.Block() as block:
        @block.tensor
        def _(eng):
            for j, c0, cw in PIECES:
                eng.matmul(ps[:, j, 0:cw], w_out, S[:, c0:c0 + cw], start=True, stop=True).then_inc(s_o, 1)

        @block.scalar
        def _(eng):
            for j, c0, cw in PIECES:
                eng.wait_ge(s_o, j + 1)
                eng.activation(T[1][:, c0:c0 + cw], ps[:, j, 0:cw], ACT.Exp, bias=b_out).then_inc(s_e, 1)
            for j, c0, cw in PIECES:
                eng.wait_ge(s_m, j + 1)
                eng.activation(T[1][:, c0:c0 + cw], T[1][:, c0:c0 + cw], ACT.Ln, bias=half, scale=0.5).then_inc(s_l, 1)

        @block.vector
        def _(eng):
            eng.tensor_scalar(b_low, b_out, -LOG2, None, ALU.add).then_inc(s_b, 1)
            for j, c0, cw in PIECES:
                eng.wait_ge(s_e, j + 1)
                eng.tensor_scalar(T[1][:, c0:c0 + cw], T[1][:, c0:c0 + cw], E_MAX, None, ALU.min).then_inc(s_m, 1)
            eng.wait_ge(s_b, 1)
            for j, c0, cw in PIECES:
                eng.wait_ge(s_l, j + 1)
                eng.scalar_tensor_tensor(T[1][:, c0:c0 + cw], ps[:, j, 0:cw], b_low, T[1][:, c0:c0 + cw],
                                         ALU.add, ALU.max)


def store(G):
    nc, sem, T, out = G["nc"], G["sem"], G["T"], G["out"]
    s_out = sem("stored")
    with nc.Block() as block:
        @block.sync
        def _(eng):
            eng.dma_start(out[:, :], T[0]).then_inc(s_out, 16)
            eng.wait_ge(s_out, 16)


def layout(inputs):
    i = {k: np.asarray(v) for k, v in inputs.items()}
    cols = lambda v: v.reshape(NC, P).T
    r = dict(x=i["x"].T, dst=i["dst"], src_cols=cols(i["src"]), dst_cols=cols(i["dst"]),
             weight_cols=cols(i["edge_weight"]), edge_attr_20=i["edge_attr_20"], edge_attr_64=i["edge_attr_64"].T,
             gin_w1=i["L0_gnn_W1"].transpose(2, 0, 1).reshape(D, GL * GH),
             gin_w2=i["L0_gnn_W2"].transpose(2, 0, 1).reshape(GH, GL * GH),
             gin_w3=i["L0_gnn_W3"].transpose(2, 0, 1).reshape(GH, GL * D),
             gin_b3=i["L0_gnn_b3"].T, gin_eps=i["L0_gnn_eps"])
    for n in ("b1", "g1", "bt1", "b2", "g2", "bt2"):
        r["gin_" + n] = i["L0_gnn_" + n].T
    w1, u1 = i["L1_gnn_W1"].T, i["L1_gnn_U1"].T
    r.update(mlp_w1a=w1[:D], mlp_w1b=w1[D:2 * D], mlp_w1e=w1[2 * D:], mlp_b1=i["L1_gnn_b1"],
             mlp_w2=i["L1_gnn_W2"].T, mlp_b2=i["L1_gnn_b2"], mlp_u1a=u1[:D], mlp_u1b=u1[D:],
             mlp_c1=i["L1_gnn_c1"], mlp_u2=i["L1_gnn_U2"].T, mlp_c2=i["L1_gnn_c2"])
    gb = np.stack([i["L2_gnn_gamma"].reshape(AL, 2, D), i["L2_gnn_beta"].reshape(AL, 2, D)], axis=1)
    r.update(agg_w1=i["L2_gnn_W1"].transpose(1, 0, 2).reshape(D, AL * AH),
             agg_w2=i["L2_gnn_W2"].reshape(AL * 2, D, D).transpose(1, 0, 2),
             agg_vec=gb.transpose(3, 0, 1, 2).reshape(D, AL * 4), agg_t=i["L2_gnn_t"])
    r.update(int_w_in=i["L3_gnn_W_in"].T, int_b_in=i["L3_gnn_b_in"], int_w_f=i["L3_gnn_W_f"].T,
             int_b_f=i["L3_gnn_b_f"], int_w_out=i["L3_gnn_W_out"].T, int_b_out=i["L3_gnn_b_out"])
    return {k: np.ascontiguousarray(v) for k, v in r.items()}


def kernel(**inputs):
    import concourse.bacc as bacc
    from concourse.bass_utils import run_bass_kernel_spmd as run
    nc = bacc.Bacc("TRN2", target_bir_lowering=False, num_devices=1)
    arrays = layout(inputs)
    aps = {k: nc.dram_tensor(k, v.shape, mybir.dt.from_np(v.dtype), kind="ExternalInput").ap()
           for k, v in arrays.items()}
    out = nc.dram_tensor("out", (D, N), F32, kind="ExternalOutput").ap()
    build(nc, aps, out)
    r = run(nc, [arrays], core_ids=[0])
    return np.ascontiguousarray(r.results[0]["out"].T)
```

```python
import numpy as np
import concourse.bass as bass
import concourse.mybir as mybir
from contextlib import ExitStack

F32, BF16, F16 = mybir.dt.float32, mybir.dt.bfloat16, mybir.dt.float16
I32, I16 = mybir.dt.int32, mybir.dt.int16
ALU = mybir.AluOpType
ACT = mybir.ActivationFunctionType
AX = mybir.AxisListType

N = 3125
E = 53125
D = 128
P = 125
NT = N // P
NC = E // P
CR = 85
CJ = NC // CR
U = 5
UH = 3
US = 2 * UH
STEPS = (NC + US - 1) // US
PW = 450
PIECES = [(j, j * PW, min(PW, N - j * PW)) for j in range((N + PW - 1) // PW)]
NP = len(PIECES)
ACT_P = [0, 2, 4]
DVE_P = [1, 3, 5, 6]
GL, GH = 4, 32
FE, FR = 64, 20
ROW = 24
ONE_C, RCUT_C, DST_C, SRC_C = 20, 21, 22, 23
AL, AH = 3, 256
EPS_MSG = 1e-7
EPS_BN = 1e-5
EPS_LN = 1e-5
BAND = 64.0
REACH = 70.0
LOG2 = float(np.log(2.0))
R_ADJ, R_DST, R_SRC, R_BAND = 0, 3, 6, 9
NR = 10


class Steps:

    def __init__(self, eng, sem, base=0, apart=False):
        self.eng, self.sem, self.base, self.n, self.apart = eng, sem, base, 0, apart

    def __call__(self, ins):
        self.n += 1
        ins.then_inc(self.sem, 1)
        self.eng.wait_ge(self.sem, self.base + self.n)
        if self.apart:
            self.eng.nop(nofuse=True)


class Words:

    def __init__(self, region, at=0, end=None):
        self.region, self.at, self.end = region, at, end or region.shape[1]

    def __call__(self, rows, cols, dt=F32):
        words = cols if dt in (F32, I32) else (cols + 1) // 2
        ap = self.region[:, self.at:self.at + words]
        self.at += words
        assert self.at <= self.end, (self.at, self.end)
        return (ap if dt == F32 else ap.bitcast(dt))[0:rows, 0:cols]


def build(nc, a, out):
    ctx = ExitStack()
    with ctx, nc.allow_non_contiguous_dma(reason="small columns"):
        used, held = {}, []

        def sem(name):
            used[name] = used.get(name, 0) + 1
            held.append(nc.alloc_semaphore(f"{name}_{used[name]}"))
            return held[-1]

        def phase(body, *args, **options):
            body(G, *args, **options)
            nc.clear_and_free_semaphores(held)
            held.clear()
            nc.all_engine_barrier()

        adj_all = ctx.enter_context(nc.sbuf_tensor("adj", [P, NT * N + 1], F16))
        adj = adj_all[:, 0:NT * N].rearrange("p (s n) -> p s n", n=N)
        work = ctx.enter_context(nc.sbuf_tensor("work", [128, 4 * N], F32))
        small = ctx.enter_context(nc.sbuf_tensor("small", [128, 1256], F32))
        ranges = ctx.enter_context(nc.sbuf_tensor("ranges", [1, NR * NT], I32))
        ident = ctx.enter_context(nc.sbuf_tensor("ident", [128, 128], F32))
        ps = ctx.enter_context(nc.psum_tensor("ps", [128, 8, 512], F32))
        T = [work[:, k * N:(k + 1) * N] for k in range(4)]

        p_rows = nc.dram_tensor("p_rows", (N, D), F32, kind="Internal").ap()
        h_rows = nc.dram_tensor("h_rows", (N, D), F32, kind="Internal").ap()
        edge_rows = nc.dram_tensor("edge_rows", (E, ROW), F32, kind="Internal").ap()
        deg_row = nc.dram_tensor("deg_row", (1, N), F32, kind="Internal").ap()
        x_kept = nc.dram_tensor("x_kept", (D, N), F32, kind="Internal").ap()

        G = dict(nc=nc, adj_words=adj_all[:, :].bitcast(F32), a=a, out=out, sem=sem, adj=adj, work=work, small=small, ranges=ranges, ident=ident,
                 ps=ps, T=T, p_rows=p_rows, h_rows=h_rows, edge_rows=edge_rows, deg_row=deg_row, x_kept=x_kept)
        index = Words(work, 6400)
        keep = dict(src_f=index(P, NC + 1), dst_f=index(P, NC + 1), pos_f=index(P, NC), meta=index(P, 3 * NC))
        phase(prepare, keep)
        phase(adjacency, keep)
        phase(gin)
        phase(layernorm, save_degree=True)
        phase(edge_mlp)
        phase(layernorm)
        phase(genconv)
        phase(layernorm)
        phase(interaction)
        phase(layernorm)
        phase(store)


def load_range(eng, ranges, row, w, hi):
    return [eng.value_load(ranges[0:1, bass.ds(w + NT * (row + k), 1)], min_val=lo, max_val=top)
            for k, (lo, top) in enumerate(((0, NC), (1, hi), (0, 1 << 20)))]


def prepare(G, keep):
    nc, a, sem, work, ranges, ident, ps = (G[k] for k in ("nc", "a", "sem", "work", "ranges", "ident", "ps"))
    src_f, dst_f, pos_f, meta = (keep[k] for k in ("src_f", "dst_f", "pos_f", "meta"))
    w_ = Words(work, 0, 6400)
    raw_s, raw_d, raw_r = w_(P, NC, I32), w_(P, NC, I32), w_(P, NC)
    rows_i, rows_f = w_(CR, CJ * P, I32), w_(CR, CJ * P)
    cmm, tile_lo, chunk_id, chunk_rev = w_(CR, 2 * CJ), w_(CR, NT), w_(CR, CJ), w_(CR, CJ)
    hit, hit2, keys, keym = w_(CR, NT * CJ), w_(CR, NT * CJ), w_(CR, 2 * NT), w_(CR, 2 * NT)
    table, tmp, fix, whole = w_(1, NR * NT), w_(1, NT), w_(1, NT), w_(1, NT, I32)
    zeros, bin_id, bins = w_(P, NC), w_(P, NT), w_(P, NT + 1)
    hi, fixb, whole_b = w_(P, NC), w_(P, NC), w_(P, NC, I32)
    incl, val = w_(P, NC), w_(P, NC)
    before, ones = w_(P, P, BF16), w_(P, P, BF16)
    hot = w_(P, NC, BF16)

    s_load, s_const, s_v = sem("indices_loaded"), sem("constants_ready"), sem("vector_step")
    s_keys, s_keym, s_hot, s_rank = sem("keys_ready"), sem("keys_reduced"), sem("bin_hot"), sem("bin_ranked")
    s_p = sem("pool_step")

    with nc.Block() as block:
        @block.sync
        def _(eng):
            eng.dma_start(raw_s, a["src_cols"][:, :]).then_inc(s_load, 16)
            eng.dma_start(raw_d, a["dst_cols"][:, :]).then_inc(s_load, 16)
            eng.dma_start(raw_r, a["weight_cols"][:, :]).then_inc(s_load, 16)
            eng.dma_start(rows_i, a["dst"].rearrange("(r c) -> r c", r=CR)).then_inc(s_load, 16)

        @block.gpsimd
        def _(eng):
            imprecise = dict(allow_small_or_imprecise_dtypes=True)
            step = Steps(eng, s_p)
            eng.iota(tile_lo, pattern=[[P, NT]], base=0, channel_multiplier=0, **imprecise).then_inc(s_const, 1)
            eng.iota(chunk_id, pattern=[[1, CJ]], base=1, channel_multiplier=CJ, **imprecise).then_inc(s_const, 1)
            eng.iota(bin_id, pattern=[[1, NT]], base=0, channel_multiplier=0, **imprecise).then_inc(s_const, 1)
            eng.memset(ident[:, :], 0.0)
            eng.memset(ones, 1.0).then_inc(s_const, 1)
            step(eng.memset(before, 1.0))
            eng.affine_select(out=ident[:, :], in_=ident[:, :], compare_op=ALU.not_equal, fill=1.0, base=0,
                              pattern=[[-1, 128]], channel_multiplier=1).then_inc(s_const, 1)
            eng.affine_select(out=before, in_=before, compare_op=ALU.is_gt, fill=0.0, base=0,
                              pattern=[[1, P]], channel_multiplier=-1).then_inc(s_const, 1)
            eng.wait_ge(s_keys, 1)
            eng.partition_all_reduce(keym, keys, CR, bass.bass_isa.ReduceOp.max).then_inc(s_keym, 1)

        @block.tensor
        def _(eng):
            eng.wait_ge(s_const, 6)
            with eng.Fori(0, NT) as h:
                eng.wait_ge(s_hot, h + 1)
                eng.matmul(ps[0:P, 0, 0:NC], before, hot, start=True, stop=True)
                eng.matmul(ps[0:P, 1, 0:NC], ones, hot, start=True, stop=True).then_inc(s_rank, 1)

        @block.vector
        def _(eng):
            step = Steps(eng, s_v)
            eng.wait_ge(s_load, 64)
            eng.wait_ge(s_const, 6)
            eng.tensor_copy(src_f[:, 0:NC], raw_s)
            eng.tensor_copy(dst_f[:, 0:NC], raw_d)
            eng.memset(src_f[:, NC:NC + 1], -1.0)
            eng.memset(dst_f[:, NC:NC + 1], -1.0)
            eng.memset(zeros, 0.0)
            eng.memset(pos_f, 0.0)
            eng.memset(bins, 0.0)
            m3 = meta.rearrange("p (c f) -> p c f", f=3)
            eng.tensor_copy(m3[:, :, 0], raw_r)
            eng.tensor_copy(m3[:, :, 1], raw_d)
            eng.tensor_copy(m3[:, :, 2], raw_s)
            eng.tensor_scalar(chunk_rev, chunk_id, -1.0, float(NC + 1), ALU.mult, ALU.add)
            step(eng.tensor_copy(rows_f, rows_i))

            r3 = rows_f.rearrange("p (j e) -> p j e", j=CJ)
            eng.tensor_reduce(cmm[:, 0:CJ], r3, axis=AX.X, op=ALU.min)
            step(eng.tensor_reduce(cmm[:, CJ:2 * CJ], r3, axis=AX.X, op=ALU.max))
            h3, g3 = (x.rearrange("p (w j) -> p w j", j=CJ) for x in (hit, hit2))
            lo3 = tile_lo.unsqueeze(2).to_broadcast([CR, NT, CJ])
            mn3, mx3 = (cmm[:, k * CJ:(k + 1) * CJ].unsqueeze(1).to_broadcast([CR, NT, CJ]) for k in (0, 1))
            id3, rv3 = (x.unsqueeze(1).to_broadcast([CR, NT, CJ]) for x in (chunk_id, chunk_rev))
            eng.tensor_tensor(h3, mx3, lo3, ALU.is_ge)
            step(eng.tensor_tensor(g3, mn3, lo3, ALU.subtract))
            step(eng.tensor_scalar(g3, g3, float(P), None, ALU.is_lt))
            step(eng.tensor_tensor(h3, h3, g3, ALU.mult))
            step(eng.tensor_tensor(g3, h3, rv3, ALU.mult))
            step(eng.tensor_reduce(keys[:, 0:NT], g3, axis=AX.X, op=ALU.max))
            step(eng.tensor_tensor(g3, h3, id3, ALU.mult))
            eng.tensor_reduce(keys[:, NT:2 * NT], g3, axis=AX.X, op=ALU.max).then_inc(s_keys, 1)

            step(eng.tensor_scalar(whole_b, src_f[:, 0:NC], 1.0 / P, None, ALU.mult))
            step(eng.tensor_copy(hi, whole_b))
            step(eng.tensor_scalar(fixb, hi, float(P), None, ALU.mult))
            step(eng.tensor_tensor(fixb, fixb, src_f[:, 0:NC], ALU.is_gt))
            step(eng.tensor_tensor(hi, hi, fixb, ALU.subtract))
            step(eng.tensor_scalar(fixb, hi, float(P), float(P), ALU.mult, ALU.add))
            step(eng.tensor_tensor(fixb, fixb, src_f[:, 0:NC], ALU.is_le))
            step(eng.tensor_tensor(hi, hi, fixb, ALU.add))

            at = step.n
            with eng.Fori(0, NT) as h:
                inner = Steps(eng, s_v, h * 6 + at)
                eng.tensor_scalar(hot, hi, bin_id[:, bass.ds(h, 1)], None, ALU.is_equal).then_inc(s_hot, 1)
                eng.wait_ge(s_rank, h + 1)
                rank, total = ps[0:P, 0, 0:NC], ps[0:P, 1, 0:NC]
                inner(eng.tensor_tensor_scan(incl, total, zeros, bins[:, bass.ds(h, 1)], ALU.add, ALU.add))
                inner(eng.tensor_tensor(val, incl, total, ALU.subtract))
                inner(eng.tensor_copy(bins[:, bass.ds(h + 1, 1)], incl[:, NC - 1:NC]))
                inner(eng.tensor_tensor(val, val, rank, ALU.add))
                inner(eng.tensor_tensor(val, val, hot, ALU.mult))
                inner(eng.tensor_tensor(pos_f, pos_f, val, ALU.add))
                assert inner.n == 6
            step.n = at + 6 * NT
            step(eng.tensor_scalar(whole_b, pos_f, 1.0 / P, None, ALU.mult))
            step(eng.tensor_copy(hi, whole_b))
            step(eng.tensor_scalar(fixb, hi, float(P), None, ALU.mult))
            step(eng.tensor_tensor(fixb, fixb, pos_f, ALU.is_gt))
            step(eng.tensor_tensor(hi, hi, fixb, ALU.subtract))
            step(eng.tensor_scalar(fixb, hi, float(P), float(P), ALU.mult, ALU.add))
            step(eng.tensor_tensor(fixb, fixb, pos_f, ALU.is_le))
            step(eng.tensor_tensor(hi, hi, fixb, ALU.add))
            step(eng.tensor_scalar(fixb, hi, -float(P), None, ALU.mult))
            step(eng.tensor_tensor(fixb, pos_f, fixb, ALU.add))
            step(eng.tensor_scalar(fixb, fixb, float(NC), None, ALU.mult))
            step(eng.tensor_tensor(pos_f, fixb, hi, ALU.add))

            def row(k):
                return table[:, k * NT:(k + 1) * NT]

            def ceil_div(out, x, size):
                step(eng.tensor_scalar(whole, x, 1.0 / size, None, ALU.mult))
                step(eng.tensor_copy(out, whole))
                step(eng.tensor_scalar(fix, out, float(size), None, ALU.mult))
                step(eng.tensor_tensor(fix, fix, x, ALU.is_lt))
                step(eng.tensor_tensor(out, out, fix, ALU.add))
                step(eng.tensor_scalar(fix, out, float(size), float(-size), ALU.mult, ALU.add))
                step(eng.tensor_tensor(fix, fix, x, ALU.is_ge))
                step(eng.tensor_tensor(out, out, fix, ALU.subtract))

            def steps_before(k):
                step(eng.tensor_tensor_scan(row(k + 2), row(k + 1), zeros[0:1, 0:NT], 0.0, ALU.add, ALU.add))
                step(eng.tensor_tensor(row(k + 2), row(k + 2), row(k + 1), ALU.subtract))

            def steps_of(k, start, size, least):
                ceil_div(row(k + 1), tmp, size)
                step(eng.tensor_scalar(row(k + 1), row(k + 1), float(least), None, ALU.max))
                step(eng.tensor_scalar(row(k), row(k + 1), -float(size), float(-(-NC // size) * size), ALU.mult, ALU.add))
                step(eng.tensor_tensor(row(k), row(k), start, ALU.min))
                steps_before(k)

            eng.wait_ge(s_keym, 1)
            start = row(R_ADJ)
            step(eng.tensor_scalar(start, keym[0:1, 0:NT], -1.0, float(NC), ALU.mult, ALU.add))
            step(eng.tensor_scalar(start, start, float(NC - 3), None, ALU.min))
            step(eng.tensor_scalar(tmp, start, 3.0, None, ALU.add))
            step(eng.tensor_tensor(tmp, keym[0:1, NT:2 * NT], tmp, ALU.max))
            step(eng.tensor_tensor(tmp, tmp, start, ALU.subtract))
            ceil_div(row(R_ADJ + 1), tmp, 2)
            steps_before(R_ADJ)
            steps_of(R_DST, start, U, 1)
            step(eng.tensor_scalar(tmp, bins[0:1, 0:NT], float(1 - P), None, ALU.add))
            ceil_div(row(R_BAND), tmp, P)
            ceil_div(tmp, bins[0:1, 1:NT + 1], P)
            step(eng.tensor_tensor(tmp, tmp, row(R_BAND), ALU.subtract))
            steps_of(R_SRC, row(R_BAND), US, 2)
            eng.tensor_copy(ranges[:, :], table)


def adjacency(G, keep):
    nc, a, sem, work, ranges, ident, ps, adj = (G[k] for k in
                                                ("nc", "a", "sem", "work", "ranges", "ident", "ps", "adj"))
    small, edge_rows = G["small"], G["edge_rows"]
    src_f, dst_f, pos_f, meta = (keep[k] for k in ("src_f", "dst_f", "pos_f", "meta"))
    w_ = Words(work, 0, 6400)
    iota16 = w_(P, N, I16)
    src_hot, dst_hot = [w_(P, N, BF16) for _ in range(2)], [w_(P, P, BF16) for _ in range(2)]
    counts, zero16, ident16 = w_(P, N, F16), small[:, 0:63].bitcast(BF16)[0:P, 0:P], small[:, 64:127].bitcast(F16)[0:P, 0:P]
    s_ = Words(small, 128)
    pay = [s_(P, ROW) for _ in range(U)]
    idx = [s_(P, 1, I32) for _ in range(U)]

    s_iota, s_const = sem("iota_ready"), sem("constants_ready")
    s_hot, s_free = [sem("hots_ready") for _ in range(2)], [sem("hots_free") for _ in range(2)]
    s_tile, s_even, s_odd = sem("tile_counted"), sem("even_pieces_copied"), sem("odd_pieces_copied")
    s_tr, s_trs, s_trv = sem("blocks_transposed"), sem("blocks_stored_scalar"), sem("blocks_stored_vector")
    s_attr, s_pay = [sem("attributes_in_row") for _ in range(U)], [sem("row_and_place_ready") for _ in range(U)]
    s_sc = [sem("row_scattered") for _ in range(U)]
    edges = [0, 7, 13, 19, NT]
    groups = [range(edges[g], edges[g + 1]) for g in range(4)]
    banks = [ps[:, 7, :].bitcast(F16), ps[:, 6, :].bitcast(F16)]

    def block_store(w, g):
        n = len(groups[g])
        return (adj[:, groups[g][0]:groups[g][-1] + 1, bass.ds(w * P, P)],
                banks[g % 2][0:P, 0:128 * n].rearrange("p (b q) -> p b q", q=128)[:, :, 0:P])

    with nc.Block() as block:
        @block.sync
        def _(eng):
            def fill(q, first):
                for k in range(U):
                    if not first:
                        eng.wait_ge(s_sc[k], q * 16)
                    eng.dma_start(pay[k][:, 0:FR], a["edge_attr_20"][bass.ds((q * U + k) * P, P), :]).then_inc(s_attr[k], 16)

            fill(0, True)
            with eng.Fori(1, NC // U) as q:
                fill(q, False)
            for k in range(U):
                eng.wait_ge(s_sc[k], 16 * (NC // U))

        @block.gpsimd
        def _(eng):
            eng.iota(iota16, pattern=[[1, N]], base=0, channel_multiplier=0,
                     allow_small_or_imprecise_dtypes=True).then_inc(s_iota, 1)
            with eng.Fori(0, NC // U) as q:
                for k in range(U):
                    eng.wait_ge(s_pay[k], q + 1)
                    eng.wait_ge(s_attr[k], q * 16 + 16)
                    eng.nop(nofuse=True)
                    eng.indirect_dma_start(edge_rows[:, :], bass.IndirectOffsetOnAxis(ap=idx[k], axis=0),
                                           pay[k], None).then_inc(s_sc[k], 16)

        @block.scalar
        def _(eng):
            def place(q, k, first):
                if not first:
                    eng.wait_ge(s_sc[k], q * 16)
                eng.activation(pay[k][:, RCUT_C:ROW], meta[:, bass.ds((q * U + k) * 3, 3)], ACT.Copy)
                if first:
                    eng.activation(pay[k][:, ONE_C:ONE_C + 1], meta[:, 0:1], ACT.Copy, scale=0.0, bias=1.0)
                eng.activation(idx[k], pos_f[:, bass.ds(q * U + k, 1)], ACT.Copy).then_inc(s_pay[k], 1)

            for k in range(U):
                place(0, k, True)

            def tile(w, rows):
                for q in rows:
                    for k in range(U):
                        place(q, k, False)
                eng.wait_ge(s_tile, w + 1)
                for j in ACT_P:
                    _, c0, cw = PIECES[j]
                    ins = eng.activation(counts[:, c0:c0 + cw], ps[0:P, j, 0:cw], ACT.Copy)
                ins.then_inc(s_even, 1)
                for i, g in enumerate((0, 2)):
                    eng.wait_ge(s_tr, w * 4 + g + 1)
                    eng.activation(*block_store(w, g), ACT.Copy).then_inc(s_trs, 1)

            with eng.Fori(0, 21) as w:
                tile(w, [w * 4 + 1 + i for i in range(4)])
            with eng.Fori(21, NT) as w:
                tile(w, [])

        @block.vector
        def _(eng):
            eng.memset(zero16, 0.0).then_inc(s_const, 1)
            eng.tensor_copy(ident16, ident[0:P, 0:P]).then_inc(s_const, 1)
            eng.wait_ge(s_iota, 1)
            with eng.Fori(0, NT) as w:
                start, count, before = load_range(eng, ranges, R_ADJ, w, (NC + 2) // 2)
                with eng.Fori(0, count) as i:
                    c, t = nc.s_assert_within(start + i * 2, 0, NC - 1), before + i
                    for k in range(2):
                        eng.wait_ge(s_free[k], t + 1)
                        eng.tensor_scalar(dst_hot[k], iota16[:, bass.ds(w * P, P)], dst_f[:, bass.ds(c + k, 1)],
                                          None, ALU.is_equal)
                        eng.tensor_scalar(src_hot[k], iota16, src_f[:, bass.ds(c + k, 1)], None,
                                          ALU.is_equal).then_inc(s_hot[k], 1)
                eng.wait_ge(s_tile, w + 1)
                for j in DVE_P:
                    _, c0, cw = PIECES[j]
                    ins = eng.tensor_copy(counts[:, c0:c0 + cw], ps[0:P, j, 0:cw])
                ins.then_inc(s_odd, 1)
                for i, g in enumerate((1, 3)):
                    eng.wait_ge(s_tr, w * 4 + g + 1)
                    eng.tensor_copy(*block_store(w, g)).then_inc(s_trv, 1)

        @block.tensor
        def _(eng):
            eng.wait_ge(s_const, 2)
            eng.nop(nofuse=True).then_inc(s_free[0], 1)
            eng.nop(nofuse=True).then_inc(s_free[1], 1)

            def pair(t, start):
                for k in range(2):
                    eng.wait_ge(s_hot[k], t + 1)
                    for j, c0, cw in PIECES:
                        ins = eng.matmul(ps[0:P, j, 0:cw], dst_hot[k], src_hot[k][:, c0:c0 + cw],
                                         start=start and k == 0, stop=False, skip_group_check=True)
                    ins.then_inc(s_free[k], 1)

            with eng.Fori(0, NT) as w:
                _, count, before = load_range(eng, ranges, R_ADJ, w, (NC + 2) // 2)
                pair(before, True)
                with eng.Fori(1, count) as i:
                    pair(before + i, False)
                eng.matmul(ps[0:P, NP - 1, 0:1], zero16, zero16[:, 0:1], start=False, stop=True,
                           skip_group_check=True).then_inc(s_tile, 1)
                eng.wait_ge(s_even, w + 1)
                eng.wait_ge(s_odd, w + 1)
                for g, blocks in enumerate(groups):
                    if g == 2:
                        eng.wait_ge(s_trs, w * 2 + 1)
                    if g == 3:
                        eng.wait_ge(s_trv, w * 2 + 1)
                    for b, s in enumerate(blocks):
                        ins = eng.transpose(banks[g % 2][0:P, b * 128:b * 128 + P], counts[:, s * P:s * P + P],
                                            ident16)
                    ins.then_inc(s_tr, 1)
                eng.wait_ge(s_trs, w * 2 + 2)
                eng.wait_ge(s_trv, w * 2 + 2)


def gin(G):
    nc, a, sem, small, ident, ps, adj, T, deg_row = (
        G[k] for k in ("nc", "a", "sem", "small", "ident", "ps", "adj", "T", "deg_row"))
    s_ = Words(small)
    w1, w2, w3 = s_(D, GL * GH), s_(GH, GL * GH), s_(GH, GL * D)
    vec = s_(GH, 6 * GL)
    b3, eps = s_(D, GL), s_(D, GL)
    w1l, w1e, w2l, w3l = s_(D, GH), s_(D, GH), s_(GH, GH), s_(GH, D)
    vl, b3l = s_(GH, 6), s_(D, 1)
    merge = s_(3 * GH + 1, GH)
    stats, mv, sd, scale, shift, tmp = s_(GH, 6 * NP), s_(GH, 2), s_(GH, 1), s_(GH, 1), s_(GH, 1), s_(GH, 1)
    epsc = s_(GH, 1)
    YW = 3 * GH + 2
    y_hbm = Words(T[3])
    parts = y_hbm(P, NT * YW, BF16).rearrange("p (s c) -> p s c", c=YW)
    rest = y_hbm(P, NT * GH).rearrange("p (s c) -> p s c", c=GH)
    X, S, zb, h = T[1], T[2], T[3][0:GH, :], T[2][0:GH, :]
    halves = [(0, 0, 16), (1, 16, NT)]

    s_load, s_merge, s_v, s_a = sem("weights_loaded"), sem("merge_ready"), sem("vector_step"), sem("scalar_step")
    s_wl, s_xa, s_xv = sem("layer_weights_ready"), sem("x_by_scalar"), sem("x_by_vector")
    s_y, s_hi, s_parts = sem("y_ready"), sem("y_high_ready"), sem("y_parts_ready")
    s_sum, s_sa, s_sv = sem("piece_summed"), sem("sum_by_scalar"), sem("sum_by_vector")
    s_z = [sem("z1_ready"), sem("z2_ready")]
    s_zb, s_var, s_sd, s_aff, s_h = ([sem(f"{n}{i}") for i in (1, 2)] for n in
                                     ("biased", "variance", "deviation", "affine", "hidden"))
    s_x = sem("x_product_ready")

    with nc.Block() as block:
        @block.sync
        def _(eng):
            for dst, src in ((T[0], a["x"]), (w1, a["gin_w1"]), (w2, a["gin_w2"]), (w3, a["gin_w3"]),
                             (b3, a["gin_b3"]),
                             (eps, a["gin_eps"].rearrange("(o l) -> o l", o=1).to_broadcast([D, GL]))):
                eng.dma_start(dst, src).then_inc(s_load, 16)
            for i, name in enumerate(("b1", "g1", "bt1", "b2", "g2", "bt2")):
                eng.dma_start(vec[:, i * GL:(i + 1) * GL], a["gin_" + name]).then_inc(s_load, 16)

        @block.vector
        def _(eng):
            once = Steps(eng, s_v)
            eng.memset(epsc, EPS_BN)
            once(eng.memset(merge, 0.0))
            for i in range(3):
                ins = eng.tensor_copy(merge[i * GH:(i + 1) * GH, :], ident[i * GH:(i + 1) * GH, i * GH:(i + 1) * GH])
            ins.then_inc(s_merge, 1)
            eng.wait_ge(s_load, 192)
            once(eng.tensor_scalar(eps, eps, 1.0, None, ALU.add))
            for j in DVE_P:
                _, c0, cw = PIECES[j]
                eng.tensor_copy(X[:, c0:c0 + cw], T[0][:, c0:c0 + cw]).then_inc(s_xv, 1)
            first = once.n
            PER = 12
            with eng.Fori(0, GL) as l:
                step = Steps(eng, s_v, l * PER + first)
                eng.wait_ge(s_xa, (l + 1) * len(ACT_P))
                eng.wait_ge(s_xv, (l + 1) * len(DVE_P))
                eng.tensor_copy(w1l, w1[:, bass.ds(l * GH, GH)])
                eng.tensor_scalar(w1e, w1[:, bass.ds(l * GH, GH)], eps[:, bass.ds(l, 1)], None, ALU.mult)
                eng.tensor_copy(w2l, w2[:, bass.ds(l * GH, GH)])
                eng.tensor_copy(w3l, w3[:, bass.ds(l * D, D)])
                eng.tensor_copy(vl, vec.rearrange("p (i l) -> p i l", l=GL)[:, :, bass.ds(l, 1)].rearrange("p i o -> p (i o)"))
                eng.tensor_copy(b3l, b3[:, bass.ds(l, 1)])
                eng.memset(parts[:, :, 3 * GH:YW], 1.0).then_inc(s_wl, 1)
                for b, s0, s1 in halves:
                    y = ps[0:P, b, 0:(s1 - s0) * GH].rearrange("p (s c) -> p s c", c=GH)
                    eng.wait_ge(s_hi, l * 2 + b + 1)
                    step(eng.tensor_tensor(rest[:, s0:s1, :], y, parts[:, s0:s1, 0:GH], ALU.subtract))
                    step(eng.tensor_copy(parts[:, s0:s1, GH:2 * GH], rest[:, s0:s1, :]))
                    eng.tensor_tensor(parts[:, s0:s1, 2 * GH:3 * GH], rest[:, s0:s1, :],
                                      parts[:, s0:s1, GH:2 * GH], ALU.subtract).then_inc(s_parts, 1)
                for i, j in enumerate(DVE_P):
                    _, c0, cw = PIECES[j]
                    eng.wait_ge(s_sum, l * NP + j + 1)
                    eng.tensor_copy(S[0:YW - 1, c0:c0 + cw], ps[0:YW - 1, j, 0:cw]).then_inc(s_sv, 1)
                for n in range(2):
                    for j, c0, cw in PIECES:
                        eng.wait_ge(s_zb[n], l * NP + j + 1)
                        ins = eng.bn_stats(stats[:, 6 * j:6 * j + 6], zb[:, c0:c0 + cw])
                    step(ins)
                    eng.nop(nofuse=True)
                    eng.bn_aggr(mv, stats.rearrange("p (j f) -> p j f", f=6)).then_inc(s_var[n], 1)
                    eng.wait_ge(s_sd[n], l + 1)
                    step(eng.reciprocal(scale, sd))
                    step(eng.tensor_tensor(scale, scale, vl[:, 3 * n + 1:3 * n + 2], ALU.mult))
                    step(eng.tensor_tensor(tmp, mv[:, 0:1], scale, ALU.mult))
                    eng.tensor_tensor(shift, vl[:, 3 * n + 2:3 * n + 3], tmp, ALU.subtract).then_inc(s_aff[n], 1)
                for j in DVE_P:
                    _, c0, cw = PIECES[j]
                    eng.wait_ge(s_x, l * NP + j + 1)
                    eng.tensor_scalar(X[:, c0:c0 + cw], ps[:, j, 0:cw], b3l, None, ALU.add).then_inc(s_xv, 1)
                assert step.n == PER, step.n

        @block.scalar
        def _(eng):
            eng.wait_ge(s_load, 192)
            for j in ACT_P:
                _, c0, cw = PIECES[j]
                eng.activation(X[:, c0:c0 + cw], T[0][:, c0:c0 + cw], ACT.Copy).then_inc(s_xa, 1)
            with eng.Fori(0, GL) as l:
                for b, s0, s1 in halves:
                    eng.wait_ge(s_y, l * 2 + b + 1)
                    eng.activation(parts[:, s0:s1, 0:GH],
                                   ps[0:P, b, 0:(s1 - s0) * GH].rearrange("p (s c) -> p s c", c=GH),
                                   ACT.Copy).then_inc(s_hi, 1)
                for j in ACT_P:
                    _, c0, cw = PIECES[j]
                    eng.wait_ge(s_sum, l * NP + j + 1)
                    eng.activation(S[0:YW - 1, c0:c0 + cw], ps[0:YW - 1, j, 0:cw], ACT.Copy).then_inc(s_sa, 1)
                for n in range(2):
                    for j, c0, cw in PIECES:
                        eng.wait_ge(s_z[n], l * NP + j + 1)
                        eng.activation(zb[:, c0:c0 + cw], ps[0:GH, j, 0:cw], ACT.Identity,
                                       bias=vl[:, 3 * n:3 * n + 1]).then_inc(s_zb[n], 1)
                    eng.wait_ge(s_var[n], l + 1)
                    eng.activation(sd, mv[:, 1:2], ACT.Sqrt, bias=epsc).then_inc(s_sd[n], 1)
                    eng.wait_ge(s_aff[n], l + 1)
                    for j, c0, cw in PIECES:
                        eng.activation(h[:, c0:c0 + cw], zb[:, c0:c0 + cw], ACT.Relu, bias=shift,
                                       scale=scale).then_inc(s_h[n], 1)
                for j in ACT_P:
                    _, c0, cw = PIECES[j]
                    eng.wait_ge(s_x, l * NP + j + 1)
                    eng.activation(X[:, c0:c0 + cw], ps[:, j, 0:cw], ACT.Identity, bias=b3l).then_inc(s_xa, 1)

        @block.tensor
        def _(eng):
            eng.wait_ge(s_merge, 1)
            with eng.Fori(0, GL) as l:
                eng.wait_ge(s_wl, l + 1)
                eng.wait_ge(s_xa, (l + 1) * len(ACT_P))
                eng.wait_ge(s_xv, (l + 1) * len(DVE_P))
                for b, s0, s1 in halves:
                    for s in range(s0, s1):
                        ins = eng.matmul(ps[0:P, b, (s - s0) * GH:(s - s0 + 1) * GH], X[:, s * P:(s + 1) * P], w1l,
                                         start=True, stop=True)
                    ins.then_inc(s_y, 1)
                eng.wait_ge(s_parts, l * 2 + 2)

                def tile(s, start, last):
                    for j, c0, cw in PIECES:
                        if isinstance(s, int):
                            w, m = parts[:, s, 0:YW - 1], adj[:, s, c0:c0 + cw]
                        else:
                            w = parts[:, bass.ds(s, 1), 0:YW - 1].rearrange("p o c -> p (o c)")
                            m = adj[:, bass.ds(s, 1), c0:c0 + cw].rearrange("p o c -> p (o c)")
                        ins = eng.matmul(ps[0:YW - 1, j, 0:cw], w, m, start=start, stop=last, skip_group_check=True)
                        if last:
                            ins.then_inc(s_sum, 1)

                tile(0, True, False)
                with eng.Fori(1, NT - 1) as s:
                    tile(s, False, False)
                tile(NT - 1, False, True)
                for j, c0, cw in PIECES:
                    if j in ACT_P:
                        eng.wait_ge(s_sa, l * len(ACT_P) + ACT_P.index(j) + 1)
                    else:
                        eng.wait_ge(s_sv, l * len(DVE_P) + DVE_P.index(j) + 1)
                    eng.matmul(ps[0:GH, j, 0:cw], merge, S[0:YW - 1, c0:c0 + cw], start=True, stop=False)
                    eng.matmul(ps[0:GH, j, 0:cw], w1e, X[:, c0:c0 + cw], start=False, stop=True).then_inc(s_z[0], 1)
                for j, c0, cw in PIECES:
                    eng.wait_ge(s_h[0], l * NP + j + 1)
                    eng.nop(nofuse=True)
                    eng.matmul(ps[0:GH, j, 0:cw], w2l, h[:, c0:c0 + cw], start=True, stop=True).then_inc(s_z[1], 1)
                for j, c0, cw in PIECES:
                    eng.wait_ge(s_h[1], l * NP + j + 1)
                    eng.matmul(ps[:, j, 0:cw], w3l, h[:, c0:c0 + cw], start=True, stop=True).then_inc(s_x, 1)


def layernorm(G, save_degree=False):
    nc, sem, small, ps, T, deg_row = (G[k] for k in ("nc", "sem", "small", "ps", "T", "deg_row"))
    s_ = Words(small)
    ones, epsc = s_(D, D), s_(D, 1)
    z, d, sq = T[1], T[2], T[3]
    s_const, s_z, s_mean, s_d, s_sq = (sem(n) for n in ("constants_ready", "residual_added", "mean_ready",
                                                        "centred", "squared"))
    s_var, s_sd, s_inv, s_deg = (sem(n) for n in ("variance_ready", "deviation_ready", "inverted", "degree_saved"))
    with nc.Block() as block:
        @block.sync
        def _(eng):
            if save_degree:
                eng.dma_start(deg_row[:, :], T[2][3 * GH:3 * GH + 1, :]).then_inc(s_deg, 16)
                eng.wait_ge(s_deg, 16)

        @block.vector
        def _(eng):
            eng.memset(epsc, EPS_LN)
            eng.memset(ones, 1.0 / D).then_inc(s_const, 1)
            for j, c0, cw in PIECES:
                eng.tensor_tensor(z[:, c0:c0 + cw], T[0][:, c0:c0 + cw], z[:, c0:c0 + cw], ALU.add).then_inc(s_z, 1)
            if save_degree:
                eng.wait_ge(s_deg, 16)
            for j, c0, cw in PIECES:
                eng.wait_ge(s_mean, j + 1)
                eng.tensor_tensor(d[:, c0:c0 + cw], z[:, c0:c0 + cw], ps[:, j, 0:cw], ALU.subtract).then_inc(s_d, 1)
            for j, c0, cw in PIECES:
                eng.wait_ge(s_sd, j + 1)
                eng.reciprocal(sq[:, c0:c0 + cw], sq[:, c0:c0 + cw]).then_inc(s_inv, 1)
                eng.wait_ge(s_inv, j + 1)
                eng.tensor_tensor(T[0][:, c0:c0 + cw], d[:, c0:c0 + cw], sq[:, c0:c0 + cw], ALU.mult)

        @block.tensor
        def _(eng):
            eng.wait_ge(s_const, 1)
            for j, c0, cw in PIECES:
                eng.wait_ge(s_z, j + 1)
                eng.matmul(ps[:, j, 0:cw], ones, z[:, c0:c0 + cw], start=True, stop=True).then_inc(s_mean, 1)
            for j, c0, cw in PIECES:
                eng.wait_ge(s_sq, j + 1)
                eng.matmul(ps[:, j, 0:cw], ones, sq[:, c0:c0 + cw], start=True, stop=True).then_inc(s_var, 1)

        @block.scalar
        def _(eng):
            for j, c0, cw in PIECES:
                eng.wait_ge(s_d, j + 1)
                eng.activation(sq[:, c0:c0 + cw], d[:, c0:c0 + cw], ACT.Square).then_inc(s_sq, 1)
            eng.wait_ge(s_const, 1)
            for j, c0, cw in PIECES:
                eng.wait_ge(s_var, j + 1)
                eng.activation(sq[:, c0:c0 + cw], ps[:, j, 0:cw], ACT.Sqrt, bias=epsc).then_inc(s_sd, 1)


def edge_mlp(G):
    nc, a, sem, work, small, ranges, ident, ps, T, p_rows, deg_row = (
        G[k] for k in ("nc", "a", "sem", "work", "small", "ranges", "ident", "ps", "T", "p_rows", "deg_row"))
    x, R = T[0], T[2]
    q_rows = work[0:P, 4 * N - NT * D:4 * N].rearrange("p (s c) -> p s c", c=D)
    r_ = Words(work, N, 2 * N)
    src_i, dst_f = r_(P, NC, I32), r_(P, NC)
    row_ring = r_(P, U * D)
    rows = [row_ring[:, k * D:(k + 1) * D] for k in range(U)]
    stage = [T[2][0:P, g * 512:(g + 1) * 512] for g in range(5)] + [row_ring[:, 0:512], row_ring[:, 512:640]]
    wa, wb = r_(D, D), r_(D, D)
    hots = r_(P, U * P)
    hot = [hots[:, k * P:(k + 1) * P] for k in range(U)]
    dst_i = hots[:, 0:NC].bitcast(I32)
    tile_lo, iota, b1 = r_(P, NT), r_(P, P), r_(P, D)
    idx = [r_(P, 1, I32) for _ in range(U)]
    s_ = Words(small)
    attr = [s_(FE, P) for _ in range(U)]
    w1e, zero = s_(FE, D), s_(1, D)
    hot_t = [s_(P, P) for _ in range(3)] + [r_(P, P) for _ in range(U - 3)]
    groups = [(g, range(4 * g, min(NT, 4 * g + 4))) for g in range((NT + 3) // 4)]

    s_load, s_const, s_v = sem("weights_loaded"), sem("constants_ready"), sem("vector_step")
    s_rows, s_p, s_q, s_prow = sem("rows_ready"), sem("p_read_out"), sem("q_read_out"), sem("p_rows_written")
    s_idx, s_g, s_attr = sem("index_ready"), [sem("row_gathered") for _ in range(U)], [sem("attributes") for _ in range(U)]
    s_hot, s_tr, s_ht = sem("hot_ready"), sem("hot_transposed"), sem("hot_t_ready")
    s_pre, s_sum, s_relu, s_agg = sem("products_ready"), sem("preactivation"), sem("relu_ready"), sem("edges_summed")
    s_tile, s_ev = sem("tile_summed"), sem("tile_read_out")
    SUM = ps[:, 7, 0:P]

    def units(eng, body, begin=None, end=None):
        with eng.Fori(0, NT) as w:
            start, count, before = load_range(eng, ranges, R_DST, w, NC // U)
            if begin:
                begin(w)
            with eng.Fori(0, count) as u:
                body(w, nc.s_assert_within(start + u * U, 0, NC - U), before + u)
            if end:
                end(w)

    with nc.Block() as block:
        @block.sync
        def _(eng):
            for dst, src in ((src_i, a["src_cols"]), (dst_i, a["dst_cols"]), (wa, a["mlp_w1a"]),
                             (wb, a["mlp_w1b"]), (w1e, a["mlp_w1e"]),
                             (b1, a["mlp_b1"].rearrange("(o c) -> o c", o=1).to_broadcast([P, D]))):
                eng.dma_start(dst, src).then_inc(s_load, 16)
            p_view = p_rows.rearrange("(s p) c -> p s c", p=P)
            for g, tiles in groups:
                eng.wait_ge(s_p, g + 1)
                eng.dma_start(p_view[:, tiles[0]:tiles[-1] + 1, :],
                              stage[g].rearrange("p (s c) -> p s c", c=D)).then_inc(s_prow, 16)

            def body(w, c, q):
                for k in range(U):
                    eng.wait_ge(s_pre, q * U + k + 1)
                    eng.dma_start(attr[k], a["edge_attr_64"][:, bass.ds((c + k) * P, P)]).then_inc(s_attr[k], 16)

            units(eng, body)

        @block.gpsimd
        def _(eng):
            imprecise = dict(allow_small_or_imprecise_dtypes=True)
            eng.iota(tile_lo, pattern=[[P, NT]], base=0, channel_multiplier=0, **imprecise).then_inc(s_const, 1)
            eng.iota(iota, pattern=[[1, P]], base=0, channel_multiplier=0, **imprecise).then_inc(s_const, 1)
            eng.memset(zero, 0.0).then_inc(s_const, 1)
            eng.wait_ge(s_load, 96)
            eng.wait_ge(s_prow, 16 * len(groups))

            def body(w, c, q):
                for k in range(U):
                    eng.wait_ge(s_agg, q * U + k + 1)
                    eng.tensor_copy(idx[k], src_i[:, bass.ds(c + k, 1)]).then_inc(s_idx, 1)
                    eng.wait_ge(s_idx, q * U + k + 1)
                    eng.nop(nofuse=True)
                    eng.indirect_dma_start(rows[k], None, p_rows[:, :],
                                           bass.IndirectOffsetOnAxis(ap=idx[k], axis=0)).then_inc(s_g[k], 16)

            units(eng, body)

        @block.vector
        def _(eng):
            eng.wait_ge(s_load, 96)
            eng.tensor_copy(dst_f, dst_i).then_inc(s_v, 1)
            for g, tiles in groups:
                n = len(tiles)
                eng.wait_ge(s_rows, g + 1)
                eng.tensor_tensor(q_rows[:, tiles[0]:tiles[-1] + 1, :],
                                  ps[0:P, 4 + g % 4, 0:n * D].rearrange("p (s c) -> p s c", c=D),
                                  b1.unsqueeze(1).to_broadcast([P, n, D]), ALU.add).then_inc(s_q, 1)
            eng.wait_ge(s_v, 1)
            eng.wait_ge(s_const, 3)

            def body(w, c, q):
                for k in range(U):
                    eng.wait_ge(s_agg, q * U + k + 1)
                    eng.tensor_scalar(hot[k], iota, tile_lo[:, bass.ds(w, 1)], dst_f[:, bass.ds(c + k, 1)],
                                      ALU.add, ALU.is_equal).then_inc(s_hot, 1)
                for k in range(U):
                    eng.wait_ge(s_pre, q * U + k + 1 + U)
                    eng.wait_ge(s_g[k], q * 16 + 16)
                    eng.tensor_tensor(rows[k], ps[0:P, k, 0:D], rows[k], ALU.add).then_inc(s_sum, 1)

            units(eng, body)

        @block.scalar
        def _(eng):
            for g, tiles in groups:
                eng.wait_ge(s_rows, g + 1)
                eng.activation(stage[g], ps[0:P, g % 4, 0:len(tiles) * D], ACT.Copy).then_inc(s_p, 1)

            def body(w, c, q):
                def transposed(k):
                    eng.wait_ge(s_tr, q * U + k + 1)
                    eng.activation(hot_t[k], ps[0:P, 5 + k % 2, 0:P], ACT.Copy).then_inc(s_ht, 1)

                def relu(k):
                    eng.wait_ge(s_sum, q * U + k + 1)
                    eng.activation(rows[k], rows[k], ACT.Relu).then_inc(s_relu, 1)

                transposed(0)
                transposed(1)
                transposed(2)
                relu(0)
                transposed(3)
                relu(1)
                transposed(4)
                relu(2)
                relu(3)
                relu(4)

            def end(w):
                eng.wait_ge(s_tile, w + 1)
                eng.activation(R[:, bass.ds(w * P, P)], SUM, ACT.Copy).then_inc(s_ev, 1)

            units(eng, body, end=end)

        @block.tensor
        def _(eng):
            eng.wait_ge(s_load, 96)
            for g, tiles in groups:
                if g >= 4:
                    eng.wait_ge(s_p, g - 3)
                    eng.wait_ge(s_q, g - 3)
                for b, w in ((g % 4, wa), (4 + g % 4, wb)):
                    for i, s in enumerate(tiles):
                        ins = eng.matmul(ps[0:P, b, i * D:(i + 1) * D], x[:, s * P:(s + 1) * P], w,
                                         start=True, stop=True)
                ins.then_inc(s_rows, 1)
            eng.wait_ge(s_p, len(groups))
            eng.wait_ge(s_q, len(groups))
            eng.wait_ge(s_const, 3)
            for _ in range(U):
                eng.nop(nofuse=True).then_inc(s_agg, 1)
                eng.nop(nofuse=True).then_inc(s_pre, 1)
            eng.nop(nofuse=True).then_inc(s_ev, 1)

            def begin(w):
                eng.wait_ge(s_ev, w + 1)
                eng.nop(nofuse=True)
                eng.matmul(SUM, zero, zero[:, 0:P], start=True, stop=False, skip_group_check=True)

            def body(w, c, q):
                def transpose(k):
                    eng.wait_ge(s_hot, q * U + k + 1)
                    if k >= 2:
                        eng.wait_ge(s_ht, q * U + k - 1)
                    eng.transpose(ps[0:P, 5 + k % 2, 0:P], hot[k], ident[0:P, 0:P]).then_inc(s_tr, 1)

                def products(k):
                    eng.wait_ge(s_ht, q * U + k + 1)
                    eng.matmul(ps[0:P, k, 0:D], hot_t[k],
                               q_rows[:, bass.ds(w, 1), :].rearrange("p o c -> p (o c)"), start=True, stop=False)
                    eng.wait_ge(s_attr[k], q * 16 + 16)
                    eng.matmul(ps[0:P, k, 0:D], attr[k], w1e, start=False, stop=True).then_inc(s_pre, 1)

                def total(k):
                    eng.wait_ge(s_relu, q * U + k + 1)
                    eng.matmul(SUM, rows[k], hot[k], start=False, stop=False, skip_group_check=True).then_inc(s_agg, 1)

                transpose(0)
                transpose(1)
                products(0)
                transpose(2)
                products(1)
                transpose(3)
                total(0)
                products(2)
                transpose(4)
                total(1)
                products(3)
                total(2)
                products(4)
                total(3)
                total(4)

            def end(w):
                eng.matmul(SUM, zero, zero[:, 0:P], start=False, stop=True, skip_group_check=True).then_inc(s_tile, 1)

            units(eng, body, begin, end)

    n_ = Words(small)
    w2, u1a, u1b, u2 = (n_(D, D) for _ in range(4))
    b2, c1, c2 = n_(1, D), n_(D, 1), n_(D, 1)
    deg, agg, out = T[3][0:1, :], T[1], T[1]
    s_load, s_m, s_mo = sem("weights_loaded"), sem("messages_ready"), sem("messages_read_out")
    s_u, s_uo, s_o = sem("hidden_ready"), sem("hidden_read_out"), sem("update_ready")
    with nc.Block() as block:
        @block.sync
        def _(eng):
            for dst, src in ((w2, a["mlp_w2"]), (u1a, a["mlp_u1a"]), (u1b, a["mlp_u1b"]), (u2, a["mlp_u2"]),
                             (b2, a["mlp_b2"].rearrange("(o c) -> o c", o=1)), (deg, deg_row),
                             (c1, a["mlp_c1"].rearrange("(c o) -> c o", o=1)),
                             (c2, a["mlp_c2"].rearrange("(c o) -> c o", o=1))):
                eng.dma_start(dst, src).then_inc(s_load, 16)

        @block.tensor
        def _(eng):
            eng.wait_ge(s_load, 128)
            for j, c0, cw in PIECES:
                eng.matmul(ps[:, j, 0:cw], w2, R[:, c0:c0 + cw], start=True, stop=False)
                eng.matmul(ps[:, j, 0:cw], b2, deg[:, c0:c0 + cw], start=False, stop=True).then_inc(s_m, 1)
            for j, c0, cw in PIECES:
                eng.wait_ge(s_mo, j + 1)
                eng.matmul(ps[:, j, 0:cw], u1b, agg[:, c0:c0 + cw], start=True, stop=False)
                eng.matmul(ps[:, j, 0:cw], u1a, x[:, c0:c0 + cw], start=False, stop=True).then_inc(s_u, 1)
            for j, c0, cw in PIECES:
                eng.wait_ge(s_uo, j + 1)
                eng.matmul(ps[:, j, 0:cw], u2, R[:, c0:c0 + cw], start=True, stop=True).then_inc(s_o, 1)

        @block.vector
        def _(eng):
            for j, c0, cw in PIECES:
                eng.wait_ge(s_m, j + 1)
                eng.tensor_copy(agg[:, c0:c0 + cw], ps[:, j, 0:cw]).then_inc(s_mo, 1)
            for j, c0, cw in PIECES:
                eng.wait_ge(s_o, j + 1)
                eng.tensor_scalar(out[:, c0:c0 + cw], ps[:, j, 0:cw], c2, None, ALU.add)

        @block.scalar
        def _(eng):
            for j, c0, cw in PIECES:
                eng.wait_ge(s_u, j + 1)
                eng.activation(R[:, c0:c0 + cw], ps[:, j, 0:cw], ACT.Relu, bias=c1).then_inc(s_uo, 1)


def genconv(G):
    nc, a, sem, small, ranges, ident, ps, adj, T, x_kept = (
        G[k] for k in ("nc", "a", "sem", "small", "ranges", "ident", "ps", "adj", "T", "x_kept"))
    acc, x, z, den = T
    h1 = [T[2], T[3]]
    w2 = T[0][:, 0:2 * D].rearrange("p (k c) -> p k c", k=2)
    s_ = Words(small)
    parts = [s_(P, 3 * D, BF16) for _ in range(2)]
    e = [s_(D, P) for _ in range(2)]
    m, rest = s_(D, P), s_(P, D)
    w1 = s_(D, AH)
    vec = s_(D, 4)
    t_all = s_(D, AL)
    ext, lim, spread, top = s_(D, 2), s_(D, 2), s_(D, 1), s_(D, 1)
    shift_s, t_l, before_f, steps_f = s_(D, 1), s_(D, 1), s_(1, 1), s_(1, 1)
    stats, mv, sd, scale, shift, tmp, epsc = (s_(D, n) for n in (6 * NP, 2, 1, 2, 2, 1, 1))
    MISC = ps[0:P, 7, 0:D]
    SL = (N - 1) // 11

    s_saved, s_t, s_w1, s_w2 = sem("x_saved"), sem("t_loaded"), sem("w1_loaded"), sem("w2_loaded")
    s_v, s_spread, s_top, s_band = sem("vector_step"), sem("spread_ready"), sem("spread_reduced"), sem("bands_ready")
    s_z, s_e, s_m, s_f = sem("exponents_ready"), sem("exp_ready"), sem("message_ready"), sem("weighted_ready")
    s_tr, s_hi, s_rest, s_mid, s_parts = (sem(n) for n in ("transposed", "high_ready", "rest_ready", "middle_ready",
                                                           "parts_ready"))
    s_used, s_sum, s_dena, s_denv = (sem(n) for n in ("parts_used", "piece_summed", "den_by_scalar", "den_by_vector"))
    s_inv, s_num, s_agg, s_h = sem("den_step"), sem("sums_combined"), sem("aggregate_step"), sem("node_input_ready")
    s_h1, s_h1o, s_var, s_sd, s_aff, s_r1 = (sem(n) for n in ("hidden_product", "hidden_read_out", "variance",
                                                              "deviation", "affine", "hidden_ready"))
    s_x, s_xa, s_xv, s_fin, s_back = (sem(n) for n in ("x_product", "x_by_scalar", "x_by_vector", "weights_free",
                                                       "x_restored"))

    def bands(eng, l):
        return [eng.value_load(ranges[0:1, bass.ds(l * 2 + NT * R_BAND + k, 1)], min_val=lo, max_val=1 << 20)
                for k, lo in ((0, 1), (1, 0))]

    def tiles(eng, body, middle=None):
        body(0, 0, True, False)
        with eng.Fori(0, 11) as i:
            body(i * 2 + 1, 1, False, False)
            body(i * 2 + 2, 0, False, False)
            if middle:
                middle(i)
        body(23, 1, False, False)
        body(24, 0, False, True)

    def tile_cols(table, s):
        return table[:, s * P:(s + 1) * P] if isinstance(s, int) else table[:, bass.ds(s * P, P)]

    with nc.Block() as block:
        @block.sync
        def _(eng):
            eng.dma_start(t_all, a["agg_t"].rearrange("(o l) -> o l", o=1).to_broadcast([D, AL])).then_inc(s_t, 16)
            eng.dma_start(x_kept[:, :], T[0]).then_inc(s_saved, 16)
            with eng.Fori(0, AL) as l:
                eng.wait_ge(s_fin, l + 1)
                eng.dma_start(w1, a["agg_w1"][:, bass.ds(l * AH, AH)]).then_inc(s_w1, 16)
                eng.dma_start(vec, a["agg_vec"][:, bass.ds(l * 4, 4)]).then_inc(s_w1, 16)
                eng.wait_ge(s_h, (l + 1) * NP)
                eng.dma_start(w2, a["agg_w2"][:, bass.ds(l * 2, 2), :]).then_inc(s_w2, 16)
            eng.wait_ge(s_fin, AL + 1)
            eng.dma_start(T[0], x_kept[:, :]).then_inc(s_back, 16)
            eng.wait_ge(s_back, 16)

        @block.gpsimd
        def _(eng):
            with eng.Fori(0, AL) as l:
                eng.wait_ge(s_spread, l + 1)
                eng.nop(nofuse=True)
                eng.partition_all_reduce(top, spread, D, bass.bass_isa.ReduceOp.max).then_inc(s_top, 1)

        @block.vector
        def _(eng):
            once = Steps(eng, s_v)
            eng.memset(epsc, EPS_BN)
            once(eng.memset(before_f, 0.0))
            eng.tensor_copy(x, T[0])
            once(eng.memset(tmp, 0.0))
            eng.wait_ge(s_t, 16)
            eng.wait_ge(s_saved, 16)
            first = once.n
            PER = 18
            with eng.Fori(0, AL) as l:
                step = Steps(eng, s_v, l * PER + first)
                eng.wait_ge(s_xa, l * len(ACT_P) + 1)
                eng.wait_ge(s_xv, l * len(DVE_P) + 1)
                eng.tensor_copy(t_l, t_all[:, bass.ds(l, 1)])
                eng.memset(acc, 0.0)
                eng.tensor_reduce(ext[:, 0:1], x, axis=AX.X, op=ALU.max)
                step(eng.tensor_reduce(ext[:, 1:2], x, axis=AX.X, op=ALU.min))
                step(eng.tensor_scalar(ext, ext, 0.0, EPS_MSG, ALU.max, ALU.add))
                step(eng.tensor_scalar(ext, ext, t_l, None, ALU.mult))
                eng.tensor_reduce(lim[:, 0:1], ext, axis=AX.X, op=ALU.max)
                step(eng.tensor_reduce(lim[:, 1:2], ext, axis=AX.X, op=ALU.min))
                step(eng.tensor_tensor(spread, lim[:, 0:1], lim[:, 1:2], ALU.subtract))
                step(eng.tensor_scalar(spread, spread, BAND - REACH, 1.0 / BAND, ALU.add, ALU.mult))
                eng.tensor_scalar(spread, spread, 0.0, float(1 << 19), ALU.max, ALU.min).then_inc(s_spread, 1)
                step(eng.tensor_copy(shift_s, lim[:, 0:1]))
                eng.wait_ge(s_top, l + 1)
                step.apart = True
                bl = ranges[0:1, bass.ds(l * 2 + NT * R_BAND, 1)]
                step(eng.tensor_scalar(bl, top[0:1, :], 1.0, None, ALU.add))
                step(eng.tensor_copy(ranges[0:1, bass.ds(l * 2 + NT * R_BAND + 1, 1)], before_f))
                step(eng.tensor_copy(steps_f, bl))
                eng.tensor_tensor(before_f, before_f, steps_f, ALU.add).then_inc(s_band, 1)
                step.apart = False
                eng.wait_ge(s_band, l + 1)
                eng.nop(nofuse=True)
                count, before = bands(eng, l)
                with eng.Fori(0, count) as b:
                    r = before + b
                    zs = Steps(eng, s_agg, r * (NP + 3))
                    for c0, c1 in ((0, P), (P, N)):
                        zc, xc = z[:, c0:c1], x[:, c0:c1]
                        zs(eng.tensor_scalar(zc, xc, 0.0, EPS_MSG, ALU.max, ALU.add))
                        eng.tensor_scalar(zc, zc, t_l, shift_s, ALU.mult, ALU.subtract).then_inc(s_z, 1)
                        eng.wait_ge(s_z, r * 4 + (2 if c0 else 0) + 1)
                        eng.tensor_scalar(zc, zc, 0.0, None, ALU.min).then_inc(s_z, 1)

                    def tile(q, s, k):
                        n = r * (2 * NT) + q * NT + s
                        if q == 1:
                            nf = r * NT + s
                            eng.tensor_scalar(m, tile_cols(x, s), 0.0, EPS_MSG, ALU.max, ALU.add).then_inc(s_m, 1)
                            eng.wait_ge(s_m, nf + 1)
                            eng.wait_ge(s_e, n + 1)
                            eng.tensor_tensor(e[k], e[k], m, ALU.mult).then_inc(s_f, 1)
                            eng.wait_ge(s_f, nf + 1)
                        eng.wait_ge(s_hi, n + 1)
                        eng.tensor_tensor(rest, MISC, parts[k][:, 0:D], ALU.subtract).then_inc(s_rest, 1)
                        eng.wait_ge(s_rest, n + 1)
                        eng.tensor_copy(parts[k][:, D:2 * D], rest).then_inc(s_mid, 1)
                        eng.wait_ge(s_mid, n + 1)
                        eng.tensor_tensor(parts[k][:, 2 * D:3 * D], rest, parts[k][:, D:2 * D],
                                          ALU.subtract).then_inc(s_parts, 1)
                        eng.wait_ge(s_parts, n + 2)
                        eng.nop(nofuse=True)

                    def weights(i, c0, cw):
                        d, ac = den[:, bass.ds(c0, cw)], acc[:, bass.ds(c0, cw)]
                        ds_ = Steps(eng, s_inv, r * 48 + i * 4, apart=True)
                        ds_(eng.tensor_scalar(d, d, 1e-31, None, ALU.max))
                        ds_(eng.reciprocal(d, d))
                        ds_(eng.scalar_tensor_tensor(d, d, float(np.exp(REACH)), d, ALU.is_le, ALU.mult))
                        ds_(eng.scalar_tensor_tensor(d, ac, 0.0, d, ALU.is_equal, ALU.mult))

                    tiles(eng, lambda s, k, first, last: tile(0, s, k))
                    for i, j in enumerate(DVE_P):
                        _, c0, cw = PIECES[j]
                        eng.wait_ge(s_sum, r * (2 * NP) + j + 2)
                        eng.tensor_copy(den[:, c0:c0 + cw], ps[:, j, 0:cw]).then_inc(s_denv, 1)
                    eng.wait_ge(s_denv, r * len(DVE_P) + len(DVE_P))
                    eng.wait_ge(s_dena, r * len(ACT_P) + len(ACT_P))
                    tiles(eng, lambda s, k, first, last: tile(1, s, k), lambda i: weights(i, i * SL, SL))
                    weights(11, 11 * SL, N - 11 * SL)
                    for j, c0, cw in PIECES:
                        eng.wait_ge(s_sum, r * (2 * NP) + NP + j + 2)
                        d, ac = den[:, c0:c0 + cw], acc[:, c0:c0 + cw]
                        eng.tensor_tensor(d, ps[:, j, 0:cw], d, ALU.mult).then_inc(s_num, 1)
                        eng.wait_ge(s_num, r * NP + j + 2)
                        zs(eng.tensor_tensor(ac, ac, d, ALU.add))
                    zs(eng.tensor_scalar(shift_s, shift_s, -BAND, None, ALU.add))
                    assert zs.n == NP + 3
                for j, c0, cw in PIECES:
                    eng.tensor_tensor(x[:, c0:c0 + cw], x[:, c0:c0 + cw], acc[:, c0:c0 + cw], ALU.add).then_inc(s_h, 1)
                eng.wait_ge(s_w1, l * 32 + 32)
                for k in range(2):
                    for j, c0, cw in PIECES:
                        eng.wait_ge(s_h1o, l * (2 * NP) + k * NP + j + 1)
                        ins = eng.bn_stats(stats[:, 6 * j:6 * j + 6], h1[k][:, c0:c0 + cw])
                    step(ins)
                    eng.nop(nofuse=True)
                    eng.bn_aggr(mv, stats.rearrange("p (j f) -> p j f", f=6)).then_inc(s_var, 1)
                    eng.wait_ge(s_sd, l * 2 + k + 1)
                    sc, sh = scale[:, k:k + 1], shift[:, k:k + 1]
                    step(eng.reciprocal(sc, sd))
                    step(eng.tensor_tensor(sc, sc, vec[:, k:k + 1], ALU.mult))
                    step(eng.tensor_tensor(tmp, mv[:, 0:1], sc, ALU.mult))
                    eng.tensor_tensor(sh, vec[:, 2 + k:3 + k], tmp, ALU.subtract).then_inc(s_aff, 1)
                for j in DVE_P:
                    _, c0, cw = PIECES[j]
                    eng.wait_ge(s_x, l * NP + j + 1)
                    eng.tensor_scalar(x[:, c0:c0 + cw], ps[:, j, 0:cw], 0.0, None, ALU.max).then_inc(s_xv, 1)
                assert step.n == PER, step.n

        @block.scalar
        def _(eng):
            with eng.Fori(0, AL) as l:
                eng.wait_ge(s_band, l + 1)
                eng.nop(nofuse=True)
                count, before = bands(eng, l)
                with eng.Fori(0, count) as b:
                    r = before + b

                    def exponential(q, s, k, first):
                        n = r * (2 * NT) + q * NT + s
                        eng.wait_ge(s_z, r * 4 + (2 if first else 4))
                        eng.wait_ge(s_tr, n + (2 if first else 1))
                        eng.activation(e[k], tile_cols(z, s), ACT.Exp).then_inc(s_e, 1)

                    def high(q, s, k, first):
                        n = r * (2 * NT) + q * NT + s
                        if first:
                            eng.wait_ge(s_sum, (r * 2 + q) * NP + 1)
                        else:
                            eng.wait_ge(s_used, (r * 2 + q) * (NT - 1) + s)
                        eng.wait_ge(s_tr, n + 3)
                        eng.activation(parts[k][:, 0:D], MISC, ACT.Copy).then_inc(s_hi, 1)

                    for q in range(2):
                        exponential(q, 0, 0, True)
                        exponential(q, 1, 1, False)

                        def body(s, k, first, last):
                            high(q, s, k, first)
                            if not last and not (isinstance(s, int) and s >= 23):
                                exponential(q, s + 2, k, False)

                        tiles(eng, body)
                        if q == 0:
                            for j in ACT_P:
                                _, c0, cw = PIECES[j]
                                eng.wait_ge(s_sum, r * (2 * NP) + j + 2)
                                eng.activation(den[:, c0:c0 + cw], ps[:, j, 0:cw], ACT.Copy).then_inc(s_dena, 1)
                for k in range(2):
                    for j, c0, cw in PIECES:
                        eng.wait_ge(s_h1, l * (2 * NP) + k * NP + j + 1)
                        eng.activation(h1[k][:, c0:c0 + cw], ps[:, j, 0:cw], ACT.Copy).then_inc(s_h1o, 1)
                    eng.wait_ge(s_var, l * 2 + k + 1)
                    eng.activation(sd, mv[:, 1:2], ACT.Sqrt, bias=epsc).then_inc(s_sd, 1)
                for j, c0, cw in PIECES:
                    for k in range(2):
                        if j == 0:
                            eng.wait_ge(s_aff, l * 2 + k + 1)
                        eng.activation(h1[k][:, c0:c0 + cw], h1[k][:, c0:c0 + cw], ACT.Relu,
                                       bias=shift[:, k:k + 1], scale=scale[:, k:k + 1]).then_inc(s_r1, 1)
                for j in ACT_P:
                    _, c0, cw = PIECES[j]
                    eng.wait_ge(s_x, l * NP + j + 1)
                    eng.activation(x[:, c0:c0 + cw], ps[:, j, 0:cw], ACT.Relu).then_inc(s_xa, 1)

        @block.tensor
        def _(eng):
            for s, n in ((s_xa, 1), (s_xv, 1), (s_num, 1), (s_tr, 2), (s_used, 1), (s_sum, 1), (s_parts, 1), (s_fin, 1)):
                for _ in range(n):
                    eng.nop(nofuse=True).then_inc(s, 1)
            with eng.Fori(0, AL) as l:
                eng.wait_ge(s_band, l + 1)
                eng.nop(nofuse=True)
                count, before = bands(eng, l)
                eng.wait_ge(s_xa, l * len(ACT_P) + 1)
                eng.wait_ge(s_xv, l * len(DVE_P) + 1)
                eng.nop(nofuse=True)
                with eng.Fori(0, count) as b:
                    r = before + b
                    for q in range(2):
                        def transpose(s, k):
                            n = r * (2 * NT) + q * NT + s
                            eng.wait_ge(s_e, n + 1) if q == 0 else eng.wait_ge(s_f, r * NT + s + 1)
                            eng.wait_ge(s_parts, n + 1)
                            eng.transpose(MISC, e[k], ident[:, :]).then_inc(s_tr, 1)

                        def products(s, k, first, last):
                            n = r * (2 * NT) + q * NT + s
                            eng.wait_ge(s_parts, n + 2)
                            for i in range(3):
                                for j, c0, cw in PIECES:
                                    if first and i == 0:
                                        if q == 0 and j == 0:
                                            eng.wait_ge(s_num, r * NP + 1)
                                        if q == 1 and j in ACT_P:
                                            eng.wait_ge(s_dena, r * len(ACT_P) + ACT_P.index(j) + 1)
                                        if q == 1 and j in DVE_P:
                                            eng.wait_ge(s_denv, r * len(DVE_P) + DVE_P.index(j) + 1)
                                    if isinstance(s, int):
                                        cols = adj[:, s, c0:c0 + cw]
                                    else:
                                        cols = adj[:, bass.ds(s, 1), c0:c0 + cw].rearrange("p o c -> p (o c)")
                                    ins = eng.matmul(ps[:, j, 0:cw], parts[k][:, i * D:(i + 1) * D], cols,
                                                     start=first and i == 0, stop=last and i == 2,
                                                     skip_group_check=True)
                                    if last and i == 2:
                                        ins.then_inc(s_sum, 1)
                            if not last:
                                ins.then_inc(s_used, 1)

                        transpose(0, 0)

                        def both(s, k, first, last):
                            if not last:
                                transpose(s + 1, 1 - k)
                            products(s, k, first, last)

                        tiles(eng, both)
                for k in range(2):
                    for j, c0, cw in PIECES:
                        if k == 0:
                            eng.wait_ge(s_h, l * NP + j + 1)
                            if j == 0:
                                eng.wait_ge(s_w1, l * 32 + 32)
                        else:
                            eng.wait_ge(s_h1o, l * (2 * NP) + j + 1)
                        eng.matmul(ps[:, j, 0:cw], w1[:, k * D:(k + 1) * D], x[:, c0:c0 + cw],
                                   start=True, stop=True).then_inc(s_h1, 1)
                eng.wait_ge(s_w2, l * 16 + 16)
                for j, c0, cw in PIECES:
                    eng.wait_ge(s_r1, l * (2 * NP) + 2 * j + 2)
                    eng.matmul(ps[:, j, 0:cw], w2[:, 0, :], h1[0][:, c0:c0 + cw], start=True, stop=False)
                    eng.matmul(ps[:, j, 0:cw], w2[:, 1, :], h1[1][:, c0:c0 + cw], start=False,
                               stop=True).then_inc(s_x, 1)
                eng.wait_ge(s_xa, (l + 1) * len(ACT_P) + 1)
                eng.wait_ge(s_xv, (l + 1) * len(DVE_P) + 1)
                eng.nop(nofuse=True).then_inc(s_fin, 1)


def interaction(G):
    nc, a, sem, work, small, ranges, ident, ps, T, adj = (
        G[k] for k in ("nc", "a", "sem", "work", "small", "ranges", "ident", "ps", "T", "adj"))
    h_rows, edge_rows = G["h_rows"], G["edge_rows"]
    x, S = T[0], T[2]
    S_late = work[:, 2 * N - P:3 * N]
    HALVES = range(2)
    free = Words(G["adj_words"])
    rows_t = free(P, (NC + 1) * ROW)
    row3 = rows_t.rearrange("p (c f) -> p c f", f=ROW)
    dst_i = free(P, NC + 1, I32)
    groups = [(g, range(4 * g, min(NT, 4 * g + 4))) for g in range((NT + 3) // 4)]
    stage = [free(P, 4 * D) for _ in groups]
    gathered, pre, soft, msg, hot = ([free(P, UH * n) for _ in HALVES] for n in (D, D, D, D, P))
    attr_t = [free(UH * ROW, P) for _ in HALVES]
    attr, rel = free(P, US * ROW), free(P, US)
    iota, tile_lo, idx = free(P, P), free(P, NT), [free(P, UH, I32) for _ in HALVES]
    b_in, zero, w_f = free(P, D), free(1, D), free(UH * ROW, UH * D)
    s_ = Words(small)
    w_in, w_out, b_out = s_(D, D), s_(D, D), s_(D, 1)
    LOADS = 5
    cuts = [i * (NC // LOADS) for i in range(LOADS + 1)]

    s_load, s_const, s_er, s_dst = sem("weights_loaded"), sem("constants_ready"), sem("edge_rows_loaded"), sem("dst_ready")
    s_rows, s_h, s_hrow, s_wz = sem("rows_ready"), sem("h_read_out"), sem("h_rows_written"), sem("weights_zeroed")
    s_st, s_rel, s_hot, s_agg = sem("attributes_staged"), sem("places_ready"), sem("hots_ready"), sem("edges_summed")
    s_idx, s_g, s_tr, s_at, s_prod, s_pre, s_min, s_exp, s_ln, s_soft, s_msg = (
        [sem(f"{n}_{h}") for h in "ab"] for n in (
            "index_ready", "rows_gathered", "transposed", "attributes_ready", "filter_product", "filter_read_out",
            "bounded", "exp_ready", "log_ready", "softplus_ready", "message_ready"))
    s_half, s_tile, s_ev = sem("half_ready"), sem("tile_summed"), sem("tile_read_out")
    A_MAX = 40.0
    half = s_(D, 1)
    SUM, PROD, TRANS = ps[:, 7, 0:P], [ps[0:P, h, 0:UH * D] for h in HALVES], [ps[0:UH * ROW, 2 + h, 0:P] for h in HALVES]
    WEIGHTS = 16 * (4 + 2 * UH)

    def units(eng, body, first=None):
        with eng.Fori(0, NT) as w:
            start, count, before = load_range(eng, ranges, R_SRC, w, STEPS)
            if first:
                first(w, nc.s_assert_within(start, 0, NC + 1 - US), before)
            with eng.Fori(1 if first else 0, count) as u:
                body(w, nc.s_assert_within(start + u * US, 0, NC + 1 - US), before + u)
        _, count, before = load_range(eng, ranges, R_SRC, NT - 1, STEPS)
        return before + count

    with nc.Block() as block:
        @block.sync
        def _(eng):
            for dst, src in ((w_in, a["int_w_in"]), (w_out, a["int_w_out"]),
                             (b_out, a["int_b_out"].rearrange("(c o) -> c o", o=1)),
                             (b_in, a["int_b_in"].rearrange("(o c) -> o c", o=1).to_broadcast([P, D]))):
                eng.dma_start(dst, src).then_inc(s_load, 16)
            er = edge_rows.rearrange("(p c) f -> p (c f)", p=P)
            for c0, c1 in zip(cuts, cuts[1:]):
                eng.dma_start(rows_t[:, c0 * ROW:c1 * ROW], er[:, c0 * ROW:c1 * ROW]).then_inc(s_er, 16)
            eng.wait_ge(s_wz, 1)
            for k in range(UH):
                cols = w_f[:, k * D:(k + 1) * D]
                eng.dma_start(cols[k * ROW:k * ROW + FR, :], a["int_w_f"]).then_inc(s_load, 16)
                eng.dma_start(cols[k * ROW + FR:k * ROW + FR + 1, :],
                              a["int_b_f"].rearrange("(o c) -> o c", o=1)).then_inc(s_load, 16)
            h_view = h_rows.rearrange("(s p) c -> p s c", p=P)
            for g, tiles in groups:
                eng.wait_ge(s_h, g + 1)
                eng.dma_start(h_view[:, tiles[0]:tiles[-1] + 1, :],
                              stage[g][:, 0:len(tiles) * D].rearrange("p (s c) -> p s c", c=D)).then_inc(s_hrow, 16)
            eng.wait_ge(s_hrow, 16 * len(groups))

        @block.gpsimd
        def _(eng):
            imprecise = dict(allow_small_or_imprecise_dtypes=True)
            eng.memset(w_f, 0.0).then_inc(s_wz, 1)
            eng.iota(tile_lo, pattern=[[P, NT]], base=0, channel_multiplier=0, **imprecise).then_inc(s_const, 1)
            eng.iota(iota, pattern=[[1, P]], base=0, channel_multiplier=0, **imprecise).then_inc(s_const, 1)
            eng.memset(zero, 0.0).then_inc(s_const, 1)
            for h in HALVES:
                eng.memset(idx[h], 0)
                eng.memset(pre[h], 0.0)
                eng.memset(soft[h], 0.0)
            eng.memset(attr, 0.0)
            eng.memset(rel, 0.0).then_inc(s_const, 1)
            eng.wait_ge(s_const, 4)
            eng.nop(nofuse=True)
            for h in HALVES:
                for k in range(UH):
                    eng.indirect_dma_start(gathered[h][:, k * D:(k + 1) * D], None, G["p_rows"][:, :],
                                           bass.IndirectOffsetOnAxis(ap=idx[h][:, k:k + 1], axis=0)
                                           ).then_inc(s_g[h], 16)
            eng.wait_ge(s_dst, 1)
            eng.wait_ge(s_hrow, 16 * len(groups))

            def body(w, c, q):
                for h in HALVES:
                    eng.wait_ge(s_msg[h], q + 1)
                    eng.nop(nofuse=True)
                    eng.tensor_copy(idx[h], dst_i[:, bass.ds(c + h * UH, UH)]).then_inc(s_idx[h], 1)
                    eng.wait_ge(s_idx[h], q + 1)
                    eng.nop(nofuse=True)
                    for k in range(UH):
                        eng.indirect_dma_start(gathered[h][:, k * D:(k + 1) * D], None, h_rows[:, :],
                                               bass.IndirectOffsetOnAxis(ap=idx[h][:, k:k + 1], axis=0)
                                               ).then_inc(s_g[h], 16)

            units(eng, body)

        @block.vector
        def _(eng):
            eng.memset(half, 0.5).then_inc(s_half, 1)
            eng.memset(row3[:, NC:NC + 1, 0:SRC_C], 0.0)
            eng.memset(row3[:, NC:NC + 1, SRC_C:ROW], -1.0)
            eng.wait_ge(s_load, WEIGHTS)
            for g, tiles in groups:
                n = len(tiles)
                eng.wait_ge(s_rows, g + 1)
                eng.tensor_tensor(stage[g][:, 0:n * D].rearrange("p (s c) -> p s c", c=D),
                                  ps[0:P, g % 4, 0:n * D].rearrange("p (s c) -> p s c", c=D),
                                  b_in.unsqueeze(1).to_broadcast([P, n, D]), ALU.add).then_inc(s_h, 1)
            eng.wait_ge(s_er, 16 * LOADS)
            eng.tensor_copy(dst_i, row3[:, :, DST_C]).then_inc(s_dst, 1)
            eng.wait_ge(s_const, 4)
            at3 = attr.rearrange("p (c f) -> p c f", f=ROW)

            def hots(q):
                eng.wait_ge(s_agg, q + 1)
                for k in range(US):
                    ins = eng.tensor_scalar(hot[k // UH][:, k % UH * P:(k % UH + 1) * P], iota, rel[:, k:k + 1],
                                            at3[:, k, RCUT_C:RCUT_C + 1], ALU.is_equal, ALU.mult)
                ins.then_inc(s_hot, 1)

            def message(q, h):
                eng.wait_ge(s_ln[h], q + 1)
                eng.scalar_tensor_tensor(soft[h], pre[h], -LOG2, soft[h], ALU.add, ALU.max).then_inc(s_soft[h], 1)
                eng.wait_ge(s_soft[h], q + 1)
                eng.wait_ge(s_g[h], (q + 1) * (16 * UH))
                eng.tensor_tensor(msg[h], soft[h], gathered[h], ALU.mult).then_inc(s_msg[h], 1)

            def body(w, c, q):
                hots(q)
                eng.wait_ge(s_hot, q + 1)
                for h in HALVES:
                    eng.wait_ge(s_tr[h], q + 1)
                eng.nop(nofuse=True)
                eng.tensor_copy(attr, row3[:, bass.ds(c, US), :].rearrange("p c f -> p (c f)")).then_inc(s_st, 1)
                eng.wait_ge(s_st, q + 1)
                eng.tensor_scalar(rel, at3[:, :, SRC_C], tile_lo[:, bass.ds(w, 1)], None, ALU.subtract).then_inc(s_rel, 1)
                for h in HALVES:
                    eng.wait_ge(s_tr[h], q + 2)
                    eng.tensor_copy(attr_t[h], TRANS[h]).then_inc(s_at[h], 1)
                for h in HALVES:
                    message(q, h)
                for h in HALVES:
                    eng.wait_ge(s_pre[h], q + 2)
                    eng.wait_ge(s_msg[h], q + 1)
                    eng.tensor_scalar(soft[h], pre[h], A_MAX, None, ALU.min).then_inc(s_min[h], 1)
                eng.wait_ge(s_rel, q + 1)

            q = units(eng, body)
            hots(q)
            for h in HALVES:
                message(q, h)

        @block.scalar
        def _(eng):
            eng.wait_ge(s_half, 1)

            def evacuate(w):
                eng.wait_ge(s_tile, w + 1)
                eng.activation(S_late[:, bass.ds(w * P, P)], SUM, ACT.Copy).then_inc(s_ev, 1)

            def body(w, c, q, first=False):
                for h in HALVES:
                    eng.wait_ge(s_prod[h], q + 1)
                    eng.wait_ge(s_soft[h], q + 1)
                    eng.activation(pre[h], PROD[h], ACT.Copy).then_inc(s_pre[h], 1)
                for h in HALVES:
                    eng.wait_ge(s_min[h], q + 1)
                    eng.activation(soft[h], soft[h], ACT.Exp).then_inc(s_exp[h], 1)
                if first:
                    evacuate(w)
                for h in HALVES:
                    eng.wait_ge(s_exp[h], q + 1)
                    eng.activation(soft[h], soft[h], ACT.Ln, bias=half[0:P, :], scale=0.5).then_inc(s_ln[h], 1)

            units(eng, body, lambda w, c, q: body(w, c, q, True))
            evacuate(NT)

        @block.tensor
        def _(eng):
            eng.wait_ge(s_load, WEIGHTS)
            for g, tiles in groups:
                if g >= 4:
                    eng.wait_ge(s_h, g - 3)
                for i, s in enumerate(tiles):
                    ins = eng.matmul(ps[0:P, g % 4, i * D:(i + 1) * D], x[:, s * P:(s + 1) * P], w_in,
                                     start=True, stop=True)
                ins.then_inc(s_rows, 1)
            eng.wait_ge(s_h, len(groups))
            eng.wait_ge(s_const, 4)
            for s in [s_agg] + s_tr + s_pre + s_ln:
                eng.nop(nofuse=True).then_inc(s, 1)

            def opened():
                eng.matmul(SUM, zero, zero[:, 0:P], start=True, stop=False, skip_group_check=True)

            def closed():
                eng.matmul(SUM, zero, zero[:, 0:P], start=False, stop=True, skip_group_check=True).then_inc(s_tile, 1)

            def front(q):
                eng.wait_ge(s_st, q + 1)
                for h in HALVES:
                    eng.transpose(TRANS[h], attr[:, h * UH * ROW:(h + 1) * UH * ROW], ident[0:P, 0:P]).then_inc(s_tr[h], 1)
                for h in HALVES:
                    eng.wait_ge(s_at[h], q + 1)
                    eng.wait_ge(s_pre[h], q + 1)
                    eng.matmul(PROD[h], attr_t[h], w_f, start=True, stop=True).then_inc(s_prod[h], 1)

            def totals(q):
                eng.wait_ge(s_hot, q + 1)
                for h in HALVES:
                    eng.wait_ge(s_msg[h], q + 1)
                    for k in range(UH):
                        ins = eng.matmul(SUM, msg[h][:, k * D:(k + 1) * D], hot[h][:, k * P:(k + 1) * P],
                                         start=False, stop=False, skip_group_check=True)
                ins.then_inc(s_agg, 1)

            def first(w, c, q):
                front(q)
                totals(q)
                closed()
                eng.wait_ge(s_ev, w + 1)
                eng.nop(nofuse=True)
                opened()

            def body(w, c, q):
                front(q)
                totals(q)

            opened()
            q = units(eng, body, first)
            totals(q)
            closed()


    s_o, s_e, s_m, s_l, s_b = (sem(n) for n in ("output_product", "exp_ready", "product_bounded", "log_ready",
                                                "bias_ready"))
    b_low, e = s_(D, 1), T[1]
    with nc.Block() as block:
        @block.tensor
        def _(eng):
            for j, c0, cw in PIECES:
                eng.matmul(ps[:, j, 0:cw], w_out, S[:, c0:c0 + cw], start=True, stop=True).then_inc(s_o, 1)

        @block.scalar
        def _(eng):
            for j, c0, cw in PIECES:
                eng.wait_ge(s_m, j + 1)
                eng.activation(e[:, c0:c0 + cw], e[:, c0:c0 + cw], ACT.Exp).then_inc(s_e, 1)
            for j, c0, cw in PIECES:
                eng.wait_ge(s_e, j + 1)
                eng.activation(e[:, c0:c0 + cw], e[:, c0:c0 + cw], ACT.Ln, bias=half, scale=0.5).then_inc(s_l, 1)

        @block.vector
        def _(eng):
            eng.tensor_scalar(b_low, b_out, -LOG2, None, ALU.add).then_inc(s_b, 1)
            for j, c0, cw in PIECES:
                eng.wait_ge(s_o, j + 1)
                eng.tensor_scalar(e[:, c0:c0 + cw], ps[:, j, 0:cw], b_out, A_MAX, ALU.add, ALU.min).then_inc(s_m, 1)
            eng.wait_ge(s_b, 1)
            for j, c0, cw in PIECES:
                eng.wait_ge(s_l, j + 1)
                eng.scalar_tensor_tensor(e[:, c0:c0 + cw], ps[:, j, 0:cw], b_low, e[:, c0:c0 + cw],
                                         ALU.add, ALU.max)


def store(G):
    nc, sem, T, out = G["nc"], G["sem"], G["T"], G["out"]
    s_out = sem("stored")
    with nc.Block() as block:
        @block.sync
        def _(eng):
            eng.dma_start(out[:, :], T[0]).then_inc(s_out, 16)
            eng.wait_ge(s_out, 16)


def layout(inputs):
    i = {k: np.asarray(v) for k, v in inputs.items()}
    cols = lambda v: v.reshape(NC, P).T
    r = dict(x=i["x"].T, dst=i["dst"], src_cols=cols(i["src"]), dst_cols=cols(i["dst"]),
             weight_cols=cols(i["edge_weight"]), edge_attr_20=i["edge_attr_20"], edge_attr_64=i["edge_attr_64"].T,
             gin_w1=i["L0_gnn_W1"].transpose(2, 0, 1).reshape(D, GL * GH),
             gin_w2=i["L0_gnn_W2"].transpose(2, 0, 1).reshape(GH, GL * GH),
             gin_w3=i["L0_gnn_W3"].transpose(2, 0, 1).reshape(GH, GL * D),
             gin_b3=i["L0_gnn_b3"].T, gin_eps=i["L0_gnn_eps"])
    for n in ("b1", "g1", "bt1", "b2", "g2", "bt2"):
        r["gin_" + n] = i["L0_gnn_" + n].T
    w1, u1 = i["L1_gnn_W1"].T, i["L1_gnn_U1"].T
    r.update(mlp_w1a=w1[:D], mlp_w1b=w1[D:2 * D], mlp_w1e=w1[2 * D:], mlp_b1=i["L1_gnn_b1"],
             mlp_w2=i["L1_gnn_W2"].T, mlp_b2=i["L1_gnn_b2"], mlp_u1a=u1[:D], mlp_u1b=u1[D:],
             mlp_c1=i["L1_gnn_c1"], mlp_u2=i["L1_gnn_U2"].T, mlp_c2=i["L1_gnn_c2"])
    gb = np.stack([i["L2_gnn_gamma"].reshape(AL, 2, D), i["L2_gnn_beta"].reshape(AL, 2, D)], axis=1)
    r.update(agg_w1=i["L2_gnn_W1"].transpose(1, 0, 2).reshape(D, AL * AH),
             agg_w2=i["L2_gnn_W2"].reshape(AL * 2, D, D).transpose(1, 0, 2),
             agg_vec=gb.transpose(3, 0, 1, 2).reshape(D, AL * 4), agg_t=i["L2_gnn_t"])
    r.update(int_w_in=i["L3_gnn_W_in"].T, int_b_in=i["L3_gnn_b_in"], int_w_f=i["L3_gnn_W_f"].T,
             int_b_f=i["L3_gnn_b_f"], int_w_out=i["L3_gnn_W_out"].T, int_b_out=i["L3_gnn_b_out"])
    return {k: np.ascontiguousarray(v) for k, v in r.items()}


def kernel(**inputs):
    import concourse.bacc as bacc
    from concourse.bass_utils import run_bass_kernel_spmd as run
    nc = bacc.Bacc("TRN2", target_bir_lowering=False, num_devices=1)
    arrays = layout(inputs)
    aps = {k: nc.dram_tensor(k, v.shape, mybir.dt.from_np(v.dtype), kind="ExternalInput").ap()
           for k, v in arrays.items()}
    out = nc.dram_tensor("out", (D, N), F32, kind="ExternalOutput").ap()
    build(nc, aps, out)
    r = run(nc, [arrays], core_ids=[0])
    return np.ascontiguousarray(r.results[0]["out"].T)
```

```python
import numpy as np
import concourse.bass as bass
import concourse.mybir as mybir
from contextlib import ExitStack

F32, BF16, F16 = mybir.dt.float32, mybir.dt.bfloat16, mybir.dt.float16
I32, I16 = mybir.dt.int32, mybir.dt.int16
ALU = mybir.AluOpType
ACT = mybir.ActivationFunctionType
AX = mybir.AxisListType

N = 3125
E = 53125
D = 128
P = 125
NT = N // P
NC = E // P
CR = 85
CJ = NC // CR
U = 5
UH = 3
US = 2 * UH
STEPS = (NC + US - 1) // US
AS = 3
ASTEPS = (NC + AS - 1) // AS
PW = 450
PIECES = [(j, j * PW, min(PW, N - j * PW)) for j in range((N + PW - 1) // PW)]
NP = len(PIECES)
ACT_P = [0, 2, 4]
DVE_P = [1, 3, 5, 6]
GL, GH = 4, 32
FE, FR = 64, 20
ROW = 24
ONE_C, RCUT_C, DST_C, SRC_C = 20, 21, 22, 23
AL, AH = 3, 256
EPS_MSG = 1e-7
EPS_BN = 1e-5
EPS_LN = 1e-5
BAND = 64.0
REACH = 70.0
LOG2 = float(np.log(2.0))
R_ADJ, R_DST, R_SRC, R_BAND = range(4)
NR = 4
assert ASTEPS < 256


class Steps:

    def __init__(self, eng, sem, base=0, apart=False):
        self.eng, self.sem, self.base, self.n, self.apart = eng, sem, base, 0, apart

    def __call__(self, ins):
        self.n += 1
        ins.then_inc(self.sem, 1)
        self.eng.wait_ge(self.sem, self.base + self.n)
        if self.apart:
            self.eng.nop(nofuse=True)


class Words:

    def __init__(self, region, at=0, end=None):
        self.region, self.at, self.end = region, at, end or region.shape[1]

    def __call__(self, rows, cols, dt=F32):
        words = cols if dt in (F32, I32) else (cols + 1) // 2
        ap = self.region[:, self.at:self.at + words]
        self.at += words
        assert self.at <= self.end, (self.at, self.end)
        return (ap if dt == F32 else ap.bitcast(dt))[0:rows, 0:cols]


def build(nc, a, out):
    ctx = ExitStack()
    with ctx, nc.allow_non_contiguous_dma(reason="small columns"):
        used, held = {}, []

        def sem(name):
            used[name] = used.get(name, 0) + 1
            held.append(nc.alloc_semaphore(f"{name}_{used[name]}"))
            return held[-1]

        def phase(body, *args, **options):
            body(G, *args, **options)
            nc.clear_and_free_semaphores(held)
            held.clear()
            nc.all_engine_barrier()

        adj_all = ctx.enter_context(nc.sbuf_tensor("adj", [P, NT * N + 1], F16))
        adj = adj_all[:, 0:NT * N].rearrange("p (s n) -> p s n", n=N)
        work = ctx.enter_context(nc.sbuf_tensor("work", [128, 4 * N], F32))
        small = ctx.enter_context(nc.sbuf_tensor("small", [128, 1256], F32))
        ranges = ctx.enter_context(nc.sbuf_tensor("ranges", [1, NR * NT], I32))
        ident = ctx.enter_context(nc.sbuf_tensor("ident", [128, 128], F32))
        ps = ctx.enter_context(nc.psum_tensor("ps", [128, 8, 512], F32))
        T = [work[:, k * N:(k + 1) * N] for k in range(4)]

        p_rows = nc.dram_tensor("p_rows", (N, D), F32, kind="Internal").ap()
        h_rows = nc.dram_tensor("h_rows", (N, D), F32, kind="Internal").ap()
        edge_rows = nc.dram_tensor("edge_rows", (E, ROW), F32, kind="Internal").ap()
        deg_row = nc.dram_tensor("deg_row", (1, N), F32, kind="Internal").ap()
        x_kept = nc.dram_tensor("x_kept", (D, N), F32, kind="Internal").ap()

        G = dict(nc=nc, a=a, out=out, sem=sem, adj=adj, adj_words=adj_all[:, :].bitcast(F32), work=work, small=small,
                 ranges=ranges, ident=ident, ps=ps, T=T, p_rows=p_rows, h_rows=h_rows, edge_rows=edge_rows,
                 deg_row=deg_row, x_kept=x_kept)
        index = Words(work, 6400)
        keep = dict(src_f=index(P, NC + 1), dst_f=index(P, NC + 1), pos_f=index(P, NC), meta=index(P, 3 * NC))
        phase(prepare, keep)
        phase(adjacency, keep)
        phase(gin)
        phase(layernorm, save_degree=True)
        phase(edge_mlp)
        phase(layernorm)
        phase(genconv)
        phase(layernorm)
        phase(interaction)
        phase(layernorm)
        phase(store)


def load_range(nc, eng, ranges, row, w, steps, size):
    word = eng.value_load(ranges[0:1, bass.ds(w + NT * row, 1)], min_val=0, max_val=(NC << 8) + steps)
    return nc.s_assert_within(word >> 8, 0, NC), nc.s_assert_within(word & 255, 1, steps)


class Passed:

    def __init__(self, nc, eng, steps):
        self.nc, self.eng, self.top = nc, eng, NT * steps
        self.register = eng.alloc_register(f"steps_{nc.get_next_instruction_name()}")
        eng.reg_mov(self.register, 0)

    def now(self):
        return self.nc.s_assert_within(self.eng.snap(self.register, min_val=1, max_val=self.top), 1, self.top)

    def add(self, steps):
        self.eng.reg_add(self.register, self.register, steps)


def first_of_all(q):
    return isinstance(q, int) and q == 0


def prepare(G, keep):
    nc, a, sem, work, ranges, ident, ps = (G[k] for k in ("nc", "a", "sem", "work", "ranges", "ident", "ps"))
    src_f, dst_f, pos_f, meta = (keep[k] for k in ("src_f", "dst_f", "pos_f", "meta"))
    w_ = Words(work, 0, 6400)
    raw_s, raw_d, raw_r = w_(P, NC, I32), w_(P, NC, I32), w_(P, NC)
    rows_i, rows_f = w_(CR, CJ * P, I32), w_(CR, CJ * P)
    cmm, tile_lo, chunk_id, chunk_rev = w_(CR, 2 * CJ), w_(CR, NT), w_(CR, CJ), w_(CR, CJ)
    hit, hit2, keys, keym = w_(CR, NT * CJ), w_(CR, NT * CJ), w_(CR, 2 * NT), w_(CR, 2 * NT)
    table, tmp, fix, whole = w_(1, NR * NT), w_(1, NT), w_(1, NT), w_(1, NT, I32)
    first, steps_n = w_(1, NT), w_(1, NT)
    NB = NT + NT % 2
    bin_id, bins = w_(P, NB), w_(1, NB + 1)
    hi, fixb, whole_b = w_(P, NC), w_(P, NC), w_(P, NC, I32)
    far = Words(work, 8960)
    place, earlier, chosen, hot = ([far(P, n, dt) for _ in range(2)] for n, dt in (
        (NC + 1, F32), (NC + 1, F32), (NC, F32), (NC, BF16)))
    before, rest = w_(P, P, BF16), w_(P, P, BF16)

    s_load, s_const, s_v = sem("indices_loaded"), sem("constants_ready"), sem("vector_step")
    s_keys, s_keym, s_hot, s_rank = sem("keys_ready"), sem("keys_reduced"), sem("bin_hot"), sem("bin_ranked")
    s_chosen, s_placed, s_bin, s_scan = sem("chosen"), sem("placed"), sem("bin_end_kept"), sem("bin_scanned")
    s_p, s_early = sem("pool_step"), sem("earlier_edges_read_out")

    with nc.Block() as block:
        @block.sync
        def _(eng):
            eng.dma_start(raw_s, a["src_cols"][:, :]).then_inc(s_load, 16)
            eng.dma_start(raw_d, a["dst_cols"][:, :]).then_inc(s_load, 16)
            eng.dma_start(raw_r, a["weight_cols"][:, :]).then_inc(s_load, 16)
            eng.dma_start(rows_i, a["dst"].rearrange("(r c) -> r c", r=CR)).then_inc(s_load, 16)

        @block.gpsimd
        def _(eng):
            imprecise = dict(allow_small_or_imprecise_dtypes=True)
            step = Steps(eng, s_p)
            eng.iota(tile_lo, pattern=[[P, NT]], base=0, channel_multiplier=0, **imprecise).then_inc(s_const, 1)
            eng.iota(chunk_id, pattern=[[1, CJ]], base=1, channel_multiplier=CJ, **imprecise).then_inc(s_const, 1)
            eng.iota(bin_id, pattern=[[1, NB]], base=0, channel_multiplier=0, **imprecise).then_inc(s_const, 1)
            eng.memset(ident[:, :], 0.0)
            eng.memset(rest, 1.0).then_inc(s_const, 1)
            step(eng.memset(before, 1.0))
            eng.affine_select(out=ident[:, :], in_=ident[:, :], compare_op=ALU.not_equal, fill=1.0, base=0,
                              pattern=[[-1, 128]], channel_multiplier=1).then_inc(s_const, 1)
            eng.affine_select(out=before, in_=before, compare_op=ALU.is_gt, fill=0.0, base=0,
                              pattern=[[1, P]], channel_multiplier=-1)
            eng.affine_select(out=rest, in_=rest, compare_op=ALU.is_ge, fill=0.0, base=0,
                              pattern=[[-1, P]], channel_multiplier=1).then_inc(s_const, 1)
            eng.wait_ge(s_keys, 1)
            eng.partition_all_reduce(keym, keys, CR, bass.bass_isa.ReduceOp.max).then_inc(s_keym, 1)
            with eng.Fori(0, NB // 2) as i:
                for k in range(2):
                    h = i * 2 + k
                    eng.wait_ge(s_chosen, h + 1)
                    eng.wait_ge(s_placed, h + 2)
                    eng.nop(nofuse=True)
                    eng.tensor_tensor(pos_f, pos_f, chosen[k], ALU.add).then_inc(s_placed, 1)
                    eng.tensor_copy(bins[:, bass.ds(h + 1, 1)], place[k][0:1, NC:NC + 1]).then_inc(s_bin, 1)

        @block.scalar
        def _(eng):
            with eng.Fori(0, NB // 2) as i:
                for k in range(2):
                    eng.wait_ge(s_rank, i * 2 + k + 1)
                    eng.activation(earlier[k][:, 0:NC], ps[0:P, 2 * k, 0:NC], ACT.Copy).then_inc(s_early, 1)

        @block.tensor
        def _(eng):
            eng.wait_ge(s_const, 6)
            for s in (s_placed, s_bin):
                for _ in range(2):
                    eng.nop(nofuse=True).then_inc(s, 1)
            with eng.Fori(0, NB // 2) as i:
                for k in range(2):
                    eng.wait_ge(s_hot, i * 2 + k + 1)
                    eng.matmul(ps[0:P, 2 * k, 0:NC], before, hot[k], start=True, stop=True)
                    eng.matmul(ps[0:P, 2 * k + 1, 1:NC + 1], rest, hot[k], start=True, stop=True).then_inc(s_rank, 1)

        @block.vector
        def _(eng):
            step = Steps(eng, s_v)
            eng.wait_ge(s_load, 64)
            eng.wait_ge(s_const, 6)
            eng.tensor_copy(src_f[:, 0:NC], raw_s)
            eng.tensor_copy(dst_f[:, 0:NC], raw_d)
            eng.memset(src_f[:, NC:NC + 1], -1.0)
            eng.memset(dst_f[:, NC:NC + 1], -1.0)
            eng.memset(pos_f, 0.0)
            eng.memset(table, 0.0)
            eng.memset(bins[:, 0:1], 0.0)
            eng.memset(place[1][:, NC:NC + 1], 0.0)
            for k in range(2):
                eng.memset(earlier[k][:, NC:NC + 1], 0.0)
                eng.memset(ps[0:P, 2 * k + 1, 0:1], 0.0)
            m3 = meta.rearrange("p (c f) -> p c f", f=3)
            eng.tensor_copy(m3[:, :, 0], raw_r)
            eng.tensor_copy(m3[:, :, 1], raw_d)
            eng.tensor_copy(m3[:, :, 2], raw_s)
            eng.tensor_scalar(chunk_rev, chunk_id, -1.0, float(NC + 1), ALU.mult, ALU.add)
            step(eng.tensor_copy(rows_f, rows_i))

            r3 = rows_f.rearrange("p (j e) -> p j e", j=CJ)
            eng.tensor_reduce(cmm[:, 0:CJ], r3, axis=AX.X, op=ALU.min)
            step(eng.tensor_reduce(cmm[:, CJ:2 * CJ], r3, axis=AX.X, op=ALU.max))
            h3, g3 = (x.rearrange("p (w j) -> p w j", j=CJ) for x in (hit, hit2))
            lo3 = tile_lo.unsqueeze(2).to_broadcast([CR, NT, CJ])
            mn3, mx3 = (cmm[:, k * CJ:(k + 1) * CJ].unsqueeze(1).to_broadcast([CR, NT, CJ]) for k in (0, 1))
            id3, rv3 = (x.unsqueeze(1).to_broadcast([CR, NT, CJ]) for x in (chunk_id, chunk_rev))
            eng.tensor_tensor(h3, mx3, lo3, ALU.is_ge)
            step(eng.tensor_tensor(g3, mn3, lo3, ALU.subtract))
            step(eng.tensor_scalar(g3, g3, float(P), None, ALU.is_lt))
            step(eng.tensor_tensor(h3, h3, g3, ALU.mult))
            step(eng.tensor_tensor(g3, h3, rv3, ALU.mult))
            step(eng.tensor_reduce(keys[:, 0:NT], g3, axis=AX.X, op=ALU.max))
            step(eng.tensor_tensor(g3, h3, id3, ALU.mult))
            eng.tensor_reduce(keys[:, NT:2 * NT], g3, axis=AX.X, op=ALU.max).then_inc(s_keys, 1)

            step(eng.tensor_scalar(whole_b, src_f[:, 0:NC], 1.0 / P, None, ALU.mult))
            step(eng.tensor_copy(hi, whole_b))
            step(eng.tensor_scalar(fixb, hi, float(P), None, ALU.mult))
            step(eng.tensor_tensor(fixb, fixb, src_f[:, 0:NC], ALU.is_gt))
            step(eng.tensor_tensor(hi, hi, fixb, ALU.subtract))
            step(eng.tensor_scalar(fixb, hi, float(P), float(P), ALU.mult, ALU.add))
            step(eng.tensor_tensor(fixb, fixb, src_f[:, 0:NC], ALU.is_le))
            step(eng.tensor_tensor(hi, hi, fixb, ALU.add))

            def hots(k, h):
                eng.tensor_scalar(hot[k], hi, bin_id[:, bass.ds(h, 1)], None, ALU.is_equal).then_inc(s_hot, 1)

            def scan(k, h):
                eng.wait_ge(s_rank, h + 1)
                eng.wait_ge(s_early, h + 1)
                eng.wait_ge(s_bin, h + 1)
                if not first_of_all(h):
                    eng.wait_ge(s_chosen, h)
                eng.tensor_tensor_scan(place[k], ps[0:P, 2 * k + 1, 0:NC + 1], earlier[k],
                                       place[1 - k][:, NC:NC + 1], ALU.add, ALU.add).then_inc(s_scan, 1)
                eng.wait_ge(s_scan, h + 1)
                eng.wait_ge(s_placed, h + 1)
                eng.nop(nofuse=True)
                eng.scalar_tensor_tensor(chosen[k], hi, bin_id[:, bass.ds(h, 1)], place[k][:, 0:NC], ALU.is_equal,
                                         ALU.mult).then_inc(s_chosen, 1)

            hots(0, 0)
            hots(1, 1)
            scan(0, 0)
            with eng.Fori(1, NB // 2) as i:
                hots(0, i * 2)
                scan(1, nc.s_assert_within(i * 2 - 1, 1, NB - 1))
                hots(1, i * 2 + 1)
                scan(0, i * 2)
            scan(1, NB - 1)
            eng.wait_ge(s_placed, NB + 2)
            eng.wait_ge(s_bin, NB + 2)
            step(eng.tensor_scalar(whole_b, pos_f, 1.0 / P, None, ALU.mult))
            step(eng.tensor_copy(hi, whole_b))
            step(eng.tensor_scalar(fixb, hi, float(P), None, ALU.mult))
            step(eng.tensor_tensor(fixb, fixb, pos_f, ALU.is_gt))
            step(eng.tensor_tensor(hi, hi, fixb, ALU.subtract))
            step(eng.tensor_scalar(fixb, hi, float(P), float(P), ALU.mult, ALU.add))
            step(eng.tensor_tensor(fixb, fixb, pos_f, ALU.is_le))
            step(eng.tensor_tensor(hi, hi, fixb, ALU.add))
            step(eng.tensor_scalar(fixb, hi, -float(P), None, ALU.mult))
            step(eng.tensor_tensor(fixb, pos_f, fixb, ALU.add))
            step(eng.tensor_scalar(fixb, fixb, float(NC), None, ALU.mult))
            step(eng.tensor_tensor(pos_f, fixb, hi, ALU.add))

            def row(k):
                return table[:, k * NT:(k + 1) * NT]

            def ceil_div(out, x, size):
                step(eng.tensor_scalar(whole, x, 1.0 / size, None, ALU.mult))
                step(eng.tensor_copy(out, whole))
                step(eng.tensor_scalar(fix, out, float(size), None, ALU.mult))
                step(eng.tensor_tensor(fix, fix, x, ALU.is_lt))
                step(eng.tensor_tensor(out, out, fix, ALU.add))
                step(eng.tensor_scalar(fix, out, float(size), float(-size), ALU.mult, ALU.add))
                step(eng.tensor_tensor(fix, fix, x, ALU.is_ge))
                step(eng.tensor_tensor(out, out, fix, ALU.subtract))

            def steps_of(k, size, least):
                ceil_div(steps_n, tmp, size)
                step(eng.tensor_scalar(steps_n, steps_n, float(least), None, ALU.max))
                step(eng.tensor_scalar(row(k), steps_n, -float(size), float(-(-NC // size) * size), ALU.mult, ALU.add))
                step(eng.tensor_tensor(row(k), row(k), first, ALU.min))
                step(eng.tensor_scalar(row(k), row(k), 256.0, None, ALU.mult))
                step(eng.tensor_tensor(row(k), row(k), steps_n, ALU.add))

            eng.wait_ge(s_keym, 1)
            step(eng.tensor_scalar(first, keym[0:1, 0:NT], -1.0, float(NC), ALU.mult, ALU.add))
            step(eng.tensor_tensor(tmp, keym[0:1, NT:2 * NT], first, ALU.subtract))
            steps_of(R_ADJ, AS, 4)
            steps_of(R_DST, US, 2)
            step(eng.tensor_scalar(tmp, bins[0:1, 0:NT], float(1 - P), None, ALU.add))
            ceil_div(first, tmp, P)
            ceil_div(tmp, bins[0:1, 1:NT + 1], P)
            step(eng.tensor_tensor(tmp, tmp, first, ALU.subtract))
            steps_of(R_SRC, US, 3)
            eng.tensor_copy(ranges[:, :], table)


def adjacency(G, keep):
    nc, a, sem, work, ranges, ident, ps, adj = (G[k] for k in
                                                ("nc", "a", "sem", "work", "ranges", "ident", "ps", "adj"))
    small, edge_rows = G["small"], G["edge_rows"]
    src_f, dst_f, pos_f, meta = (keep[k] for k in ("src_f", "dst_f", "pos_f", "meta"))
    w_, far = Words(work, 0, 6400), Words(work, 8960)
    iota16 = w_(P, N, I16)
    src_hot = [w_(P, N, BF16), w_(P, N, BF16), far(P, N, BF16)]
    dst_hot = [far(P, P, BF16) for _ in range(AS)]
    counts = w_(P, N, F16)
    s_ = Words(small)
    zero16, ident16 = s_(P, P, BF16), s_(P, P, F16)
    pay, idx = s_(P, U * ROW), s_(P, U, I32)
    pay3 = pay.rearrange("p (k f) -> p k f", f=ROW)
    m3 = meta.rearrange("p (c f) -> p c f", f=3)
    SETS = ((0, 3), (3, U))

    s_iota, s_const = sem("iota_ready"), sem("constants_ready")
    s_hot, s_free = [sem("hots_ready") for _ in range(AS)], [sem("hots_free") for _ in range(AS)]
    s_tile, s_tr, s_store = sem("tile_counted"), sem("blocks_transposed"), sem("blocks_stored")
    s_cs, s_cv = sem("pieces_copied_by_scalar"), sem("pieces_copied_by_vector")
    s_attr, s_meta, s_sc = ([sem(f"{n}_{b}") for b in "ab"] for n in
                            ("attributes_in_rows", "row_and_place_ready", "rows_scattered"))
    on_scalar, on_vector = [0, 2, 4, 6], [1, 3, 5]
    edges = [0, 7, 13, 19, NT]
    groups = [range(edges[g], edges[g + 1]) for g in range(4)]
    MISC = ps[:, 7, :].bitcast(F16)

    with nc.Block() as block:
        @block.sync
        def _(eng):
            def fill(q):
                for b, (k0, k1) in enumerate(SETS):
                    if not first_of_all(q):
                        eng.wait_ge(s_sc[b], q * (16 * (k1 - k0)))
                    eng.dma_start(pay3[:, k0:k1, 0:FR], a["edge_attr_20"][bass.ds((q * U + k0) * P, (k1 - k0) * P), :]
                                  .rearrange("(k p) f -> p k f", p=P)).then_inc(s_attr[b], 16)

            fill(0)
            with eng.Fori(1, NC // U) as q:
                fill(q)
            for b, (k0, k1) in enumerate(SETS):
                eng.wait_ge(s_sc[b], (k1 - k0) * 16 * (NC // U))

        @block.gpsimd
        def _(eng):
            eng.iota(iota16, pattern=[[1, N]], base=0, channel_multiplier=0,
                     allow_small_or_imprecise_dtypes=True).then_inc(s_iota, 1)
            eng.memset(pay3[:, :, ONE_C:ONE_C + 1], 1.0)

            def scatter(q):
                for b, (k0, k1) in enumerate(SETS):
                    if not first_of_all(q):
                        eng.wait_ge(s_sc[b], q * (16 * (k1 - k0)))
                        eng.nop(nofuse=True)
                    c, n = q * U + k0, k1 - k0
                    eng.tensor_copy(pay3[:, k0:k1, RCUT_C:ROW], m3[:, bass.ds(c, n), :])
                    eng.tensor_copy(idx[:, k0:k1], pos_f[:, bass.ds(c, n)]).then_inc(s_meta[b], 1)
                    eng.wait_ge(s_meta[b], q + 1)
                    eng.wait_ge(s_attr[b], q * 16 + 16)
                    eng.nop(nofuse=True)
                    for k in range(k0, k1):
                        eng.indirect_dma_start(edge_rows[:, :],
                                               bass.IndirectOffsetOnAxis(ap=idx[:, k:k + 1], axis=0),
                                               pay[:, k * ROW:(k + 1) * ROW], None).then_inc(s_sc[b], 16)

            scatter(0)
            with eng.Fori(1, NC // U) as q:
                scatter(q)

        @block.scalar
        def _(eng):
            def store(w, g):
                n = len(groups[g])
                at = nc.s_assert_within(w * P - P, 0, N - P) if not isinstance(w, int) else w * P - P
                eng.wait_ge(s_tr, (w - 1) * 4 + g + 1)
                eng.activation(adj[:, groups[g][0]:groups[g][-1] + 1, bass.ds(at, P)],
                               MISC[0:P, 0:128 * n].rearrange("p (b q) -> p b q", q=128)[:, :, 0:P],
                               ACT.Copy).then_inc(s_store, 1)

            def tile(w):
                if not first_of_all(w):
                    for g in range(4):
                        store(w, g)
                for j in on_scalar:
                    _, c0, cw = PIECES[j]
                    eng.wait_ge(s_tile, w * NP + j + 1)
                    eng.activation(counts[:, c0:c0 + cw], ps[0:P, j, 0:cw], ACT.Copy).then_inc(s_cs, 1)

            tile(0)
            with eng.Fori(1, NT) as w:
                tile(nc.s_assert_within(w, 1, NT))
            for g in range(4):
                store(NT, g)

        @block.vector
        def _(eng):
            eng.memset(zero16, 0.0).then_inc(s_const, 1)
            eng.tensor_copy(ident16, ident[0:P, 0:P]).then_inc(s_const, 1)
            eng.wait_ge(s_iota, 1)

            def hots(w, c, t, k, opens=False):
                if not first_of_all(t):
                    eng.wait_ge(s_free[k], t)
                    if opens and k == AS - 1:
                        eng.wait_ge(s_tile, w * NP)
                eng.tensor_scalar(dst_hot[k], iota16[:, bass.ds(w * P, P)], dst_f[:, bass.ds(c + k, 1)],
                                  None, ALU.is_equal)
                eng.tensor_scalar(src_hot[k], iota16, src_f[:, bass.ds(c + k, 1)], None,
                                  ALU.is_equal).then_inc(s_hot[k], 1)

            def at(start, i):
                return nc.s_assert_within(start + i * AS, 0, NC + 1 - AS)

            def tile(w):
                start, count = load_range(nc, eng, ranges, R_ADJ, w, ASTEPS, AS)
                t = 0 if first_of_all(w) else passed.now()
                hots(w, at(start, 0), t, AS - 1, opens=True)
                with eng.Fori(1, count) as i:
                    for k in range(AS):
                        hots(w, at(start, i), t + i, k)
                passed.add(count)
                if not (isinstance(w, int) and w == NT - 1):
                    begin, _ = load_range(nc, eng, ranges, R_ADJ, w + 1, ASTEPS, AS)
                    t = passed.now()
                    for k in range(AS - 1):
                        hots(w + 1, at(begin, 0), t, k)
                for j in on_vector:
                    _, c0, cw = PIECES[j]
                    eng.wait_ge(s_tile, w * NP + j + 1)
                    eng.tensor_copy(counts[:, c0:c0 + cw], ps[0:P, j, 0:cw]).then_inc(s_cv, 1)

            passed = Passed(nc, eng, ASTEPS)
            begin, _ = load_range(nc, eng, ranges, R_ADJ, 0, ASTEPS, AS)
            for k in range(AS - 1):
                hots(0, at(begin, 0), 0, k)
            tile(0)
            with eng.Fori(1, NT - 1) as w:
                tile(w)
            tile(NT - 1)

        @block.tensor
        def _(eng):
            eng.wait_ge(s_const, 2)

            passed = Passed(nc, eng, ASTEPS)

            def step(t, opens=None, closes=None):
                for k in range(AS):
                    if closes is not None and k == AS - 1:
                        transposes(closes, 3)
                    eng.wait_ge(s_hot[k], t + 1)
                    for j, c0, cw in PIECES:
                        if opens is not None and k == 0 and not first_of_all(opens):
                            if j in on_scalar:
                                eng.wait_ge(s_cs, (opens - 1) * len(on_scalar) + on_scalar.index(j) + 1)
                            else:
                                eng.wait_ge(s_cv, (opens - 1) * len(on_vector) + on_vector.index(j) + 1)
                        ins = eng.matmul(ps[0:P, j, 0:cw], dst_hot[k], src_hot[k][:, c0:c0 + cw],
                                         start=opens is not None and k == 0,
                                         stop=closes is not None and k == AS - 1, skip_group_check=True)
                        if closes is not None and k == AS - 1:
                            ins.then_inc(s_tile, 1)
                    if closes is not None and k == AS - 1:
                        ins = eng.nop(nofuse=True)
                    ins.then_inc(s_free[k], 1)

            def transposes(w, g):
                if first_of_all(w):
                    return
                if g:
                    eng.wait_ge(s_store, (w - 1) * 4 + g)
                for b, s in enumerate(groups[g]):
                    ins = eng.transpose(MISC[0:P, b * 128:b * 128 + P], counts[:, s * P:s * P + P], ident16)
                ins.then_inc(s_tr, 1)

            def tile(w):
                _, count = load_range(nc, eng, ranges, R_ADJ, w, ASTEPS, AS)
                before = 0 if first_of_all(w) else passed.now()
                step(before, opens=w)
                transposes(w, 0)
                step(before + 1)
                transposes(w, 1)
                with eng.Fori(2, count - 1) as i:
                    step(before + i)
                transposes(w, 2)
                step(before + count - 1, closes=w)
                passed.add(count)

            tile(0)
            with eng.Fori(1, NT) as w:
                tile(nc.s_assert_within(w, 1, NT))
            eng.wait_ge(s_cs, NT * len(on_scalar))
            eng.wait_ge(s_cv, NT * len(on_vector))
            for g in range(4):
                transposes(NT, g)


def gin(G):
    nc, a, sem, small, ident, ps, adj, T = (G[k] for k in ("nc", "a", "sem", "small", "ident", "ps", "adj", "T"))
    s_ = Words(small)
    w1, w2, w3 = s_(D, GL * GH), s_(GH, GL * GH), s_(GH, GL * D)
    vec = s_(GH, 6 * GL)
    b3, eps = s_(D, GL), s_(D, GL)
    w1l, w1e, w2l, w3l = s_(D, GH), s_(D, GH), s_(GH, GH), s_(GH, D)
    vl, b3l = s_(GH, 6), s_(D, 1)
    merge = s_(3 * GH + 1, GH)
    stats, mv, sd, scale, shift, tmp = s_(GH, 6 * NP), s_(GH, 2), s_(GH, 1), s_(GH, 1), s_(GH, 1), s_(GH, 1)
    epsc = s_(GH, 1)
    YW = 3 * GH + 2
    y_ = Words(T[3])
    parts = y_(P, NT * YW, BF16).rearrange("p (s c) -> p s c", c=YW)
    rest = y_(P, NT * GH).rearrange("p (s c) -> p s c", c=GH)
    X, S, zb, h = T[1], T[2], T[3][0:GH, :], T[2][0:GH, :]
    halves = [(0, 0, 16), (1, 16, NT)]

    s_load, s_merge, s_v = sem("weights_loaded"), sem("merge_ready"), sem("vector_step")
    s_wl, s_xa, s_xv = sem("layer_weights_ready"), sem("x_by_scalar"), sem("x_by_vector")
    s_y, s_hi, s_parts = sem("y_ready"), sem("y_high_ready"), sem("y_parts_ready")
    s_sum, s_sa, s_sv = sem("piece_summed"), sem("sum_by_scalar"), sem("sum_by_vector")
    s_z = [sem("z1_ready"), sem("z2_ready")]
    s_zb, s_var, s_sd, s_aff, s_h = ([sem(f"{n}{i}") for i in (1, 2)] for n in
                                     ("biased", "variance", "deviation", "affine", "hidden"))
    s_x = sem("x_product_ready")

    with nc.Block() as block:
        @block.sync
        def _(eng):
            for dst, src in ((T[0], a["x"]), (w1, a["gin_w1"]), (w2, a["gin_w2"]), (w3, a["gin_w3"]),
                             (b3, a["gin_b3"]),
                             (eps, a["gin_eps"].rearrange("(o l) -> o l", o=1).to_broadcast([D, GL]))):
                eng.dma_start(dst, src).then_inc(s_load, 16)
            for i, name in enumerate(("b1", "g1", "bt1", "b2", "g2", "bt2")):
                eng.dma_start(vec[:, i * GL:(i + 1) * GL], a["gin_" + name]).then_inc(s_load, 16)

        @block.vector
        def _(eng):
            once = Steps(eng, s_v)
            eng.memset(epsc, EPS_BN)
            once(eng.memset(merge, 0.0))
            for i in range(3):
                ins = eng.tensor_copy(merge[i * GH:(i + 1) * GH, :], ident[i * GH:(i + 1) * GH, i * GH:(i + 1) * GH])
            ins.then_inc(s_merge, 1)
            eng.wait_ge(s_load, 192)
            once(eng.tensor_scalar(eps, eps, 1.0, None, ALU.add))
            for j in DVE_P:
                _, c0, cw = PIECES[j]
                eng.tensor_copy(X[:, c0:c0 + cw], T[0][:, c0:c0 + cw]).then_inc(s_xv, 1)
            first = once.n
            PER = 12
            with eng.Fori(0, GL) as l:
                step = Steps(eng, s_v, l * PER + first)
                eng.wait_ge(s_xa, (l + 1) * len(ACT_P))
                eng.wait_ge(s_xv, (l + 1) * len(DVE_P))
                eng.tensor_copy(w1l, w1[:, bass.ds(l * GH, GH)])
                eng.tensor_scalar(w1e, w1[:, bass.ds(l * GH, GH)], eps[:, bass.ds(l, 1)], None, ALU.mult)
                eng.tensor_copy(w2l, w2[:, bass.ds(l * GH, GH)])
                eng.tensor_copy(w3l, w3[:, bass.ds(l * D, D)])
                eng.tensor_copy(vl, vec.rearrange("p (i l) -> p i l", l=GL)[:, :, bass.ds(l, 1)].rearrange("p i o -> p (i o)"))
                eng.tensor_copy(b3l, b3[:, bass.ds(l, 1)])
                eng.memset(parts[:, :, 3 * GH:YW], 1.0).then_inc(s_wl, 1)
                for b, s0, s1 in halves:
                    y = ps[0:P, b, 0:(s1 - s0) * GH].rearrange("p (s c) -> p s c", c=GH)
                    eng.wait_ge(s_hi, l * 2 + b + 1)
                    step(eng.tensor_tensor(rest[:, s0:s1, :], y, parts[:, s0:s1, 0:GH], ALU.subtract))
                    step(eng.tensor_copy(parts[:, s0:s1, GH:2 * GH], rest[:, s0:s1, :]))
                    eng.tensor_tensor(parts[:, s0:s1, 2 * GH:3 * GH], rest[:, s0:s1, :],
                                      parts[:, s0:s1, GH:2 * GH], ALU.subtract).then_inc(s_parts, 1)
                for i, j in enumerate(DVE_P):
                    _, c0, cw = PIECES[j]
                    eng.wait_ge(s_sum, l * NP + j + 1)
                    eng.tensor_copy(S[0:YW - 1, c0:c0 + cw], ps[0:YW - 1, j, 0:cw]).then_inc(s_sv, 1)
                for n in range(2):
                    for j, c0, cw in PIECES:
                        eng.wait_ge(s_zb[n], l * NP + j + 1)
                        ins = eng.bn_stats(stats[:, 6 * j:6 * j + 6], zb[:, c0:c0 + cw])
                    step(ins)
                    eng.nop(nofuse=True)
                    eng.bn_aggr(mv, stats.rearrange("p (j f) -> p j f", f=6)).then_inc(s_var[n], 1)
                    eng.wait_ge(s_sd[n], l + 1)
                    step(eng.reciprocal(scale, sd))
                    step(eng.tensor_tensor(scale, scale, vl[:, 3 * n + 1:3 * n + 2], ALU.mult))
                    step(eng.tensor_tensor(tmp, mv[:, 0:1], scale, ALU.mult))
                    eng.tensor_tensor(shift, vl[:, 3 * n + 2:3 * n + 3], tmp, ALU.subtract).then_inc(s_aff[n], 1)
                for j in DVE_P:
                    _, c0, cw = PIECES[j]
                    eng.wait_ge(s_x, l * NP + j + 1)
                    eng.tensor_scalar(X[:, c0:c0 + cw], ps[:, j, 0:cw], b3l, None, ALU.add).then_inc(s_xv, 1)
                assert step.n == PER, step.n

        @block.scalar
        def _(eng):
            eng.wait_ge(s_load, 192)
            for j in ACT_P:
                _, c0, cw = PIECES[j]
                eng.activation(X[:, c0:c0 + cw], T[0][:, c0:c0 + cw], ACT.Copy).then_inc(s_xa, 1)
            with eng.Fori(0, GL) as l:
                for b, s0, s1 in halves:
                    eng.wait_ge(s_y, l * 2 + b + 1)
                    eng.activation(parts[:, s0:s1, 0:GH],
                                   ps[0:P, b, 0:(s1 - s0) * GH].rearrange("p (s c) -> p s c", c=GH),
                                   ACT.Copy).then_inc(s_hi, 1)
                for j in ACT_P:
                    _, c0, cw = PIECES[j]
                    eng.wait_ge(s_sum, l * NP + j + 1)
                    eng.activation(S[0:YW - 1, c0:c0 + cw], ps[0:YW - 1, j, 0:cw], ACT.Copy).then_inc(s_sa, 1)
                for n in range(2):
                    for j, c0, cw in PIECES:
                        eng.wait_ge(s_z[n], l * NP + j + 1)
                        eng.activation(zb[:, c0:c0 + cw], ps[0:GH, j, 0:cw], ACT.Identity,
                                       bias=vl[:, 3 * n:3 * n + 1]).then_inc(s_zb[n], 1)
                    eng.wait_ge(s_var[n], l + 1)
                    eng.activation(sd, mv[:, 1:2], ACT.Sqrt, bias=epsc).then_inc(s_sd[n], 1)
                    eng.wait_ge(s_aff[n], l + 1)
                    for j, c0, cw in PIECES:
                        eng.activation(h[:, c0:c0 + cw], zb[:, c0:c0 + cw], ACT.Relu, bias=shift,
                                       scale=scale).then_inc(s_h[n], 1)
                for j in ACT_P:
                    _, c0, cw = PIECES[j]
                    eng.wait_ge(s_x, l * NP + j + 1)
                    eng.activation(X[:, c0:c0 + cw], ps[:, j, 0:cw], ACT.Identity, bias=b3l).then_inc(s_xa, 1)

        @block.tensor
        def _(eng):
            eng.wait_ge(s_merge, 1)
            with eng.Fori(0, GL) as l:
                eng.wait_ge(s_wl, l + 1)
                eng.wait_ge(s_xa, (l + 1) * len(ACT_P))
                eng.wait_ge(s_xv, (l + 1) * len(DVE_P))
                for b, s0, s1 in halves:
                    for s in range(s0, s1):
                        ins = eng.matmul(ps[0:P, b, (s - s0) * GH:(s - s0 + 1) * GH], X[:, s * P:(s + 1) * P], w1l,
                                         start=True, stop=True)
                    ins.then_inc(s_y, 1)
                eng.wait_ge(s_parts, l * 2 + 2)

                def tile(s, start, last):
                    for j, c0, cw in PIECES:
                        if isinstance(s, int):
                            w, m = parts[:, s, 0:YW - 1], adj[:, s, c0:c0 + cw]
                        else:
                            w = parts[:, bass.ds(s, 1), 0:YW - 1].rearrange("p o c -> p (o c)")
                            m = adj[:, bass.ds(s, 1), c0:c0 + cw].rearrange("p o c -> p (o c)")
                        ins = eng.matmul(ps[0:YW - 1, j, 0:cw], w, m, start=start, stop=last, skip_group_check=True)
                        if last:
                            ins.then_inc(s_sum, 1)

                tile(0, True, False)
                with eng.Fori(1, NT - 1) as s:
                    tile(s, False, False)
                tile(NT - 1, False, True)
                for j, c0, cw in PIECES:
                    if j in ACT_P:
                        eng.wait_ge(s_sa, l * len(ACT_P) + ACT_P.index(j) + 1)
                    else:
                        eng.wait_ge(s_sv, l * len(DVE_P) + DVE_P.index(j) + 1)
                    eng.matmul(ps[0:GH, j, 0:cw], merge, S[0:YW - 1, c0:c0 + cw], start=True, stop=False)
                    eng.matmul(ps[0:GH, j, 0:cw], w1e, X[:, c0:c0 + cw], start=False, stop=True).then_inc(s_z[0], 1)
                for j, c0, cw in PIECES:
                    eng.wait_ge(s_h[0], l * NP + j + 1)
                    eng.nop(nofuse=True)
                    eng.matmul(ps[0:GH, j, 0:cw], w2l, h[:, c0:c0 + cw], start=True, stop=True).then_inc(s_z[1], 1)
                for j, c0, cw in PIECES:
                    eng.wait_ge(s_h[1], l * NP + j + 1)
                    eng.matmul(ps[:, j, 0:cw], w3l, h[:, c0:c0 + cw], start=True, stop=True).then_inc(s_x, 1)


def layernorm(G, save_degree=False):
    nc, sem, small, ident, ps, T, deg_row = (G[k] for k in ("nc", "sem", "small", "ident", "ps", "T", "deg_row"))
    s_ = Words(small)
    ones, epsc, inv = s_(D, D), s_(D, 1), s_(P, NT)
    groups = [(g, range(4 * g, min(NT, 4 * g + 4))) for g in range((NT + 3) // 4)]
    z, d, sq = T[1], T[2], T[3]
    s_const, s_z, s_mean, s_d, s_sq = (sem(n) for n in ("constants_ready", "residual_added", "mean_ready",
                                                        "centred", "squared"))
    s_var, s_sd, s_inv, s_spread, s_deg = (sem(n) for n in ("variance_ready", "deviation_ready", "inverted",
                                                            "spread_over_channels", "degree_saved"))
    with nc.Block() as block:
        @block.sync
        def _(eng):
            if save_degree:
                eng.dma_start(deg_row[:, :], T[2][3 * GH:3 * GH + 1, :]).then_inc(s_deg, 16)
                eng.wait_ge(s_deg, 16)

        @block.vector
        def _(eng):
            eng.memset(epsc, EPS_LN)
            eng.memset(ones, 1.0 / D).then_inc(s_const, 1)
            for j, c0, cw in PIECES:
                eng.tensor_tensor(z[:, c0:c0 + cw], T[0][:, c0:c0 + cw], z[:, c0:c0 + cw], ALU.add).then_inc(s_z, 1)
            if save_degree:
                eng.wait_ge(s_deg, 16)
            for j, c0, cw in PIECES:
                eng.wait_ge(s_mean, j + 1)
                eng.tensor_tensor(d[:, c0:c0 + cw], z[:, c0:c0 + cw], ps[:, j, 0:cw], ALU.subtract).then_inc(s_d, 1)
            eng.wait_ge(s_sd, 1)
            eng.reciprocal(inv, inv).then_inc(s_inv, 1)
            for g, tiles in groups:
                c0, c1 = tiles[0] * P, (tiles[-1] + 1) * P
                eng.wait_ge(s_spread, g + 1)
                eng.tensor_tensor(T[0][:, c0:c1], d[:, c0:c1], ps[:, g, 0:c1 - c0], ALU.mult)

        @block.tensor
        def _(eng):
            eng.wait_ge(s_const, 1)
            for j, c0, cw in PIECES:
                eng.wait_ge(s_z, j + 1)
                eng.matmul(ps[:, j, 0:cw], ones, z[:, c0:c0 + cw], start=True, stop=True).then_inc(s_mean, 1)
            for s in range(NT):
                if s == 0 or (s * P + P - 1) // PW != (s * P - 1) // PW:
                    eng.wait_ge(s_sq, (s * P + P - 1) // PW + 1)
                ins = eng.matmul(ps[0:P, 7, s:s + 1], sq[:, s * P:(s + 1) * P], ones[:, 0:1], start=True, stop=True)
            ins.then_inc(s_var, 1)
            eng.wait_ge(s_inv, 1)
            for g, tiles in groups:
                for i, s in enumerate(tiles):
                    ins = eng.matmul(ps[:, g, i * P:(i + 1) * P], inv[:, s:s + 1].to_broadcast([P, D]),
                                     ident[0:P, 0:P], start=True, stop=True)
                ins.then_inc(s_spread, 1)

        @block.scalar
        def _(eng):
            for j, c0, cw in PIECES:
                eng.wait_ge(s_d, j + 1)
                eng.activation(sq[:, c0:c0 + cw], d[:, c0:c0 + cw], ACT.Square).then_inc(s_sq, 1)
            eng.wait_ge(s_const, 1)
            eng.wait_ge(s_var, 1)
            eng.activation(inv, ps[0:P, 7, 0:NT], ACT.Sqrt, bias=epsc[0:P, :]).then_inc(s_sd, 1)


def walk(nc, eng, ranges, row, body, end):
    def at(start, u):
        return nc.s_assert_within(start + u * US, 0, NC + 1 - US)

    passed = Passed(nc, eng, STEPS)
    start, count = load_range(nc, eng, ranges, row, 0, STEPS, US)
    body(0, at(start, 0), 0, True)
    with eng.Fori(1, count) as u:
        body(0, at(start, u), nc.s_assert_within(u, 1, STEPS), False)
    passed.add(count)
    with eng.Fori(1, NT) as w:
        start, count = load_range(nc, eng, ranges, row, w, STEPS, US)
        before = passed.now()
        body(w, at(start, 0), before, True)
        with eng.Fori(1, count) as u:
            body(w, at(start, u), before + u, False)
        passed.add(count)
    end(passed.now())


def edge_mlp(G):
    nc, a, sem, work, small, ranges, ident, ps, T, p_rows, deg_row, x_kept = (
        G[k] for k in ("nc", "a", "sem", "work", "small", "ranges", "ident", "ps", "T", "p_rows", "deg_row", "x_kept"))
    x, R = T[0], T[2]
    gathered = [T[0][0:P, h * UH * D:(h + 1) * UH * D] for h in range(2)]
    HALVES = range(2)
    q_rows = work[0:P, 4 * N - NT * D:4 * N].rearrange("p (s c) -> p s c", c=D)
    r_ = Words(work, N, 2 * N)
    src_i, dst_f = r_(P, NC + 1, I32), r_(P, NC + 1)
    row_ring = r_(P, US * D)
    rows = [row_ring[:, h * UH * D:(h + 1) * UH * D] for h in HALVES]
    stage = [T[2][0:P, g * 512:(g + 1) * 512] for g in range(5)] + [row_ring[:, 0:512], row_ring[:, 512:640]]
    hots = r_(P, US * P)
    hot = [hots[:, h * UH * P:(h + 1) * UH * P] for h in HALVES]
    dst_i = hots[:, 0:NC].bitcast(I32)
    setup = Words(small)
    wa, wb, b1 = setup(D, D), setup(D, D), setup(P, D)
    hot16 = [r_(P, UH * P, BF16) for _ in HALVES]
    q_part = [r_(P, D, BF16) for _ in range(3)]
    tile_lo, iota = r_(P, NT), r_(P, P)
    idx = [r_(P, UH, I32) for _ in HALVES]
    s_ = Words(small)
    attr = [s_(FE, UH * P) for _ in HALVES]
    zero = small[FE:FE + 1, UH * P:UH * P + D].bitcast(BF16)[:, 0:D]
    w1e = s_(FE, D)
    hot_t = [s_(P, UH * P, BF16) for _ in HALVES]
    groups = [(g, range(4 * g, min(NT, 4 * g + 4))) for g in range((NT + 3) // 4)]

    s_load, s_const, s_dst = sem("weights_loaded"), sem("constants_ready"), sem("dst_ready")
    s_rows, s_p, s_q, s_prow = sem("rows_ready"), sem("p_read_out"), sem("q_read_out"), sem("p_rows_written")
    s_idx, s_g, s_attr, s_h16, s_tr, s_ht, s_h32, s_prod, s_add, s_relu, s_tot = (
        [sem(f"{n}_{h}") for h in "ab"] for n in (
            "index_ready", "rows_gathered", "attributes", "hots_ready", "hots_transposed", "hots_t_ready",
            "hots_widened", "products_ready", "preactivation", "relu_ready", "half_summed"))
    s_kept, s_split, s_parts = sem("x_kept"), sem("split_step"), sem("q_parts_ready")
    s_tile, s_ev = sem("tile_summed"), sem("tile_read_out")
    SUM, PROD = ps[:, 7, 0:P], [ps[0:P, h, 0:UH * D] for h in HALVES]
    TRANS = [ps[:, 2 + h, :].bitcast(BF16)[0:P, 0:UH * 128].rearrange("p (k e) -> p k e", e=128)[:, :, 0:P]
             for h in HALVES]
    ident16 = ident[:, :].bitcast(BF16).rearrange("p (c t) -> p c t", t=2)[0:P, 0:P, 1]

    with nc.Block() as block:
        @block.sync
        def _(eng):
            for dst, src in ((src_i[:, 0:NC], a["src_cols"]), (dst_i, a["dst_cols"]), (wa, a["mlp_w1a"]),
                             (wb, a["mlp_w1b"]),
                             (b1, a["mlp_b1"].rearrange("(o c) -> o c", o=1).to_broadcast([P, D]))):
                eng.dma_start(dst, src).then_inc(s_load, 16)
            eng.dma_start(x_kept[:, :], x).then_inc(s_kept, 16)
            p_view = p_rows.rearrange("(s p) c -> p s c", p=P)
            for g, tiles in groups:
                eng.wait_ge(s_p, g + 1)
                eng.dma_start(p_view[:, tiles[0]:tiles[-1] + 1, :],
                              stage[g].rearrange("p (s c) -> p s c", c=D)).then_inc(s_prow, 16)
            eng.wait_ge(s_rows, len(groups))
            eng.wait_ge(s_q, len(groups))
            eng.dma_start(w1e, a["mlp_w1e"]).then_inc(s_load, 16)

            def body(w, c, q, opens):
                for h in HALVES:
                    if not first_of_all(q):
                        eng.wait_ge(s_prod[h], q)
                    eng.dma_start(attr[h], a["edge_attr_64"][:, bass.ds((c + h * UH) * P, UH * P)]).then_inc(s_attr[h], 16)

            walk(nc, eng, ranges, R_DST, body, lambda q: None)

        @block.gpsimd
        def _(eng):
            imprecise = dict(allow_small_or_imprecise_dtypes=True)
            eng.iota(tile_lo, pattern=[[P, NT]], base=0, channel_multiplier=0, **imprecise).then_inc(s_const, 1)
            eng.iota(iota, pattern=[[1, P]], base=0, channel_multiplier=0, **imprecise).then_inc(s_const, 1)
            eng.memset(src_i[:, NC:NC + 1], 0)
            eng.memset(dst_f[:, NC:NC + 1], -1.0).then_inc(s_const, 1)
            eng.wait_ge(s_load, 96)
            eng.wait_ge(s_prow, 16 * len(groups))
            eng.wait_ge(s_kept, 16)

            def body(w, c, q, opens):
                for h in HALVES:
                    if not first_of_all(q):
                        eng.wait_ge(s_add[h], q)
                        eng.nop(nofuse=True)
                    eng.tensor_copy(idx[h], src_i[:, bass.ds(c + h * UH, UH)]).then_inc(s_idx[h], 1)
                    eng.wait_ge(s_idx[h], q + 1)
                    eng.nop(nofuse=True)
                    for k in range(UH):
                        eng.indirect_dma_start(gathered[h][:, k * D:(k + 1) * D], None, p_rows[:, :],
                                               bass.IndirectOffsetOnAxis(ap=idx[h][:, k:k + 1], axis=0)
                                               ).then_inc(s_g[h], 16)

            walk(nc, eng, ranges, R_DST, body, lambda q: None)

        @block.vector
        def _(eng):
            eng.wait_ge(s_load, 80)
            eng.tensor_copy(dst_f[:, 0:NC], dst_i).then_inc(s_dst, 1)
            for g, tiles in groups:
                n = len(tiles)
                eng.wait_ge(s_rows, g + 1)
                eng.tensor_tensor(q_rows[:, tiles[0]:tiles[-1] + 1, :],
                                  ps[0:P, 4 + g % 4, 0:n * D].rearrange("p (s c) -> p s c", c=D),
                                  b1.unsqueeze(1).to_broadcast([P, n, D]), ALU.add).then_inc(s_q, 1)
            eng.wait_ge(s_dst, 1)
            eng.wait_ge(s_q, len(groups))
            eng.memset(zero, 0.0).then_inc(s_const, 1)
            eng.wait_ge(s_const, 4)

            def hots_of(w, c, q, h):
                if not first_of_all(q):
                    eng.wait_ge(s_tr[h], q)
                    eng.wait_ge(s_h32[h], q)
                for k in range(UH):
                    ins = eng.tensor_scalar(hot16[h][:, k * P:(k + 1) * P], iota, tile_lo[:, bass.ds(w, 1)],
                                            dst_f[:, bass.ds(c + h * UH + k, 1)], ALU.add, ALU.is_equal)
                ins.then_inc(s_h16[h], 1)

            def add(n, h):
                eng.wait_ge(s_prod[h], n)
                eng.wait_ge(s_g[h], n * (16 * UH))
                if h == 1 or not isinstance(n, int):
                    eng.wait_ge(s_tot[h], n - 1 + h)
                eng.tensor_tensor(rows[h], PROD[h], gathered[h], ALU.add).then_inc(s_add[h], 1)

            def split(w, q):
                rest = q_rows[:, bass.ds(w, 1), :].rearrange("p o c -> p (o c)")
                if not first_of_all(q):
                    for h in HALVES:
                        eng.wait_ge(s_prod[h], q)
                    eng.nop(nofuse=True)
                for k in range(2):
                    eng.tensor_copy(q_part[k], rest).then_inc(s_split, 1)
                    eng.wait_ge(s_split, w * 4 + 2 * k + 1)
                    eng.tensor_tensor(rest, rest, q_part[k], ALU.subtract).then_inc(s_split, 1)
                    eng.wait_ge(s_split, w * 4 + 2 * k + 2)
                    eng.nop(nofuse=True)
                eng.tensor_copy(q_part[2], rest).then_inc(s_parts, 1)

            def transposed(q, h):
                eng.wait_ge(s_tr[h], q + 1)
                if not first_of_all(q):
                    eng.wait_ge(s_prod[h], q)
                eng.tensor_copy(hot_t[h].rearrange("p (k e) -> p k e", e=P), TRANS[h]).then_inc(s_ht[h], 1)

            def body(w, c, q, opens):
                for h in HALVES:
                    hots_of(w, c, q, h)
                if not first_of_all(q):
                    add(q, 1)
                if opens:
                    split(w, q)
                for h in HALVES:
                    transposed(q, h)
                add(q + 1, 0)

            walk(nc, eng, ranges, R_DST, body, lambda q: add(q, 1))

        @block.scalar
        def _(eng):
            for g, tiles in groups:
                eng.wait_ge(s_rows, g + 1)
                eng.activation(stage[g], ps[0:P, g % 4, 0:len(tiles) * D], ACT.Copy).then_inc(s_p, 1)
            eng.wait_ge(s_dst, 1)

            def relu(n, h):
                eng.wait_ge(s_add[h], n)
                eng.activation(rows[h], rows[h], ACT.Relu).then_inc(s_relu[h], 1)

            def widen(q, h):
                eng.wait_ge(s_h16[h], q + 1)
                if h == 1 or not first_of_all(q):
                    eng.wait_ge(s_tot[h], q + h)
                eng.activation(hot[h], hot16[h], ACT.Copy).then_inc(s_h32[h], 1)

            def evacuate(w):
                eng.wait_ge(s_tile, w)
                at = nc.s_assert_within(w * P - P, 0, N - P) if not isinstance(w, int) else w * P - P
                eng.activation(R[:, bass.ds(at, P)], SUM, ACT.Copy).then_inc(s_ev, 1)

            def body(w, c, q, opens):
                if not first_of_all(q):
                    relu(q, 1)
                widen(q, 0)
                if opens and not first_of_all(q):
                    evacuate(w)
                widen(q, 1)
                relu(q + 1, 0)

            walk(nc, eng, ranges, R_DST, body, lambda q: relu(q, 1))
            evacuate(NT)

        @block.tensor
        def _(eng):
            eng.wait_ge(s_load, 80)
            for g, tiles in groups:
                if g >= 4:
                    eng.wait_ge(s_p, g - 3)
                    eng.wait_ge(s_q, g - 3)
                for b, w in ((g % 4, wa), (4 + g % 4, wb)):
                    for i, s in enumerate(tiles):
                        ins = eng.matmul(ps[0:P, b, i * D:(i + 1) * D], x[:, s * P:(s + 1) * P], w,
                                         start=True, stop=True)
                ins.then_inc(s_rows, 1)
            eng.wait_ge(s_p, len(groups))
            eng.wait_ge(s_q, len(groups))
            eng.wait_ge(s_const, 4)
            eng.wait_ge(s_load, 96)
            eng.nop(nofuse=True).then_inc(s_tot[1], 1)

            def boundary(start):
                n = P if start else 1
                return eng.matmul(SUM[:, 0:n], zero, zero[:, 0:n], start=start, stop=not start, skip_group_check=True)

            def products(q, h):
                eng.wait_ge(s_ht[h], q + 1)
                if not first_of_all(q):
                    eng.wait_ge(s_add[h], q)
                eng.wait_ge(s_attr[h], q * 16 + 16)
                for k in range(UH):
                    out = PROD[h][:, k * D:(k + 1) * D]
                    for part in q_part:
                        eng.matmul(out, hot_t[h][:, k * P:(k + 1) * P], part, start=part is q_part[0], stop=False)
                    ins = eng.matmul(out, attr[h][:, k * P:(k + 1) * P], w1e, start=False, stop=True)
                ins.then_inc(s_prod[h], 1)

            def total(n, h):
                eng.wait_ge(s_h32[h], n)
                eng.wait_ge(s_relu[h], n)
                for k in range(UH):
                    ins = eng.matmul(SUM, rows[h][:, k * D:(k + 1) * D], hot[h][:, k * P:(k + 1) * P],
                                     start=False, stop=False, skip_group_check=True)
                ins.then_inc(s_tot[h], 1)

            def body(w, c, q, opens):
                for h in HALVES:
                    eng.wait_ge(s_h16[h], q + 1)
                    if not first_of_all(q):
                        eng.wait_ge(s_ht[h], q)
                    for k in range(UH):
                        ins = eng.transpose(TRANS[h][:, k, :], hot16[h][:, k * P:(k + 1) * P], ident16)
                    ins.then_inc(s_tr[h], 1)
                if not first_of_all(q):
                    total(q, 1)
                    if opens:
                        boundary(False).then_inc(s_tile, 1)
                if opens:
                    eng.wait_ge(s_parts, w + 1)
                products(q, 0)
                products(q, 1)
                if opens:
                    if not first_of_all(q):
                        eng.wait_ge(s_ev, w)
                        eng.nop(nofuse=True)
                    boundary(True)
                total(q + 1, 0)

            def end(q):
                total(q, 1)
                boundary(False).then_inc(s_tile, 1)

            walk(nc, eng, ranges, R_DST, body, end)

    n_ = Words(small)
    w2, u1a, u1b, u2 = (n_(D, D) for _ in range(4))
    b2, c1, c2 = n_(1, D), n_(D, 1), n_(D, 1)
    deg, agg, out = T[3][0:1, :], T[1], T[1]
    s_load, s_back, s_m, s_mo = (sem(n) for n in ("weights_loaded", "x_back", "messages_ready", "messages_read_out"))
    s_u, s_uo, s_o = sem("hidden_ready"), sem("hidden_read_out"), sem("update_ready")
    with nc.Block() as block:
        @block.sync
        def _(eng):
            for dst, src in ((w2, a["mlp_w2"]), (u1a, a["mlp_u1a"]), (u1b, a["mlp_u1b"]), (u2, a["mlp_u2"]),
                             (b2, a["mlp_b2"].rearrange("(o c) -> o c", o=1)), (deg, deg_row),
                             (c1, a["mlp_c1"].rearrange("(c o) -> c o", o=1)),
                             (c2, a["mlp_c2"].rearrange("(c o) -> c o", o=1))):
                eng.dma_start(dst, src).then_inc(s_load, 16)
            eng.dma_start(x, x_kept[:, :]).then_inc(s_back, 16)

        @block.tensor
        def _(eng):
            eng.wait_ge(s_load, 128)
            for j, c0, cw in PIECES:
                eng.matmul(ps[:, j, 0:cw], w2, R[:, c0:c0 + cw], start=True, stop=False)
                eng.matmul(ps[:, j, 0:cw], b2, deg[:, c0:c0 + cw], start=False, stop=True).then_inc(s_m, 1)
            eng.wait_ge(s_back, 16)
            for j, c0, cw in PIECES:
                eng.wait_ge(s_mo, j + 1)
                eng.matmul(ps[:, j, 0:cw], u1b, agg[:, c0:c0 + cw], start=True, stop=False)
                eng.matmul(ps[:, j, 0:cw], u1a, x[:, c0:c0 + cw], start=False, stop=True).then_inc(s_u, 1)
            for j, c0, cw in PIECES:
                eng.wait_ge(s_uo, j + 1)
                eng.matmul(ps[:, j, 0:cw], u2, R[:, c0:c0 + cw], start=True, stop=True).then_inc(s_o, 1)

        @block.vector
        def _(eng):
            for j, c0, cw in PIECES:
                eng.wait_ge(s_m, j + 1)
                eng.tensor_copy(agg[:, c0:c0 + cw], ps[:, j, 0:cw]).then_inc(s_mo, 1)
            for j, c0, cw in PIECES:
                eng.wait_ge(s_o, j + 1)
                eng.tensor_scalar(out[:, c0:c0 + cw], ps[:, j, 0:cw], c2, None, ALU.add)

        @block.scalar
        def _(eng):
            for j, c0, cw in PIECES:
                eng.wait_ge(s_u, j + 1)
                eng.activation(R[:, c0:c0 + cw], ps[:, j, 0:cw], ACT.Relu, bias=c1).then_inc(s_uo, 1)


def genconv(G):
    nc, a, sem, small, ranges, ident, ps, adj, T, x_kept = (
        G[k] for k in ("nc", "a", "sem", "small", "ranges", "ident", "ps", "adj", "T", "x_kept"))
    acc, x, z, den = T
    h1 = [T[2], T[3]]
    w2 = T[0][:, 0:2 * D].rearrange("p (k c) -> p k c", k=2)
    s_ = Words(small)
    parts = [s_(P, 3 * D, BF16) for _ in range(2)]
    e = [s_(D, P) for _ in range(2)]
    m, rest = s_(D, P), s_(P, D)
    w1 = s_(D, AH)
    vec = s_(D, 4)
    t_all = s_(D, AL)
    logits, eps_t = s_(D, 2), s_(D, 1)
    ext, lim, spread, top = s_(D, 2), s_(D, 2), s_(D, 1), s_(D, 1)
    shift_s, t_l, before_f, steps_f = s_(D, 1), s_(D, 1), s_(1, 1), s_(1, 1)
    stats, mv, sd, scale, shift, tmp, epsc = (s_(D, n) for n in (6 * NP, 2, 1, 2, 2, 1, 1))
    greatest, shift_z = s_(D, NP), s_(D, 1)
    MISC = ps[0:P, 7, 0:D]

    s_saved, s_t, s_w1, s_w2 = sem("x_saved"), sem("t_loaded"), sem("w1_loaded"), sem("w2_loaded")
    s_v, s_spread, s_top, s_band = sem("vector_step"), sem("spread_ready"), sem("spread_reduced"), sem("bands_ready")
    s_z, s_e, s_m, s_f = sem("exponents_ready"), sem("exp_ready"), sem("message_ready"), sem("weighted_ready")
    s_tr, s_hi, s_rest, s_mid, s_parts = (sem(n) for n in ("transposed", "high_ready", "rest_ready", "middle_ready",
                                                           "parts_ready"))
    s_used, s_sum, s_dena, s_denv = (sem(n) for n in ("parts_used", "piece_summed", "den_by_scalar", "den_by_vector"))
    s_inv, s_num, s_agg, s_h = sem("den_step"), sem("sums_combined"), sem("aggregate_step"), sem("node_input_ready")
    s_h1, s_h1o, s_var, s_sd, s_aff, s_r1 = (sem(n) for n in ("hidden_product", "hidden_read_out", "variance",
                                                              "deviation", "affine", "hidden_ready"))
    s_acc, s_copied = sem("aggregate_cleared"), sem("x_copied")
    s_x, s_xa, s_xv, s_fin, s_back = (sem(n) for n in ("x_product", "x_by_scalar", "x_by_vector", "weights_free",
                                                       "x_restored"))

    def bands(eng, l):
        return [eng.value_load(ranges[0:1, bass.ds(l * 2 + NT * R_BAND + k, 1)], min_val=lo, max_val=1 << 20)
                for k, lo in ((0, 1), (1, 0))]

    def tiles(eng, body):
        body(0, 0, True, False)
        with eng.Fori(0, 11) as i:
            body(i * 2 + 1, 1, False, False)
            body(i * 2 + 2, 0, False, False)
        body(23, 1, False, False)
        body(24, 0, False, True)

    def tile_cols(table, s):
        return table[:, s * P:(s + 1) * P] if isinstance(s, int) else table[:, bass.ds(s * P, P)]

    with nc.Block() as block:
        @block.sync
        def _(eng):
            eng.dma_start(t_all, a["agg_t"].rearrange("(o l) -> o l", o=1).to_broadcast([D, AL])).then_inc(s_t, 16)
            eng.dma_start(x_kept[:, :], T[0]).then_inc(s_saved, 16)
            with eng.Fori(0, AL) as l:
                eng.wait_ge(s_fin, l + 1)
                eng.dma_start(w1, a["agg_w1"][:, bass.ds(l * AH, AH)]).then_inc(s_w1, 16)
                eng.dma_start(vec, a["agg_vec"][:, bass.ds(l * 4, 4)]).then_inc(s_w1, 16)
                eng.wait_ge(s_h, (l + 1) * NP)
                eng.dma_start(w2, a["agg_w2"][:, bass.ds(l * 2, 2), :]).then_inc(s_w2, 16)
            eng.wait_ge(s_fin, AL + 1)
            eng.dma_start(T[0], x_kept[:, :]).then_inc(s_back, 16)
            eng.wait_ge(s_back, 16)

        @block.gpsimd
        def _(eng):
            with eng.Fori(0, AL) as l:
                eng.wait_ge(s_spread, l + 1)
                eng.nop(nofuse=True)
                eng.partition_all_reduce(top, spread, D, bass.bass_isa.ReduceOp.max).then_inc(s_top, 1)
                eng.wait_ge(s_copied, 1)
                eng.wait_ge(s_saved, 16)
                eng.wait_ge(s_fin, l + 1)
                eng.memset(acc, 0.0).then_inc(s_acc, 1)
                eng.wait_ge(s_band, l + 1)
                eng.nop(nofuse=True)
                count, before = bands(eng, l)
                with eng.Fori(0, count) as b:
                    r = before + b

                    def weighted(s, k, first, last):
                        n, nf = r * (2 * NT) + NT + s, r * NT + s
                        eng.wait_ge(s_m, nf + 1)
                        eng.wait_ge(s_e, n + 1)
                        eng.tensor_tensor(e[k], e[k], m, ALU.mult).then_inc(s_f, 1)

                    tiles(eng, weighted)

        @block.vector
        def _(eng):
            once = Steps(eng, s_v)
            eng.memset(epsc, EPS_BN)
            once(eng.memset(before_f, 0.0))
            eng.tensor_copy(x, T[0]).then_inc(s_copied, 1)
            eng.wait_ge(s_copied, 1)
            for j, c0, cw in PIECES:
                eng.tensor_reduce(greatest[:, j:j + 1], x[:, c0:c0 + cw], axis=AX.X, op=ALU.max)
            once(eng.memset(ext[:, 1:2], 0.0))
            eng.wait_ge(s_t, 16)
            eng.wait_ge(s_saved, 16)
            first = once.n
            PER = 20
            with eng.Fori(0, AL) as l:
                step = Steps(eng, s_v, l * PER + first)
                eng.wait_ge(s_xa, l * len(ACT_P) + 1)
                eng.wait_ge(s_xv, l * len(DVE_P) + 1)
                eng.tensor_copy(t_l, t_all[:, bass.ds(l, 1)])
                step(eng.tensor_reduce(ext[:, 0:1], greatest, axis=AX.X, op=ALU.max))
                step(eng.tensor_scalar(logits, ext, 0.0, EPS_MSG, ALU.max, ALU.add))
                step(eng.tensor_scalar(logits, logits, t_l, None, ALU.mult))
                eng.tensor_reduce(lim[:, 0:1], logits, axis=AX.X, op=ALU.max)
                step(eng.tensor_reduce(lim[:, 1:2], logits, axis=AX.X, op=ALU.min))
                step(eng.tensor_scalar(eps_t, t_l, EPS_MSG, None, ALU.mult))
                step(eng.tensor_tensor(spread, lim[:, 0:1], lim[:, 1:2], ALU.subtract))
                step(eng.tensor_scalar(spread, spread, BAND - REACH, 1.0 / BAND, ALU.add, ALU.mult))
                eng.tensor_scalar(spread, spread, 0.0, float(1 << 19), ALU.max, ALU.min).then_inc(s_spread, 1)
                step(eng.tensor_copy(shift_s, lim[:, 0:1]))
                eng.wait_ge(s_top, l + 1)
                step.apart = True
                bl = ranges[0:1, bass.ds(l * 2 + NT * R_BAND, 1)]
                step(eng.tensor_scalar(bl, top[0:1, :], 1.0, None, ALU.add))
                step(eng.tensor_copy(ranges[0:1, bass.ds(l * 2 + NT * R_BAND + 1, 1)], before_f))
                step(eng.tensor_copy(steps_f, bl))
                eng.tensor_tensor(before_f, before_f, steps_f, ALU.add).then_inc(s_band, 1)
                step.apart = False
                eng.wait_ge(s_band, l + 1)
                eng.nop(nofuse=True)
                count, before = bands(eng, l)
                with eng.Fori(0, count) as b:
                    r = before + b
                    zs = Steps(eng, s_agg, r * (NP + 4))
                    zs(eng.tensor_tensor(shift_z, eps_t, shift_s, ALU.subtract))

                    def exponents(c0, c1):
                        zc = z[:, c0:c1]
                        zs(eng.tensor_scalar(zc, x[:, c0:c1], 0.0, t_l, ALU.max, ALU.mult))
                        eng.tensor_scalar(zc, zc, shift_z, 0.0, ALU.add, ALU.min).then_inc(s_z, 1)

                    exponents(0, 2 * P)

                    def message(s):
                        eng.wait_ge(s_f, r * NT + s + 1)
                        eng.tensor_scalar(m, tile_cols(x, s), 0.0, EPS_MSG, ALU.max, ALU.add).then_inc(s_m, 1)

                    def tile(q, s, k, last=False):
                        n = r * (2 * NT) + q * NT + s
                        eng.wait_ge(s_hi, n + 1)
                        if q == 1 and not last:
                            message(s + 1)
                        eng.tensor_tensor(rest, MISC, parts[k][:, 0:D], ALU.subtract).then_inc(s_rest, 1)
                        eng.wait_ge(s_rest, n + 1)
                        eng.tensor_copy(parts[k][:, D:2 * D], rest).then_inc(s_mid, 1)
                        eng.wait_ge(s_mid, n + 1)
                        eng.tensor_tensor(parts[k][:, 2 * D:3 * D], rest, parts[k][:, D:2 * D],
                                          ALU.subtract).then_inc(s_parts, 1)
                        eng.wait_ge(s_parts, n + 2)
                        eng.nop(nofuse=True)

                    def weights(i, c0, cw):
                        d, ac = den[:, bass.ds(c0, cw)], acc[:, bass.ds(c0, cw)]
                        ds_ = Steps(eng, s_inv, r * (4 * NT) + i * 4, apart=True)
                        ds_(eng.tensor_scalar(d, d, 1e-31, None, ALU.max))
                        ds_(eng.reciprocal(d, d))
                        ds_(eng.scalar_tensor_tensor(d, d, float(np.exp(REACH)), d, ALU.is_le, ALU.mult))
                        ds_(eng.scalar_tensor_tensor(d, ac, 0.0, d, ALU.is_equal, ALU.mult))

                    def tile_and_exponents(s, k, first, last):
                        tile(0, s, k)
                        if first:
                            exponents(2 * P, N)

                    tiles(eng, tile_and_exponents)
                    for i, j in enumerate(DVE_P):
                        _, c0, cw = PIECES[j]
                        eng.wait_ge(s_sum, r * (2 * NP) + j + 2)
                        eng.tensor_copy(den[:, c0:c0 + cw], ps[:, j, 0:cw]).then_inc(s_denv, 1)
                    eng.wait_ge(s_denv, r * len(DVE_P) + len(DVE_P))
                    eng.wait_ge(s_dena, r * len(ACT_P) + len(ACT_P))

                    eng.wait_ge(s_acc, l + 1)

                    def tile_and_weights(s, k, first, last):
                        tile(1, s, k, last)
                        weights(s, s * P, P)

                    message(0)
                    tiles(eng, tile_and_weights)
                    for j, c0, cw in PIECES:
                        eng.wait_ge(s_sum, r * (2 * NP) + NP + j + 2)
                        d, ac = den[:, c0:c0 + cw], acc[:, c0:c0 + cw]
                        eng.tensor_tensor(d, ps[:, j, 0:cw], d, ALU.mult).then_inc(s_num, 1)
                        eng.wait_ge(s_num, r * NP + j + 2)
                        zs(eng.tensor_tensor(ac, ac, d, ALU.add))
                    zs(eng.tensor_scalar(shift_s, shift_s, -BAND, None, ALU.add))
                    assert zs.n == NP + 4
                for j, c0, cw in PIECES:
                    eng.tensor_tensor(x[:, c0:c0 + cw], x[:, c0:c0 + cw], acc[:, c0:c0 + cw], ALU.add).then_inc(s_h, 1)
                eng.wait_ge(s_w1, l * 32 + 32)
                for k in range(2):
                    for j, c0, cw in PIECES:
                        eng.wait_ge(s_h1o, l * (2 * NP) + k * NP + j + 1)
                        ins = eng.bn_stats(stats[:, 6 * j:6 * j + 6], h1[k][:, c0:c0 + cw])
                    step(ins)
                    eng.nop(nofuse=True)
                    eng.bn_aggr(mv, stats.rearrange("p (j f) -> p j f", f=6)).then_inc(s_var, 1)
                    eng.wait_ge(s_sd, l * 2 + k + 1)
                    sc, sh = scale[:, k:k + 1], shift[:, k:k + 1]
                    step(eng.reciprocal(sc, sd))
                    step(eng.tensor_tensor(sc, sc, vec[:, k:k + 1], ALU.mult))
                    step(eng.tensor_tensor(tmp, mv[:, 0:1], sc, ALU.mult))
                    eng.tensor_tensor(sh, vec[:, 2 + k:3 + k], tmp, ALU.subtract).then_inc(s_aff, 1)
                for j, c0, cw in PIECES:
                    if j in DVE_P:
                        eng.wait_ge(s_x, l * NP + j + 1)
                        eng.tensor_scalar(x[:, c0:c0 + cw], ps[:, j, 0:cw], 0.0, None, ALU.max).then_inc(s_xv, 1)
                        eng.wait_ge(s_xv, l * len(DVE_P) + DVE_P.index(j) + 2)
                    else:
                        eng.wait_ge(s_xa, l * len(ACT_P) + ACT_P.index(j) + 2)
                    ins = eng.tensor_reduce(greatest[:, j:j + 1], x[:, c0:c0 + cw], axis=AX.X, op=ALU.max)
                step(ins)
                assert step.n == PER, step.n

        @block.scalar
        def _(eng):
            with eng.Fori(0, AL) as l:
                eng.wait_ge(s_band, l + 1)
                eng.nop(nofuse=True)
                count, before = bands(eng, l)
                with eng.Fori(0, count) as b:
                    r = before + b

                    def exponential(q, s, k, first):
                        n = r * (2 * NT) + q * NT + s
                        eng.wait_ge(s_z, r * 2 + (1 if isinstance(s, int) and s < 2 else 2))
                        eng.wait_ge(s_tr, n + (2 if first else 1))
                        eng.activation(e[k], tile_cols(z, s), ACT.Exp).then_inc(s_e, 1)

                    def high(q, s, k, first):
                        n = r * (2 * NT) + q * NT + s
                        if first:
                            eng.wait_ge(s_sum, (r * 2 + q) * NP + 1)
                        else:
                            eng.wait_ge(s_used, (r * 2 + q) * (NT - 1) + s)
                        eng.wait_ge(s_tr, n + 3)
                        eng.activation(parts[k][:, 0:D], MISC, ACT.Copy).then_inc(s_hi, 1)

                    for q in range(2):
                        exponential(q, 0, 0, True)
                        exponential(q, 1, 1, False)

                        def body(s, k, first, last):
                            high(q, s, k, first)
                            if not last and not (isinstance(s, int) and s >= 23):
                                exponential(q, s + 2, k, False)

                        tiles(eng, body)
                        if q == 0:
                            for j in ACT_P:
                                _, c0, cw = PIECES[j]
                                eng.wait_ge(s_sum, r * (2 * NP) + j + 2)
                                eng.activation(den[:, c0:c0 + cw], ps[:, j, 0:cw], ACT.Copy).then_inc(s_dena, 1)
                for k in range(2):
                    for j, c0, cw in PIECES:
                        eng.wait_ge(s_h1, l * (2 * NP) + k * NP + j + 1)
                        eng.activation(h1[k][:, c0:c0 + cw], ps[:, j, 0:cw], ACT.Copy).then_inc(s_h1o, 1)
                    eng.wait_ge(s_var, l * 2 + k + 1)
                    eng.activation(sd, mv[:, 1:2], ACT.Sqrt, bias=epsc).then_inc(s_sd, 1)
                for j, c0, cw in PIECES:
                    for k in range(2):
                        if j == 0:
                            eng.wait_ge(s_aff, l * 2 + k + 1)
                        eng.activation(h1[k][:, c0:c0 + cw], h1[k][:, c0:c0 + cw], ACT.Relu,
                                       bias=shift[:, k:k + 1], scale=scale[:, k:k + 1]).then_inc(s_r1, 1)
                for j in ACT_P:
                    _, c0, cw = PIECES[j]
                    eng.wait_ge(s_x, l * NP + j + 1)
                    eng.activation(x[:, c0:c0 + cw], ps[:, j, 0:cw], ACT.Relu).then_inc(s_xa, 1)

        @block.tensor
        def _(eng):
            for s, n in ((s_xa, 1), (s_xv, 1), (s_num, 1), (s_f, 1), (s_tr, 2), (s_used, 1), (s_sum, 1), (s_parts, 1), (s_fin, 1)):
                for _ in range(n):
                    eng.nop(nofuse=True).then_inc(s, 1)
            with eng.Fori(0, AL) as l:
                eng.wait_ge(s_band, l + 1)
                eng.nop(nofuse=True)
                count, before = bands(eng, l)
                eng.wait_ge(s_xa, l * len(ACT_P) + 1)
                eng.wait_ge(s_xv, l * len(DVE_P) + 1)
                eng.nop(nofuse=True)
                with eng.Fori(0, count) as b:
                    r = before + b
                    for q in range(2):
                        def transpose(s, k):
                            n = r * (2 * NT) + q * NT + s
                            eng.wait_ge(s_e, n + 1) if q == 0 else eng.wait_ge(s_f, r * NT + s + 2)
                            eng.wait_ge(s_parts, n + 1)
                            eng.transpose(MISC, e[k], ident[:, :]).then_inc(s_tr, 1)

                        def products(s, k, first, last):
                            n = r * (2 * NT) + q * NT + s
                            eng.wait_ge(s_parts, n + 2)
                            for i in range(3):
                                for j, c0, cw in PIECES:
                                    if first and i == 0:
                                        if q == 0 and j == 0:
                                            eng.wait_ge(s_num, r * NP + 1)
                                        if q == 1 and j in ACT_P:
                                            eng.wait_ge(s_dena, r * len(ACT_P) + ACT_P.index(j) + 1)
                                        if q == 1 and j in DVE_P:
                                            eng.wait_ge(s_denv, r * len(DVE_P) + DVE_P.index(j) + 1)
                                    if isinstance(s, int):
                                        cols = adj[:, s, c0:c0 + cw]
                                    else:
                                        cols = adj[:, bass.ds(s, 1), c0:c0 + cw].rearrange("p o c -> p (o c)")
                                    ins = eng.matmul(ps[:, j, 0:cw], parts[k][:, i * D:(i + 1) * D], cols,
                                                     start=first and i == 0, stop=last and i == 2,
                                                     skip_group_check=True)
                                    if last and i == 2:
                                        ins.then_inc(s_sum, 1)
                            if not last:
                                ins.then_inc(s_used, 1)

                        transpose(0, 0)

                        def both(s, k, first, last):
                            if not last:
                                transpose(s + 1, 1 - k)
                            products(s, k, first, last)

                        tiles(eng, both)
                for k in range(2):
                    for j, c0, cw in PIECES:
                        if k == 0:
                            eng.wait_ge(s_h, l * NP + j + 1)
                            if j == 0:
                                eng.wait_ge(s_w1, l * 32 + 32)
                        else:
                            eng.wait_ge(s_h1o, l * (2 * NP) + j + 1)
                        eng.matmul(ps[:, j, 0:cw], w1[:, k * D:(k + 1) * D], x[:, c0:c0 + cw],
                                   start=True, stop=True).then_inc(s_h1, 1)
                eng.wait_ge(s_w2, l * 16 + 16)
                for j, c0, cw in PIECES:
                    eng.wait_ge(s_r1, l * (2 * NP) + 2 * j + 2)
                    eng.matmul(ps[:, j, 0:cw], w2[:, 0, :], h1[0][:, c0:c0 + cw], start=True, stop=False)
                    eng.matmul(ps[:, j, 0:cw], w2[:, 1, :], h1[1][:, c0:c0 + cw], start=False,
                               stop=True).then_inc(s_x, 1)
                eng.wait_ge(s_xa, (l + 1) * len(ACT_P) + 1)
                eng.wait_ge(s_xv, (l + 1) * len(DVE_P) + 1)
                eng.nop(nofuse=True).then_inc(s_fin, 1)


def interaction(G):
    nc, a, sem, work, small, ranges, ident, ps, T = (
        G[k] for k in ("nc", "a", "sem", "work", "small", "ranges", "ident", "ps", "T"))
    h_rows, edge_rows = G["h_rows"], G["edge_rows"]
    x, S = T[0], T[2]
    S_late = work[:, 2 * N - P:3 * N]
    HALVES = range(2)
    free = Words(G["adj_words"])
    rows_t = free(P, (NC + 1) * ROW)
    row3 = rows_t.rearrange("p (c f) -> p c f", f=ROW)
    dst_i = free(P, NC + 1, I32)
    groups = [(g, range(4 * g, min(NT, 4 * g + 4))) for g in range((NT + 3) // 4)]
    stage = [free(P, 4 * D) for _ in groups]
    gathered, pre, soft, msg, hot = ([free(P, UH * n) for _ in HALVES] for n in (D, D, D, D, P))
    attr_t = [free(UH * ROW, P) for _ in HALVES]
    attr, rel, rcut = free(P, US * ROW), free(P, US), free(P, US)
    iota, tile_lo, idx = free(P, P), free(P, NT), [free(P, UH, I32) for _ in HALVES]
    b_in, zero, w_f = free(P, D), free(1, D, BF16), free(UH * ROW, UH * D)
    s_ = Words(small)
    w_in, w_out, b_out = s_(D, D), s_(D, D), s_(D, 1)
    LOADS = 5
    cuts = [i * (NC // LOADS) for i in range(LOADS + 1)]

    s_load, s_const, s_er, s_dst = sem("weights_loaded"), sem("constants_ready"), sem("edge_rows_loaded"), sem("dst_ready")
    s_rows, s_h, s_hrow, s_wz = sem("rows_ready"), sem("h_read_out"), sem("h_rows_written"), sem("weights_zeroed")
    s_st, s_rel, s_hot, s_agg = sem("attributes_staged"), sem("places_ready"), sem("hots_ready"), sem("edges_summed")
    s_idx, s_g, s_tr, s_at, s_prod, s_pre, s_min, s_exp, s_ln, s_soft, s_msg = (
        [sem(f"{n}_{h}") for h in "ab"] for n in (
            "index_ready", "rows_gathered", "transposed", "attributes_ready", "filter_product", "filter_read_out",
            "bounded", "exp_ready", "log_ready", "softplus_ready", "message_ready"))
    s_half, s_tile, s_ev = sem("half_ready"), sem("tile_summed"), sem("tile_read_out")
    A_MAX = 40.0
    half = s_(D, 1)
    SUM, PROD, TRANS = ps[:, 7, 0:P], [ps[0:P, h, 0:UH * D] for h in HALVES], [ps[0:UH * ROW, 2 + h, 0:P] for h in HALVES]
    WEIGHTS = 16 * (2 + 2 * UH)
    s_in = sem("input_weights_loaded")

    def units(eng, body, first=None, second=None):
        def at(start, u):
            return nc.s_assert_within(start + u * US, 0, NC + 1 - US)

        register = eng.alloc_register(f"steps_{nc.get_next_instruction_name()}")
        eng.reg_mov(register, 0)
        peeled = [b for b in (first, second) if b]
        with eng.Fori(0, NT) as w:
            start, count = load_range(nc, eng, ranges, R_SRC, w, STEPS, US)
            before = eng.snap(register, min_val=0, max_val=NT * STEPS)
            for u, b in enumerate(peeled):
                b(w, at(start, u), before + u)
            with eng.Fori(len(peeled), count) as u:
                body(w, at(start, u), before + u)
            eng.reg_add(register, register, count)
        return eng.snap(register, min_val=1, max_val=NT * STEPS)

    with nc.Block() as block:
        @block.sync
        def _(eng):
            for dst, src in ((w_in, a["int_w_in"]),
                             (b_in, a["int_b_in"].rearrange("(o c) -> o c", o=1).to_broadcast([P, D]))):
                eng.dma_start(dst, src).then_inc(s_in, 16)
            for dst, src in ((w_out, a["int_w_out"]), (b_out, a["int_b_out"].rearrange("(c o) -> c o", o=1))):
                eng.dma_start(dst, src).then_inc(s_load, 16)
            er = edge_rows.rearrange("(p c) f -> p (c f)", p=P)
            for c0, c1 in zip(cuts, cuts[1:]):
                eng.dma_start(rows_t[:, c0 * ROW:c1 * ROW], er[:, c0 * ROW:c1 * ROW]).then_inc(s_er, 16)
            eng.wait_ge(s_wz, 1)
            for k in range(UH):
                cols = w_f[:, k * D:(k + 1) * D]
                eng.dma_start(cols[k * ROW:k * ROW + FR, :], a["int_w_f"]).then_inc(s_load, 16)
                eng.dma_start(cols[k * ROW + FR:k * ROW + FR + 1, :],
                              a["int_b_f"].rearrange("(o c) -> o c", o=1)).then_inc(s_load, 16)
            h_view = h_rows.rearrange("(s p) c -> p s c", p=P)
            for g, tiles in groups:
                eng.wait_ge(s_h, g + 1)
                eng.dma_start(h_view[:, tiles[0]:tiles[-1] + 1, :],
                              stage[g][:, 0:len(tiles) * D].rearrange("p (s c) -> p s c", c=D)).then_inc(s_hrow, 16)
            eng.wait_ge(s_hrow, 16 * len(groups))

        @block.gpsimd
        def _(eng):
            imprecise = dict(allow_small_or_imprecise_dtypes=True)
            eng.memset(w_f, 0.0).then_inc(s_wz, 1)
            eng.iota(tile_lo, pattern=[[P, NT]], base=0, channel_multiplier=0, **imprecise).then_inc(s_const, 1)
            eng.iota(iota, pattern=[[1, P]], base=0, channel_multiplier=0, **imprecise).then_inc(s_const, 1)
            eng.memset(zero, 0.0).then_inc(s_const, 1)
            for h in HALVES:
                eng.memset(idx[h], 0)
                eng.memset(pre[h], 0.0)
                eng.memset(soft[h], 0.0)
            eng.memset(attr, 0.0)
            eng.memset(rcut, 0.0)
            eng.memset(rel, 0.0).then_inc(s_const, 1)
            eng.wait_ge(s_const, 4)
            eng.nop(nofuse=True)
            for h in HALVES:
                for k in range(UH):
                    eng.indirect_dma_start(gathered[h][:, k * D:(k + 1) * D], None, G["p_rows"][:, :],
                                           bass.IndirectOffsetOnAxis(ap=idx[h][:, k:k + 1], axis=0)
                                           ).then_inc(s_g[h], 16)
            eng.wait_ge(s_dst, 1)
            eng.wait_ge(s_hrow, 16 * len(groups))

            def body(w, c, q):
                for h in HALVES:
                    eng.wait_ge(s_msg[h], q + 1)
                    eng.nop(nofuse=True)
                    eng.tensor_copy(idx[h], dst_i[:, bass.ds(c + h * UH, UH)]).then_inc(s_idx[h], 1)
                    eng.wait_ge(s_idx[h], q + 1)
                    eng.nop(nofuse=True)
                    for k in range(UH):
                        eng.indirect_dma_start(gathered[h][:, k * D:(k + 1) * D], None, h_rows[:, :],
                                               bass.IndirectOffsetOnAxis(ap=idx[h][:, k:k + 1], axis=0)
                                               ).then_inc(s_g[h], 16)

            units(eng, body)

        @block.vector
        def _(eng):
            eng.memset(half, 0.5).then_inc(s_half, 1)
            eng.memset(row3[:, NC:NC + 1, 0:SRC_C], 0.0)
            eng.memset(row3[:, NC:NC + 1, SRC_C:ROW], -1.0)
            eng.wait_ge(s_in, 32)
            for g, tiles in groups:
                n = len(tiles)
                eng.wait_ge(s_rows, g + 1)
                eng.tensor_tensor(stage[g][:, 0:n * D].rearrange("p (s c) -> p s c", c=D),
                                  ps[0:P, g % 4, 0:n * D].rearrange("p (s c) -> p s c", c=D),
                                  b_in.unsqueeze(1).to_broadcast([P, n, D]), ALU.add).then_inc(s_h, 1)
            eng.wait_ge(s_er, 16 * LOADS)
            eng.tensor_copy(dst_i, row3[:, :, DST_C]).then_inc(s_dst, 1)
            eng.wait_ge(s_const, 4)
            at3 = attr.rearrange("p (c f) -> p c f", f=ROW)

            def hots(q):
                eng.wait_ge(s_agg, q + 1)
                for k in range(US):
                    ins = eng.tensor_scalar(hot[k // UH][:, k % UH * P:(k % UH + 1) * P], iota, rel[:, k:k + 1],
                                            rcut[:, k:k + 1], ALU.is_equal, ALU.mult)
                ins.then_inc(s_hot, 1)

            def message(q, h):
                eng.wait_ge(s_ln[h], q + 1)
                eng.scalar_tensor_tensor(soft[h], pre[h], -LOG2, soft[h], ALU.add, ALU.max).then_inc(s_soft[h], 1)
                eng.wait_ge(s_soft[h], q + 1)
                eng.wait_ge(s_g[h], (q + 1) * (16 * UH))
                eng.tensor_tensor(msg[h], soft[h], gathered[h], ALU.mult).then_inc(s_msg[h], 1)

            def body(w, c, q):
                for h in HALVES:
                    eng.wait_ge(s_tr[h], q + 1)
                eng.nop(nofuse=True)
                eng.tensor_copy(attr, row3[:, bass.ds(c, US), :].rearrange("p c f -> p (c f)")).then_inc(s_st, 1)
                for h in HALVES:
                    eng.wait_ge(s_tr[h], q + 2)
                    eng.tensor_copy(attr_t[h], TRANS[h]).then_inc(s_at[h], 1)
                hots(q)
                eng.wait_ge(s_hot, q + 1)
                eng.wait_ge(s_st, q + 1)
                eng.tensor_scalar(rel, at3[:, :, SRC_C], tile_lo[:, bass.ds(w, 1)], None, ALU.subtract)
                eng.tensor_copy(rcut, at3[:, :, RCUT_C]).then_inc(s_rel, 1)
                for h in HALVES:
                    message(q, h)
                for h in HALVES:
                    eng.wait_ge(s_pre[h], q + 2)
                    eng.wait_ge(s_msg[h], q + 1)
                    eng.tensor_scalar(soft[h], pre[h], A_MAX, None, ALU.min).then_inc(s_min[h], 1)
                eng.wait_ge(s_rel, q + 1)

            q = units(eng, body)
            hots(q)
            for h in HALVES:
                message(q, h)

        @block.scalar
        def _(eng):
            eng.wait_ge(s_half, 1)

            def evacuate(w):
                eng.wait_ge(s_tile, w + 1)
                eng.activation(S_late[:, bass.ds(w * P, P)], SUM, ACT.Copy).then_inc(s_ev, 1)

            def body(w, c, q, first=False):
                for h in HALVES:
                    eng.wait_ge(s_prod[h], q + 1)
                    eng.wait_ge(s_soft[h], q + 1)
                    eng.activation(pre[h], PROD[h], ACT.Copy).then_inc(s_pre[h], 1)
                for h in HALVES:
                    eng.wait_ge(s_min[h], q + 1)
                    eng.activation(soft[h], soft[h], ACT.Exp).then_inc(s_exp[h], 1)
                for h in HALVES:
                    eng.wait_ge(s_exp[h], q + 1)
                    eng.activation(soft[h], soft[h], ACT.Ln, bias=half[0:P, :], scale=0.5).then_inc(s_ln[h], 1)
                if first:
                    evacuate(w)

            units(eng, body, lambda w, c, q: body(w, c, q, True))
            evacuate(NT)

        @block.tensor
        def _(eng):
            eng.wait_ge(s_in, 32)
            for g, tiles in groups:
                if g >= 4:
                    eng.wait_ge(s_h, g - 3)
                for i, s in enumerate(tiles):
                    ins = eng.matmul(ps[0:P, g % 4, i * D:(i + 1) * D], x[:, s * P:(s + 1) * P], w_in,
                                     start=True, stop=True)
                ins.then_inc(s_rows, 1)
            eng.wait_ge(s_h, len(groups))
            eng.wait_ge(s_const, 4)
            eng.wait_ge(s_load, WEIGHTS)
            for s in [s_agg] + s_tr + s_pre + s_ln:
                eng.nop(nofuse=True).then_inc(s, 1)

            def opened():
                eng.matmul(SUM, zero, zero[:, 0:P], start=True, stop=False, skip_group_check=True)

            def closed():
                eng.matmul(SUM[:, 0:1], zero, zero[:, 0:1], start=False, stop=True,
                           skip_group_check=True).then_inc(s_tile, 1)

            def front(q):
                eng.wait_ge(s_st, q + 1)
                for h in HALVES:
                    eng.transpose(TRANS[h], attr[:, h * UH * ROW:(h + 1) * UH * ROW], ident[0:P, 0:P]).then_inc(s_tr[h], 1)
                for h in HALVES:
                    eng.wait_ge(s_at[h], q + 1)
                    eng.wait_ge(s_pre[h], q + 1)
                    eng.matmul(PROD[h], attr_t[h], w_f, start=True, stop=True).then_inc(s_prod[h], 1)

            def totals(q):
                eng.wait_ge(s_hot, q + 1)
                for h in HALVES:
                    eng.wait_ge(s_msg[h], q + 1)
                    for k in range(UH):
                        ins = eng.matmul(SUM, msg[h][:, k * D:(k + 1) * D], hot[h][:, k * P:(k + 1) * P],
                                         start=False, stop=False, skip_group_check=True)
                ins.then_inc(s_agg, 1)

            def first(w, c, q):
                front(q)
                totals(q)
                closed()

            def second(w, c, q):
                front(q)
                eng.wait_ge(s_ev, w + 1)
                eng.nop(nofuse=True)
                opened()
                totals(q)

            def body(w, c, q):
                front(q)
                totals(q)

            opened()
            q = units(eng, body, first, second)
            totals(q)
            closed()


    s_o, s_e, s_m, s_l, s_b = (sem(n) for n in ("output_product", "exp_ready", "product_bounded", "log_ready",
                                                "bias_ready"))
    b_low, e = s_(D, 1), T[1]
    with nc.Block() as block:
        @block.tensor
        def _(eng):
            for j, c0, cw in PIECES:
                eng.matmul(ps[:, j, 0:cw], w_out, S[:, c0:c0 + cw], start=True, stop=True).then_inc(s_o, 1)

        @block.scalar
        def _(eng):
            for j, c0, cw in PIECES:
                eng.wait_ge(s_m, j + 1)
                eng.activation(e[:, c0:c0 + cw], e[:, c0:c0 + cw], ACT.Exp).then_inc(s_e, 1)
            for j, c0, cw in PIECES:
                eng.wait_ge(s_e, j + 1)
                eng.activation(e[:, c0:c0 + cw], e[:, c0:c0 + cw], ACT.Ln, bias=half, scale=0.5).then_inc(s_l, 1)

        @block.vector
        def _(eng):
            eng.tensor_scalar(b_low, b_out, -LOG2, None, ALU.add).then_inc(s_b, 1)
            for j, c0, cw in PIECES:
                eng.wait_ge(s_o, j + 1)
                eng.tensor_scalar(e[:, c0:c0 + cw], ps[:, j, 0:cw], b_out, A_MAX, ALU.add, ALU.min).then_inc(s_m, 1)
            eng.wait_ge(s_b, 1)
            for j, c0, cw in PIECES:
                eng.wait_ge(s_l, j + 1)
                eng.scalar_tensor_tensor(e[:, c0:c0 + cw], ps[:, j, 0:cw], b_low, e[:, c0:c0 + cw],
                                         ALU.add, ALU.max)


def store(G):
    nc, sem, T, out = G["nc"], G["sem"], G["T"], G["out"]
    s_out = sem("stored")
    with nc.Block() as block:
        @block.sync
        def _(eng):
            eng.dma_start(out[:, :], T[0]).then_inc(s_out, 16)
            eng.wait_ge(s_out, 16)


def layout(inputs):
    i = {k: np.asarray(v) for k, v in inputs.items()}
    cols = lambda v: v.reshape(NC, P).T
    spare = lambda v: np.concatenate([v, np.zeros((v.shape[0], (STEPS * US - NC) * P), v.dtype)], axis=1)
    r = dict(x=i["x"].T, dst=i["dst"], src_cols=cols(i["src"]), dst_cols=cols(i["dst"]),
             weight_cols=cols(i["edge_weight"]), edge_attr_20=i["edge_attr_20"], edge_attr_64=spare(i["edge_attr_64"].T),
             gin_w1=i["L0_gnn_W1"].transpose(2, 0, 1).reshape(D, GL * GH),
             gin_w2=i["L0_gnn_W2"].transpose(2, 0, 1).reshape(GH, GL * GH),
             gin_w3=i["L0_gnn_W3"].transpose(2, 0, 1).reshape(GH, GL * D),
             gin_b3=i["L0_gnn_b3"].T, gin_eps=i["L0_gnn_eps"])
    for n in ("b1", "g1", "bt1", "b2", "g2", "bt2"):
        r["gin_" + n] = i["L0_gnn_" + n].T
    w1, u1 = i["L1_gnn_W1"].T, i["L1_gnn_U1"].T
    r.update(mlp_w1a=w1[:D], mlp_w1b=w1[D:2 * D], mlp_w1e=w1[2 * D:], mlp_b1=i["L1_gnn_b1"],
             mlp_w2=i["L1_gnn_W2"].T, mlp_b2=i["L1_gnn_b2"], mlp_u1a=u1[:D], mlp_u1b=u1[D:],
             mlp_c1=i["L1_gnn_c1"], mlp_u2=i["L1_gnn_U2"].T, mlp_c2=i["L1_gnn_c2"])
    gb = np.stack([i["L2_gnn_gamma"].reshape(AL, 2, D), i["L2_gnn_beta"].reshape(AL, 2, D)], axis=1)
    r.update(agg_w1=i["L2_gnn_W1"].transpose(1, 0, 2).reshape(D, AL * AH),
             agg_w2=i["L2_gnn_W2"].reshape(AL * 2, D, D).transpose(1, 0, 2),
             agg_vec=gb.transpose(3, 0, 1, 2).reshape(D, AL * 4), agg_t=i["L2_gnn_t"])
    r.update(int_w_in=i["L3_gnn_W_in"].T, int_b_in=i["L3_gnn_b_in"], int_w_f=i["L3_gnn_W_f"].T,
             int_b_f=i["L3_gnn_b_f"], int_w_out=i["L3_gnn_W_out"].T, int_b_out=i["L3_gnn_b_out"])
    return {k: np.ascontiguousarray(v) for k, v in r.items()}


def kernel(**inputs):
    import concourse.bacc as bacc
    from concourse.bass_utils import run_bass_kernel_spmd as run
    nc = bacc.Bacc("TRN2", target_bir_lowering=False, num_devices=1)
    arrays = layout(inputs)
    aps = {k: nc.dram_tensor(k, v.shape, mybir.dt.from_np(v.dtype), kind="ExternalInput").ap()
           for k, v in arrays.items()}
    out = nc.dram_tensor("out", (D, N), F32, kind="ExternalOutput").ap()
    build(nc, aps, out)
    r = run(nc, [arrays], core_ids=[0])
    return np.ascontiguousarray(r.results[0]["out"].T)
```
